# Optimizing a Trainium2 kernel written in Bass

```python
import numpy as np
import jax
import jax.numpy as jnp

def _softmax(x, axis=-1):
    return jax.nn.softmax(x, axis=axis)

def _gelu(x):
    return jax.nn.gelu(x, approximate=True)

def _silu(x):
    return jax.nn.silu(x)

def _sigmoid(x):
    return jax.nn.sigmoid(x)

def _layernorm(x, axis=-1, eps=1e-05):
    m = jnp.mean(x, axis=axis, keepdims=True)
    v = jnp.var(x, axis=axis, keepdims=True)
    return (x - m) / jnp.sqrt(v + eps)

def _scatter_add(tgt, idx, src, axis=0):
    return tgt.at[idx].add(src)

def _segment_sum(src, seg, n):
    return jax.ops.segment_sum(src, seg, n)
kernel_name = 'mk_xattn_ffn_d2_seqx_r4_cc5652'

def setup_inputs(seed: int=0):
    np.random.seed(seed)
    _w = jnp.asarray

    def _rec_inputs():
        import jax
        import jax.numpy as jnp
        _rk = jax.random.key(seed)
        x = -0.0002928 + 1 * jax.random.normal(jax.random.fold_in(_rk, 1), (8, 512, 256), jnp.float32)
        _lenS = 512 - jax.random.randint(jax.random.fold_in(_rk, 7), (8,), 0, max(1, 512 // 4) + 1, jnp.int32)
        _lenS2 = 64 - jax.random.randint(jax.random.fold_in(_rk, 8), (8,), 0, max(1, 64 // 4) + 1, jnp.int32)
        _ctx_1024P = jax.random.normal(jax.random.fold_in(_rk, 11), (8, 16, 256), jnp.float32)
        _ctx_1024c = jax.random.dirichlet(jax.random.fold_in(_rk, 511), 0.3 * jnp.ones((16,), jnp.float32), (8, 64))
        _ctx_1024t = jnp.einsum('bsk,bkd->bsd', _ctx_1024c, _ctx_1024P)
        _ctx_1024t = _ctx_1024t * jax.lax.rsqrt(jnp.mean(jnp.square(_ctx_1024t)) + 1e-12) * 0.953939
        ctx_1024 = -1.39393e-06 + 0.999914 * (_ctx_1024t + 0.3 * jax.random.normal(jax.random.fold_in(_rk, 611), (8, 64, 256), jnp.float32))
        _validS = jnp.arange(512)[None, :] < _lenS[:, None]
        _validS2 = jnp.arange(64)[None, :] < _lenS2[:, None]
        _causal = jnp.tril(jnp.ones((512, 512), dtype=bool))
        mask_Bx1x1xS2_ff0 = jnp.where(jnp.ones((8, 1, 1, 64), dtype=bool), 0.0, -1000000000.0).astype(jnp.float32)
        return (x, ctx_1024, mask_Bx1x1xS2_ff0)
    x, ctx_1024, mask_Bx1x1xS2_ff0 = _rec_inputs()

    def _L0_xattn_setup():
        import jax, jax.numpy as jnp
        import numpy as np
        D_MODEL = 256
        HEAD = 16
        D_K = D_MODEL // HEAD
        key = jax.random.key(seed)
        ks = jax.random.split(key, 11)
        B, S = (2, 512)
        scale = 1.0 / np.sqrt(D_MODEL)
        inp = {'q': jax.random.normal(ks[0], (B, S, D_MODEL), dtype=jnp.float32), 'k': jax.random.normal(ks[1], (B, S, D_MODEL), dtype=jnp.float32), 'v': jax.random.normal(ks[2], (B, S, D_MODEL), dtype=jnp.float32), 'wq': jax.random.normal(ks[3], (D_MODEL, D_MODEL), dtype=jnp.float32) * scale, 'bq': jnp.zeros((D_MODEL,), dtype=jnp.float32), 'wk': jax.random.normal(ks[4], (D_MODEL, D_MODEL), dtype=jnp.float32) * scale, 'bk': jnp.zeros((D_MODEL,), dtype=jnp.float32), 'wv': jax.random.normal(ks[5], (D_MODEL, D_MODEL), dtype=jnp.float32) * scale, 'bv': jnp.zeros((D_MODEL,), dtype=jnp.float32), 'wo': jax.random.normal(ks[6], (D_MODEL, D_MODEL), dtype=jnp.float32) * scale, 'bo': jnp.zeros((D_MODEL,), dtype=jnp.float32)}
        return inp
    _L0_xattn_all = _L0_xattn_setup()
    _L0_xattn_in = {k: v for k, v in _L0_xattn_all.items() if k in ('wq', 'bq', 'wk', 'bk', 'wv', 'bv', 'wo', 'bo')}
    del _L0_xattn_all

    def _L0_ffn_setup():
        import jax, jax.numpy as jnp
        import numpy as np
        CAPACITY_RATIO = 0.75
        key = jax.random.key(seed)
        k1, k2, k3 = jax.random.split(key, 3)
        B, L, D = (4, 2048, 256)
        x = jax.random.normal(k1, (B, L, D), dtype=jnp.float32)
        w_router = jax.random.normal(k2, (D,), dtype=jnp.float32) * 0.02
        w_block = jax.random.normal(k3, (D, D), dtype=jnp.float32) * 0.02
        return {'x': x, 'w_router': w_router, 'w_block': w_block}
    _L0_ffn_all = _L0_ffn_setup()
    _L0_ffn_in = {k: v for k, v in _L0_ffn_all.items() if k in ('w_router', 'w_block')}
    del _L0_ffn_all

    def _L1_xattn_setup():
        import jax, jax.numpy as jnp
        import numpy as np
        D_MODEL = 256
        NUM_HEADS = 16
        DEPTH = D_MODEL // NUM_HEADS

        def _split_heads(x):
            B, S, _ = x.shape
            return x.reshape(B, S, NUM_HEADS, DEPTH).transpose(0, 2, 1, 3)
        key = jax.random.key(seed)
        ks = jax.random.split(key, 12)
        B, S = (4, 512)
        scale = 1.0 / np.sqrt(D_MODEL)
        inp = {'query': jax.random.normal(ks[0], (B, S, D_MODEL), dtype=jnp.float32), 'key': jax.random.normal(ks[1], (B, S, D_MODEL), dtype=jnp.float32), 'value': jax.random.normal(ks[2], (B, S, D_MODEL), dtype=jnp.float32), 'mask': jnp.zeros((B, 1, 1, S), dtype=jnp.float32), 'Wq': jax.random.normal(ks[3], (D_MODEL, D_MODEL), dtype=jnp.float32) * scale, 'bq': jnp.zeros((D_MODEL,), dtype=jnp.float32), 'Wk': jax.random.normal(ks[4], (D_MODEL, D_MODEL), dtype=jnp.float32) * scale, 'bk': jnp.zeros((D_MODEL,), dtype=jnp.float32), 'Wv': jax.random.normal(ks[5], (D_MODEL, D_MODEL), dtype=jnp.float32) * scale, 'bv': jnp.zeros((D_MODEL,), dtype=jnp.float32), 'Wo': jax.random.normal(ks[6], (D_MODEL, D_MODEL), dtype=jnp.float32) * scale, 'bo': jnp.zeros((D_MODEL,), dtype=jnp.float32)}
        return inp
    _L1_xattn_all = _L1_xattn_setup()
    _L1_xattn_in = {k: v for k, v in _L1_xattn_all.items() if k in ('Wq', 'bq', 'Wk', 'bk', 'Wv', 'bv', 'Wo', 'bo')}
    del _L1_xattn_all

    def _L1_ffn_setup():
        import jax, jax.numpy as jnp
        import numpy as np
        TOP_K = 2
        key = jax.random.key(seed)
        k1, k2, k3, k4 = jax.random.split(key, 4)
        B, S, H, I, E = (2, 512, 256, 1024, 8)
        return {'hidden_states': jax.random.normal(k1, (B, S, H), jnp.float32), 'gate_w': jax.random.normal(k2, (E, H), jnp.float32) * 0.02, 'gate_up_proj': jax.random.normal(k3, (E, 2 * I, H), jnp.float32) * 0.02, 'down_proj': jax.random.normal(k4, (E, H, I), jnp.float32) * 0.02}
    _L1_ffn_all = _L1_ffn_setup()
    _L1_ffn_in = {k: v for k, v in _L1_ffn_all.items() if k in ('gate_w', 'gate_up_proj', 'down_proj')}
    del _L1_ffn_all
    return {'x': x, 'ctx_1024': ctx_1024, 'mask_Bx1x1xS2_ff0': mask_Bx1x1xS2_ff0, 'L0_xattn_wq': _L0_xattn_in['wq'], 'L0_xattn_bq': _L0_xattn_in['bq'], 'L0_xattn_wk': _L0_xattn_in['wk'], 'L0_xattn_bk': _L0_xattn_in['bk'], 'L0_xattn_wv': _L0_xattn_in['wv'], 'L0_xattn_bv': _L0_xattn_in['bv'], 'L0_xattn_wo': _L0_xattn_in['wo'], 'L0_xattn_bo': _L0_xattn_in['bo'], 'L0_ffn_w_router': _L0_ffn_in['w_router'], 'L0_ffn_w_block': _L0_ffn_in['w_block'], 'L1_xattn_Wq': _L1_xattn_in['Wq'], 'L1_xattn_bq': _L1_xattn_in['bq'], 'L1_xattn_Wk': _L1_xattn_in['Wk'], 'L1_xattn_bk': _L1_xattn_in['bk'], 'L1_xattn_Wv': _L1_xattn_in['Wv'], 'L1_xattn_bv': _L1_xattn_in['bv'], 'L1_xattn_Wo': _L1_xattn_in['Wo'], 'L1_xattn_bo': _L1_xattn_in['bo'], 'L1_ffn_gate_w': _L1_ffn_in['gate_w'], 'L1_ffn_gate_up_proj': _L1_ffn_in['gate_up_proj'], 'L1_ffn_down_proj': _L1_ffn_in['down_proj']}

def reference(x, ctx_1024, mask_Bx1x1xS2_ff0, L0_xattn_wq, L0_xattn_bq, L0_xattn_wk, L0_xattn_bk, L0_xattn_wv, L0_xattn_bv, L0_xattn_wo, L0_xattn_bo, L0_ffn_w_router, L0_ffn_w_block, L1_xattn_Wq, L1_xattn_bq, L1_xattn_Wk, L1_xattn_bk, L1_xattn_Wv, L1_xattn_bv, L1_xattn_Wo, L1_xattn_bo, L1_ffn_gate_w, L1_ffn_gate_up_proj, L1_ffn_down_proj):
    import jax
    import jax.numpy as jnp

    def _L0_xattn_ref(q, k, v, wq, bq, wk, bk, wv, bv, wo, bo):
        import jax, jax.numpy as jnp
        import numpy as np
        D_MODEL = 256
        HEAD = 16
        D_K = D_MODEL // HEAD
        B, S, _ = q.shape

        def proj(x, w, b):
            y = x @ w.T + b
            return y.reshape(B, -1, HEAD, D_K).transpose(0, 2, 1, 3)
        qh, kh, vh = (proj(q, wq, bq), proj(k, wk, bk), proj(v, wv, bv))
        scores = jnp.einsum('bhqd,bhkd->bhqk', qh, kh) / jnp.sqrt(jnp.float32(D_K))
        probs = jax.nn.softmax(scores, axis=-1)
        ctx = jnp.einsum('bhqk,bhkd->bhqd', probs, vh)
        concat = ctx.transpose(0, 2, 1, 3).reshape(B, S, D_MODEL)
        return concat @ wo.T + bo

    def _L0_ffn_ref(x, w_router, w_block):
        import jax, jax.numpy as jnp
        import numpy as np
        CAPACITY_RATIO = 0.75
        B, L, D = x.shape
        k = max(1, int(L * CAPACITY_RATIO))
        scores = jnp.einsum('bld,d->bl', x, w_router)
        _, top_idx = jax.lax.top_k(scores, k)
        selected = jnp.take_along_axis(x, top_idx[:, :, None], axis=1)
        processed = jax.nn.gelu(jnp.einsum('bkd,de->bke', selected, w_block))
        batch_idx = jnp.arange(B)[:, None]
        out = x.at[batch_idx, top_idx].set(processed)
        return out

    def _L1_xattn_ref(query, key, value, mask, Wq, bq, Wk, bk, Wv, bv, Wo, bo):
        import jax, jax.numpy as jnp
        import numpy as np
        D_MODEL = 256
        NUM_HEADS = 16
        DEPTH = D_MODEL // NUM_HEADS

        def _split_heads(x):
            B, S, _ = x.shape
            return x.reshape(B, S, NUM_HEADS, DEPTH).transpose(0, 2, 1, 3)
        B, Sq, _ = query.shape
        q = _split_heads(query @ Wq + bq)
        k = _split_heads(key @ Wk + bk)
        v = _split_heads(value @ Wv + bv)
        logits = jnp.einsum('bhqd,bhkd->bhqk', q, k) / jnp.sqrt(jnp.float32(DEPTH))
        logits = logits + mask * -1000000000.0
        attn = jax.nn.softmax(logits, axis=-1)
        ctx = jnp.einsum('bhqk,bhkd->bhqd', attn, v)
        ctx = ctx.transpose(0, 2, 1, 3).reshape(B, Sq, D_MODEL)
        return ctx @ Wo + bo

    def _L1_ffn_ref(hidden_states, gate_w, gate_up_proj, down_proj):
        import jax, jax.numpy as jnp
        import numpy as np
        TOP_K = 2
        B, S, H = hidden_states.shape
        E = gate_w.shape[0]
        x = hidden_states.reshape(-1, H)
        T = x.shape[0]
        probs = jax.nn.softmax(x @ gate_w.T, axis=-1)
        w, idx = jax.lax.top_k(probs, TOP_K)
        w = w / jnp.sum(w, axis=-1, keepdims=True)
        combine = jnp.zeros((T, E), x.dtype).at[jnp.arange(T)[:, None], idx].add(w)

        def step(acc, inputs):
            gup, dn, ce = inputs
            g, u = jnp.split(x @ gup.T, 2, axis=-1)
            acc = acc + ce[:, None] * (jax.nn.silu(g) * u @ dn.T)
            return (acc, None)
        out, _ = jax.lax.scan(step, jnp.zeros_like(x), (gate_up_proj, down_proj, combine.T))
        return out.reshape(B, S, H)
    x = x + _L0_xattn_ref(_layernorm(x, axis=-1), ctx_1024, ctx_1024, L0_xattn_wq, L0_xattn_bq, L0_xattn_wk, L0_xattn_bk, L0_xattn_wv, L0_xattn_bv, L0_xattn_wo, L0_xattn_bo)
    x = x + _L0_ffn_ref(_layernorm(x, axis=-1), L0_ffn_w_router, L0_ffn_w_block)
    x = x + _L1_xattn_ref(_layernorm(x, axis=-1), ctx_1024, ctx_1024, mask_Bx1x1xS2_ff0, L1_xattn_Wq, L1_xattn_bq, L1_xattn_Wk, L1_xattn_bk, L1_xattn_Wv, L1_xattn_bv, L1_xattn_Wo, L1_xattn_bo)
    x = x + _L1_ffn_ref(_layernorm(x, axis=-1), L1_ffn_gate_w, L1_ffn_gate_up_proj, L1_ffn_down_proj)
    return x

_drawn_inputs = setup_inputs


def setup_inputs(seed=0):
    import zlib

    import numpy as np

    out = dict(_drawn_inputs(seed))
    spreads = {'L0_xattn_bq': (0.0, 0.1),
     'L0_xattn_bk': (0.0, 0.8),
     'L0_xattn_bv': (0.0, 0.1),
     'L0_xattn_bo': (0.0, 0.1),
     'L1_xattn_bq': (0.0, 0.1),
     'L1_xattn_bk': (0.0, 0.1),
     'L1_xattn_bv': (0.0, 0.1),
     'L1_xattn_bo': (0.0, 0.1)}
    factors = {'L1_ffn_gate_w': 4.804, 'L1_ffn_gate_up_proj': 4.278, 'L1_ffn_down_proj': 4.272}
    for name, (base, spread) in spreads.items():
        noise = np.random.default_rng([zlib.crc32(name.encode()), seed]).standard_normal(out[name].shape)
        drawn = base * np.exp(spread * noise) if base else spread * noise
        out[name] = jnp.asarray(drawn.astype(out[name].dtype))
    for name, factor in factors.items():
        out[name] = (out[name] * factor).astype(out[name].dtype)
    return out
```

```python
from contextlib import ExitStack

import numpy as np

import concourse.bass as bass
from concourse import mybir

P = 128
B, S, D = 8, 512, 256
SK = 64
H, DH = 16, 16
T = B * S
TJ = S // P
KD = D // P
HH = H // KD
NPAIR = H // 2
PH = NPAIR // 2
KEEP = int(S * 0.75)
E, F = 8, 1024
FC = F // P
TOPK = 2
TT = 256
MINT = 2
PAD = MINT * TT
CAP = T + PAD
NTMAX = T * TOPK // TT + MINT * E
ROW = D + E + 1
NEG = -1.0e9
EPS = 1e-5
SCALE = float(DH) ** -0.5

C_ID = 0
C_TRI = C_ID + P
C_SEL = C_TRI + P
C_MROW = C_SEL + NPAIR * P
C_BD = C_MROW + P
C_TRI8 = C_BD + HH
C_BASE = C_TRI8 + (E + 1) * E
C_N = C_BASE + E


def build(nc, x_in, ctxT_in, maskr_in, maskc_in, w_in, bcol_in, brow_in, wb_in, gate_in, gu_in, dn_in,
          const_in, tok_in, pad_in, zero_in, out):
    f32, f32r, bf16, i32 = mybir.dt.float32, mybir.dt.float32r, mybir.dt.bfloat16, mybir.dt.int32
    ALU, ACT, AX = mybir.AluOpType, mybir.ActivationFunctionType, mybir.AxisListType
    slots = nc.dram_tensor("slots", [E * CAP, ROW], f32).ap()
    ctx = ExitStack()
    ds = bass.ds

    def sb(name, shape, dt, c=None):
        return (c or ctx).enter_context(nc.sbuf_tensor(name, shape, dt))

    def sem(name):
        return ctx.enter_context(nc.semaphore(name))

    def flat(t):
        return t[:].rearrange("p k b r s -> p (k b r s)")

    def asf(ap):
        return ap.bitcast(f32)

    with ctx:
        bank = [ctx.enter_context(nc.psum_tensor(f"bank{i}", [P, 512], f32)) for i in range(8)]
        ident = sb("ident", [P, P], f32)
        bounds = sb("bounds", [1, E + 1 + E], i32)
        
        att = ExitStack()
        with att:
            a = lambda name, shape, dt: sb(name, shape, dt, att)
            x = a("x", [P, T // P, D], f32)
            const = a("const", [P, C_N], f32)
            tokid = a("tokid", [P, T // P], i32)
            sel = a("sel", [P, NPAIR * P], f32r)
            mrow = a("mrow", [P, P], f32r)
            trib = a("trib", [P, P], bf16)
            oneb = a("oneb", [P, P], bf16)
            oblk = a("oblk", [P, 2 * DH], f32)
            epst = a("epst", [P, 1], f32)
            wraw = a("wraw", [P, 4, KD, D], f32)
            whi = a("whi", [P, 4, KD, D], f32r)
            wlo = a("wlo", [P, 4, KD, D], f32r)
            bcol = a("bcol", [P, 2, 2, KD], f32)
            brow = a("brow", [P, 2, 2, D], f32)
            craw = a("craw", [P, KD, B, 2, SK], f32)
            chi = a("chi", [P, KD, B, 2, SK], f32r)
            clo = a("clo", [P, KD, B, 2, SK], f32r)
            khi = a("khi", [P, KD, B * SK], f32r)
            klo = a("klo", [P, KD, B * SK], f32r)
            kb = [a(f"kb{p}", [P, 2, KD, HH * SK], f32r) for p in range(2)]
            vall = a("vall", [P, B, NPAIR, 2 * DH], f32)
            vb = [a(f"vb{p}", [P, NPAIR, 2 * DH], f32) for p in range(2)]
            mraw = a("mraw", [P, B * SK], f32)
            mkr = a("mkr", [P, B * SK], f32r)
            mkc = a("mkc", [P, B], f32)
            mkb = [a(f"mkb{p}", [P, 1], f32) for p in range(2)]
            xn = a("xn", [P, TJ, ROW], f32)
            st = a("st", [P, TJ, 6], f32)
            mv = a("mv", [P, TJ, 2], f32)
            rs = a("rs", [P, 5, TJ], f32)
            xh = a("xh", [P, KD, S], f32r)
            xl = a("xl", [P, KD, S], f32r)
            qh = a("qh", [P, KD, S], f32r)
            ql = a("ql", [P, KD, S], f32r)
            mx = a("mx", [P, TJ, P], f32)
            mm = a("mm", [P, S], f32r)
            pr = a("pr", [P, NPAIR, S], f32)
            lnd = a("lnd", [P, S], f32)
            rec = a("rec", [P, S], f32)
            cf = a("cf", [P, KD, S], f32)
            ch = a("ch", [P, KD, S], f32r)
            cl = a("cl", [P, KD, S], f32r)
            wbraw = a("wbraw", [P, KD, D + 2], f32)
            wbh = a("wbh", [P, KD, D + 2], f32r)
            wbl = a("wbl", [P, KD, D + 2], f32r)
            gl = pr[:, 0:2, :].rearrange("p a (b d) -> p (a b) d", d=D)
            sc = a("sc", [P, TJ], f32)
            srow = a("srow", [P, S], f32)
            cmp1 = a("cmp1", [P, TJ, S], bf16)
            cmp2 = a("cmp2", [P, TJ, P], bf16)
            keep = a("keep", [P, 2, TJ], f32)
            gt = a("gt", [P, KD, E], f32)
            lg = a("lg", [P, TJ, E], f32)
            ex = a("ex", [P, TJ, E], f32)
            m1 = a("m1", [P, TJ], f32)
            r1 = a("r1", [P, TJ, E, E], f32)
            r2 = a("r2", [P, TJ, E, E], f32)
            rank = a("rank", [P, TJ, E], f32)
            pick = a("pick", [P, TJ, E], f32)
            pickb = a("pickb", [P, TJ, E], bf16)
            es = a("es", [P, TJ, E], f32)
            sm = a("sm", [P, 2, TJ], f32)
            run = a("run", [P, E], f32)
            slot = a("slot", [P, TJ, E], f32)
            s2 = a("s2", [P, TOPK, TJ, E], f32)
            sf = a("sf", [P, TOPK, TJ], f32)
            si = a("si", [P, TOPK, TJ], i32)
            cn = a("cn", [P, 4, E + 1], f32)
            ci = a("ci", [P, 2, E + 1], i32)

            n_ = {k: sem(k) for k in (
                "x0_in x_in const_in w0_in w1_in consts_ready w_hi w_lo kv_ps k_hi k_lo v_done mask_ready "
                "stats rstd_act rstd xn_ready xT_ps xT_hi xT_lo q_ps q_hi q_lo s_ps max_done max_twice mT_ps m_hi m_lo "
                "st_ps exp_done pv_ps ln_done rec_done ctx_f ctx_hi ctx_lo o_ps x_bo x_new kblk "
                "f_ps gelu score srow_ps srow cmp cnt_ps keep_ok ffn_t ffn_x bn newton passed passed_pool setup ln_act pool_setup "
                "lg_ps lg_sb exps sel_b pos_ps slot_ok scattered row_free xrow_ok x_out pads bounds_ok route counts").split()}
            g = type("Sems", (), n_)

            block = att.enter_context(nc.Block())

            def pipeline(eng, first, step, layer):
                first(layer * B)
                with eng.Fori(0, (B - 2) // 2) as i:
                    step(i * 2 + layer * B, i * 2, 0, True)
                    step(i * 2 + (layer * B + 1), i * 2 + 1, 1, True)
                step(layer * B + B - 2, B - 2, 0, True)
                step(layer * B + B - 1, B - 1, 1, False)

            @block.sync
            def _(sp):
                sp.dma_start(const[:], const_in).then_inc(g.const_in, 16)
                sp.dma_start(x[:, 0:TJ, :], x_in[0:S, :].rearrange("(t p) d -> p t d", p=P)).then_inc(g.x0_in, 16)
                for b in range(1, B):
                    sp.dma_start(x[:, b * TJ:(b + 1) * TJ, :],
                                 x_in[b * S:(b + 1) * S, :].rearrange("(t p) d -> p t d", p=P)).then_inc(g.x_in, 16)
                sp.dma_start(out[T:T + PAD, :], zero_in).then_inc(g.x_out, 16)
                with sp.Fori(0, B) as b:
                    sp.wait_ge(g.x_new, (b + B) * 2 + 3)
                    sp.dma_start(out[ds(b * S, S), :].rearrange("(t p) d -> p t d", p=P),
                                 x[:, ds(b * TJ, TJ), :]).then_inc(g.x_out, 16)
                sp.wait_ge(g.bounds_ok, 1)
                sp.wait_ge(g.scattered, B * TOPK * TJ * 16)
                with sp.Fori(0, E) as e:
                    r = sp.value_load(bounds[0:1, ds(e + (E + 1), 1)], min_val=0, max_val=E * CAP - PAD)
                    sp.dma_start(slots[ds(r, PAD), :], pad_in).then_inc(g.pads, 16)
                sp.wait_ge(g.pads, E * 16)
                sp.wait_ge(g.x_out, (B + 1) * 16)

            @block.gpsimd
            def _(pool):
                pool.sem_inc(g.row_free, 1)
                pool.memset(mm[:].bitcast(i32), 0)
                pool.memset(mkr[:].bitcast(i32), 0)
                pool.memset(mx[:], 0.0)
                pool.memset(oneb[:], 1.0)
                pool.memset(epst[:], EPS)
                pool.memset(oblk[:], 0.0)
                pool.memset(vall[:], 0.0).then_inc(g.pool_setup, 1)
                pool.wait_ge(g.pool_setup, 1)
                pool.memset(oblk[0:SK, 0:DH], 1.0)
                pool.memset(oblk[SK:P, DH:2 * DH], 1.0).then_inc(g.consts_ready, 1)

                def rstd(l):
                    pool.wait_ge(g.stats, l + 1)
                    pool.tensor_tensor(rs[:, 4, :], mv[:, :, 1], epst[:, 0:1].to_broadcast([P, TJ]), ALU.add)
                    pool.wait_ge(g.rstd_act, l + 1)
                    pool.tensor_tensor(rs[:, 2, :], rs[:, 1, :], rs[:, 1, :], ALU.mult).then_inc(g.newton, 1)
                    pool.wait_ge(g.newton, l * 3 + 1)
                    pool.tensor_tensor(rs[:, 2, :], rs[:, 4, :], rs[:, 2, :], ALU.mult).then_inc(g.newton, 1)
                    pool.wait_ge(g.newton, l * 3 + 2)
                    pool.sem_inc(g.passed_pool, 1)
                    pool.tensor_scalar(rs[:, 2, :], rs[:, 2, :], -0.5, 1.5, ALU.mult, ALU.add).then_inc(g.newton, 1)
                    pool.wait_ge(g.newton, l * 3 + 3)
                    pool.tensor_tensor(rs[:, 3, :], rs[:, 1, :], rs[:, 2, :], ALU.mult).then_inc(g.rstd, 1)

                def keys(layer, n, b, par):
                    if isinstance(n, int) and n % B == 0:
                        pool.wait_ge(g.k_lo, (layer + 1) * KD)
                        pool.wait_ge(g.v_done, (layer + 1) * B)
                    else:
                        pool.wait_ge(g.mT_ps, n)
                    for part, src in ((0, khi), (1, klo)):
                        for c in range(KD):
                            pool.tensor_tensor(
                                kb[par][:, part, c, :].rearrange("p (h k) -> p h k", h=HH),
                                asf(src[:, c, ds(b * SK, SK)]).unsqueeze(1).to_broadcast([P, HH, SK]),
                                const[:, C_BD:C_BD + HH].unsqueeze(2).to_broadcast([P, HH, SK]), ALU.mult)
                    if layer:
                        if isinstance(n, int) and n == B:
                            pool.wait_ge(g.mask_ready, 1)
                        pool.tensor_copy(mkb[par][:], mkc[:, ds(b, 1)])
                    pool.tensor_copy(vb[par][:].rearrange("p a b -> p (a b)"),
                                     vall[:, ds(b, 1), :, :].rearrange("p o a b -> p (o a b)")).then_inc(g.kblk, 1)

                def add_bo(layer, n, l, b):
                    pool.wait_ge(g.xn_ready, l + 1)
                    xb = x[:, ds(b * TJ, TJ), :]
                    pool.tensor_tensor(xb, xb, brow[:, layer, 1, :].unsqueeze(1).to_broadcast([P, TJ, D]),
                                       ALU.add).then_inc(g.x_bo, 1)

                for layer in range(2):
                    pool.wait_ge(g.const_in, 16)
                    pool.wait_ge(g.w0_in, 64)

                    def first(n):
                        rstd(n + layer * B)
                        add_bo(layer, n, n + layer * B, 0)
                        keys(layer, n, 0, 0)

                    def step(n, b, par, nxt):
                        if nxt:
                            rstd(n + (1 + layer * B))
                            add_bo(layer, n + 1, n + (1 + layer * B), b + 1)
                            keys(layer, n + 1, b + 1, 1 - par)

                    pipeline(pool, first, step, layer)
                    if layer == 0:
                        with pool.Fori(0, B) as b:
                            rstd(b + B)
                with pool.Fori(0, B) as b:
                    rstd(b + 3 * B)
                    pool.wait_ge(g.slot_ok, b + 1)
                    pool.wait_ge(g.xrow_ok, b + 1)
                    pool.sem_inc(g.passed_pool, 1)
                    for kk in range(TOPK):
                        for j in range(TJ):
                            pool.indirect_dma_start(slots, bass.IndirectOffsetOnAxis(ap=si[:, kk, j:j + 1], axis=0),
                                                    xn[:, j, :], None).then_inc(g.scattered, 16)
                    pool.wait_ge(g.scattered, b * (TOPK * TJ * 16) + TOPK * TJ * 16)
                    pool.sem_inc(g.row_free, 1)
                pool.wait_ge(g.scattered, B * TOPK * TJ * 16)

            @block.scalar
            def _(act):
                act.dma_start(wraw[:], w_in[0]).then_inc(g.w0_in, 16)
                act.dma_start(craw[:], ctxT_in).then_inc(g.w0_in, 16)
                act.dma_start(bcol[:], bcol_in).then_inc(g.w0_in, 16)
                act.dma_start(brow[:], brow_in).then_inc(g.w0_in, 16)
                act.dma_start(wbraw[:], wb_in).then_inc(g.w1_in, 16)
                act.dma_start(gt[:], gate_in).then_inc(g.w1_in, 16)
                act.dma_start(tokid[:], tok_in).then_inc(g.w1_in, 16)
                for r in (0, 32):
                    act.dma_start(mraw[r:r + 1, :], maskr_in).then_inc(g.w1_in, 16)
                act.dma_start(mkc[:], maskc_in).then_inc(g.w1_in, 16)

                def rstd(l):
                    act.wait_ge(g.stats, l + 1)
                    act.activation(rs[:, 0, :], mv[:, :, 1], ACT.Ln, bias=epst[:, 0:1]).then_inc(g.ln_act, 1)
                    act.wait_ge(g.ln_act, l + 1)
                    act.activation(rs[:, 1, :], rs[:, 0, :], ACT.Exp, scale=-0.5).then_inc(g.rstd_act, 1)

                def xT(l):
                    for c in range(KD):
                        act.wait_ge(g.xT_ps, l * KD + (c + 1))
                        act.activation(xh[:, c, :], bank[c][:], ACT.Copy).then_inc(g.xT_hi, 1)

                for layer in range(2):
                    if layer:
                        act.wait_ge(g.o_ps, 2 * B)
                        act.wait_ge(g.w_lo, 1)
                        act.dma_start(wraw[:], w_in[1]).then_inc(g.w0_in, 16)
                        act.wait_ge(g.w0_in, 80)
                    else:
                        act.wait_ge(g.w0_in, 64)
                        act.activation(flat(chi), flat(craw), ACT.Copy)
                        act.wait_ge(g.consts_ready, 1)
                    act.activation(whi[:], wraw[:], ACT.Copy).then_inc(g.w_hi, 1)
                    for c in range(KD):
                        act.wait_ge(g.kv_ps, (layer * (KD + B)) + c + 1)
                        act.activation(khi[:, c, :], bank[c][:], ACT.Identity, bias=bcol[:, layer, 1, c:c + 1]).then_inc(g.k_hi, 1)

                    def q_hi(n):
                        for c in range(KD):
                            act.wait_ge(g.q_ps, n * KD + (c + 1))
                            act.activation(qh[:, c, :], bank[c][:], ACT.Identity, bias=bcol[:, layer, 0, c:c + 1]).then_inc(g.q_hi, 1)

                    def m_hi(n):
                        act.wait_ge(g.mT_ps, n + 1)
                        act.activation(mm[0:64, :], bank[2][0:64, :], ACT.Copy, scale=-1.0).then_inc(g.m_hi, 1)

                    def exps(n, par, pairs):
                        for p in pairs:
                            act.wait_ge(g.st_ps, n * NPAIR + (p + 1))
                            act.activation(pr[:, p, :], bank[4 + p % 2][:], ACT.Exp, scale=SCALE,
                                           bias=mkb[par][:, 0:1] if layer else 0.0).then_inc(g.exp_done, 1)

                    def recip(n, h):
                        act.wait_ge(g.pv_ps, n * KD + (h + 1))
                        act.activation(lnd[:], bank[7][:], ACT.Ln).then_inc(g.ln_done, 1)
                        act.wait_ge(g.ln_done, n * KD + (h + 1))
                        act.activation(rec[:], lnd[:], ACT.Exp, scale=-1.0).then_inc(g.rec_done, 1)

                    def ctx_hi(n, h):
                        act.wait_ge(g.ctx_f, n * KD + (h + 2))
                        act.activation(ch[:, h, :], cf[:, h, :], ACT.Copy).then_inc(g.ctx_hi, 1)

                    def first(n):
                        rstd(n + layer * B)
                        xT(n + layer * B)
                        q_hi(n)
                        m_hi(n)

                    def step(n, b, par, nxt):
                        exps(n, par, (0, 1))
                        if nxt:
                            rstd(n + (1 + layer * B))
                        exps(n, par, (2, 3, 4, 5))
                        recip(n, 0)
                        exps(n, par, (6, 7))
                        if nxt:
                            xT(n + (1 + layer * B))
                        ctx_hi(n, 0)
                        recip(n, 1)
                        if nxt:
                            q_hi(n + 1)
                        ctx_hi(n, 1)
                        if nxt:
                            m_hi(n + 1)

                    if layer == 0:
                        act.sem_inc(g.exp_done, 2)
                    else:
                        act.wait_ge(g.mask_ready, 1)
                    pipeline(act, first, step, layer)

                    if layer == 0:
                        with act.Fori(0, B) as b:
                            rstd(b + B)
                            xT(b + B)
                            for j in range(TJ):
                                act.wait_ge(g.f_ps, b * TJ + (j + 1))
                                act.activation(gl[:, j, :], bank[2 + j][:, 0:D], ACT.Gelu_apprx_tanh).then_inc(g.gelu, 1)
                            act.wait_ge(g.srow_ps, b + 1)
                            act.activation(srow[:], bank[6][:], ACT.Copy).then_inc(g.srow, 1)

                with act.Fori(0, B) as b:
                    rstd(b + 3 * B)
                    for c in range(KD):
                        act.wait_ge(g.xT_ps, (b + 3 * B) * KD + (c + 1))
                        act.activation(cf[:, c, :], bank[c][:], ACT.Copy).then_inc(g.xT_hi, 1)
                    act.wait_ge(g.lg_sb, b + 1)
                    act.activation(ex[:], es[:], ACT.Exp).then_inc(g.exps, 1)

            @block.tensor
            def _(pe):
                def three(o, ahi, alo, bhi, blo, first=True, last=True):
                    n = len(ahi)
                    for c in range(n):
                        pe.matmul(o, ahi[c], bhi[c], start=first and c == 0, stop=False)
                        pe.matmul(o, ahi[c], blo[c], start=False, stop=False)
                        ins = pe.matmul(o, alo[c], bhi[c], start=False, stop=last and c == n - 1)
                    return ins

                def tr(l):
                    pe.wait_ge(g.xn_ready, l + 1)
                    for c in range(KD):
                        for j in range(TJ):
                            ins = pe.transpose(bank[c][:, j * P:(j + 1) * P], xn[:, j, c * P:(c + 1) * P], ident[:])
                        ins.then_inc(g.xT_ps, 1)

                pe.wait_ge(g.consts_ready, 2)
                for layer in range(2):
                    pe.wait_ge(g.w_lo, layer + 1)
                    if layer:
                        pe.wait_ge(g.ffn_x, B + 1)
                    for c in range(KD):
                        three(bank[c][:], [whi[:, 1, k, c * P:(c + 1) * P] for k in range(KD)],
                              [wlo[:, 1, k, c * P:(c + 1) * P] for k in range(KD)],
                              [chi[:, k, :, 0, :] for k in range(KD)], [clo[:, k, :, 0, :] for k in range(KD)]).then_inc(g.kv_ps, 1)
                    for b in range(B):
                        if b >= 2:
                            pe.wait_ge(g.v_done, layer * B + b - 1)
                        dup = lambda t, k: t[:, k, b, :, :].rearrange("p r k -> p (r k)")
                        three(bank[4 + b % 2][:, 0:D], [dup(chi, k) for k in range(KD)], [dup(clo, k) for k in range(KD)],
                              [whi[:, 2, k, :] for k in range(KD)], [wlo[:, 2, k, :] for k in range(KD)]).then_inc(g.kv_ps, 1)

                    def q_proj(n, l):
                        pe.wait_ge(g.xT_lo, l * KD + KD)
                        for c in range(KD):
                            three(bank[c][:], [whi[:, 0, k, c * P:(c + 1) * P] for k in range(KD)],
                                  [wlo[:, 0, k, c * P:(c + 1) * P] for k in range(KD)],
                                  [xh[:, k, :] for k in range(KD)], [xl[:, k, :] for k in range(KD)]).then_inc(g.q_ps, 1)

                    def maxima(n, b, par):
                        pe.wait_ge(g.q_hi, n * KD + KD)
                        pe.wait_ge(g.kblk, n + 1)
                        for u in range(TJ * KD):
                            j, c = u // KD, u % KD
                            pe.wait_ge(g.max_done, n * TJ * KD + (u + 1))
                            ins = pe.matmul(bank[2 + c][:], qh[:, c, j * P:(j + 1) * P], kb[par][:, 0, c, :],
                                            start=True, stop=not layer)
                            if layer:
                                ins = pe.matmul(bank[2 + c][:], mrow[:], mkr[:, ds(b * SK, SK)].unsqueeze(1).to_broadcast([P, HH, SK]),
                                                start=False, stop=True)
                            ins.then_inc(g.s_ps, 1)

                    def maxima_T(n):
                        pe.wait_ge(g.max_twice, n + 1)
                        for j in range(TJ):
                            ins = pe.transpose(bank[2][:, j * P:(j + 1) * P], mx[:, j, :], ident[:])
                        ins.then_inc(g.mT_ps, 1)

                    def scores(n, par, pairs):
                        for p in pairs:
                            c, o = p // PH, (p % PH) * P
                            pe.wait_ge(g.exp_done, n * NPAIR + (p + 1))
                            k_ = kb[par]
                            three(bank[4 + p % 2][:], [k_[:, 0, c, o:o + P]], [k_[:, 1, c, o:o + P]],
                                  [qh[:, c, :]], [ql[:, c, :]], last=False)
                            pe.matmul(bank[4 + p % 2][:], sel[:, p * P:(p + 1) * P], mm[:], start=False, stop=True).then_inc(g.st_ps, 1)

                    def values(n, par, h):
                        pe.wait_ge(g.exp_done, n * NPAIR + (PH * (h + 1) + 2))
                        pe.wait_ge(g.ctx_f, n * KD + (h + 1))
                        for dst, w in ((6, None), (7, oblk)):
                            for j in range(PH):
                                p = h * PH + j
                                ins = pe.matmul(bank[dst][32 * j:32 * j + 32, :], vb[par][:, p, :] if w is None else w[:],
                                                pr[:, p, :], start=True, stop=True)
                        ins.then_inc(g.pv_ps, 1)

                    def out_proj(n):
                        pe.wait_ge(g.ctx_lo, n * KD + KD)
                        for u in range(2):
                            for t in range(2):
                                j = 2 * u + t
                                ins = three(bank[u][:, t * D:(t + 1) * D], [ch[:, k, j * P:(j + 1) * P] for k in range(KD)],
                                            [cl[:, k, j * P:(j + 1) * P] for k in range(KD)],
                                            [whi[:, 3, k, :] for k in range(KD)], [wlo[:, 3, k, :] for k in range(KD)])
                            ins.then_inc(g.o_ps, 1)

                    def first(n):
                        pe.wait_ge(g.k_lo, (layer + 1) * KD)
                        pe.wait_ge(g.v_done, (layer + 1) * B)
                        if layer:
                            pe.wait_ge(g.mask_ready, 1)
                        tr(n + layer * B)
                        q_proj(n, n + layer * B)
                        maxima(n, 0, 0)
                        maxima_T(n)

                    def step(n, b, par, nxt):
                        pe.wait_ge(g.q_lo, n * KD + KD)
                        pe.wait_ge(g.m_lo, n + 1)
                        scores(n, par, range(0, 6))
                        values(n, par, 0)
                        scores(n, par, (6, 7))
                        if nxt:
                            pe.wait_ge(g.x_new, n * 2 + 1)
                            tr(n + (1 + layer * B))
                        values(n, par, 1)
                        if nxt:
                            q_proj(n + 1, n + (1 + layer * B))
                            maxima(n + 1, b + 1, 1 - par)
                            pe.wait_ge(g.q_lo, (n + 1) * KD + KD)
                        out_proj(n)
                        if nxt:
                            maxima_T(n + 1)

                    pipeline(pe, first, step, layer)

                    if layer == 0:
                        with pe.Fori(0, B) as b:
                            pe.wait_ge(g.x_new, B * 2 + 1)
                            tr(b + B)
                            pe.wait_ge(g.xT_lo, (b + B) * KD + KD)
                            for j in range(TJ):
                                if j == 0:
                                    pe.wait_ge(g.ffn_x, b + 1)
                                three(bank[2 + j][:, 0:D + 2], [xh[:, k, j * P:(j + 1) * P] for k in range(KD)],
                                      [xl[:, k, j * P:(j + 1) * P] for k in range(KD)],
                                      [wbh[:, k, :] for k in range(KD)], [wbl[:, k, :] for k in range(KD)]).then_inc(g.f_ps, 1)
                            pe.wait_ge(g.score, b + 1)
                            for j in range(TJ):
                                ins = pe.transpose(bank[6][:, j * P:(j + 1) * P], sc[:, j:j + 1].to_broadcast([P, P]), ident[:])
                            ins.then_inc(g.srow_ps, 1)
                            pe.wait_ge(g.cmp, b + 1)
                            for i in range(TJ):
                                for j in range(TJ):
                                    pe.matmul(bank[7][:, i:i + 1], cmp1[:, j, i * P:(i + 1) * P], oneb[:, 0:1], start=j == 0, stop=False)
                                ins = pe.matmul(bank[7][:, i:i + 1], cmp2[:, i, :], oneb[:, 0:1], start=False, stop=True)
                            ins.then_inc(g.cnt_ps, 1)

                with pe.Fori(0, B) as b:
                    pe.wait_ge(g.xT_hi, (b + 3 * B) * KD)
                    pe.wait_ge(g.x_new, B * 4 + 1)
                    tr(b + 3 * B)
                    pe.wait_ge(g.xT_hi, (b + 3 * B) * KD + KD)
                    for j in range(TJ):
                        for k in range(KD):
                            ins = pe.matmul(bank[2][:, j * E:(j + 1) * E], cf[:, k, j * P:(j + 1) * P], gt[:, k, :],
                                            start=k == 0, stop=k == KD - 1)
                    ins.then_inc(g.lg_ps, 1)
                    pe.wait_ge(g.sel_b, b + 1)
                    for j in range(TJ):
                        for i in range(j):
                            pe.matmul(bank[3][:, j * E:(j + 1) * E], oneb[:], pickb[:, i, :], start=i == 0, stop=False)
                        pe.matmul(bank[3][:, j * E:(j + 1) * E], trib[:], pickb[:, j, :], start=j == 0, stop=True)
                    for i in range(TJ):
                        ins = pe.matmul(bank[3][:, TJ * E:(TJ + 1) * E], oneb[:], pickb[:, i, :], start=i == 0, stop=i == TJ - 1)
                    ins.then_inc(g.pos_ps, 1)

            @block.vector
            def _(v):
                v.wait_ge(g.const_in, 16)
                v.tensor_copy(ident[:], const[:, C_ID:C_ID + P])
                v.tensor_copy(trib[:], const[:, C_TRI:C_TRI + P])
                v.tensor_copy(sel[:], const[:, C_SEL:C_SEL + NPAIR * P])
                v.tensor_copy(mrow[:], const[:, C_MROW:C_MROW + P])
                v.tensor_copy(run[:], const[:, C_BASE:C_BASE + E])
                v.sem_inc(g.ctx_f, 1)
                v.sem_inc(g.x_new, 1)
                v.sem_inc(g.max_done, 2)
                v.sem_inc(g.ffn_x, 1)
                v.wait_ge(g.consts_ready, 1)
                v.wait_ge(g.w1_in, 96)
                v.tensor_copy(wbh[:], wbraw[:]).then_inc(g.setup, 1)
                for r in (0, 32):
                    v.tensor_scalar(mraw[r:r + 1, :], mraw[r:r + 1, :], NEG, 1.0 / SCALE, ALU.mult, ALU.mult)
                v.tensor_scalar(mkc[:], mkc[:], NEG, None, ALU.mult).then_inc(g.setup, 1)
                v.wait_ge(g.setup, 2)
                for r in (0, 32):
                    last = v.tensor_copy(mkr[r:r + 1, :], mraw[r:r + 1, :])
                last.then_inc(g.setup, 1)
                v.wait_ge(g.setup, 3)
                v.tensor_tensor(mkr[32:33, :], mraw[32:33, :], asf(mkr[32:33, :]), ALU.subtract).then_inc(g.mask_ready, 1)
                v.tensor_tensor(wbl[:], wbraw[:], asf(wbh[:]), ALU.subtract).then_inc(g.consts_ready, 1)

                def norm_a(l, b):
                    for j in range(TJ):
                        ins = v.bn_stats(st[:, j, :], x[:, ds(b * TJ + j, 1), :].rearrange("p o d -> p (o d)"))
                    ins.then_inc(g.bn, 1)
                    v.wait_ge(g.bn, l + 1)
                    v.sem_inc(g.passed, 1)
                    for j in range(TJ):
                        ins = v.bn_aggr(mv[:, j, :], st[:, j, :])
                    ins.then_inc(g.stats, 1)

                def norm_b(l, b):
                    v.wait_ge(g.rstd, l + 1)
                    if not isinstance(l, int) or l:
                        v.wait_ge(g.xT_ps, l * KD)
                    for j in range(TJ):
                        ins = v.tensor_scalar(xn[:, j, 0:D], x[:, ds(b * TJ + j, 1), :].rearrange("p o d -> p (o d)"),
                                              mv[:, j, 0:1], rs[:, 3, j:j + 1], ALU.subtract, ALU.mult)
                    ins.then_inc(g.xn_ready, 1)

                def xT_lo(l):
                    for c in range(KD):
                        v.wait_ge(g.xT_hi, l * KD + (c + 1))
                        v.tensor_tensor(xl[:, c, :], bank[c][:], asf(xh[:, c, :]), ALU.subtract).then_inc(g.xT_lo, 1)

                for layer in range(2):
                    v.wait_ge(g.w_hi, layer + 1)
                    if layer == 0:
                        v.tensor_tensor(flat(clo), flat(craw), asf(flat(chi)), ALU.subtract)
                    v.tensor_tensor(wlo[:], wraw[:], asf(whi[:]), ALU.subtract).then_inc(g.w_lo, 1)
                    for c in range(KD):
                        v.wait_ge(g.k_hi, layer * KD + c + 1)
                        v.scalar_tensor_tensor(klo[:, c, :], bank[c][:], bcol[:, layer, 1, c:c + 1], asf(khi[:, c, :]),
                                               ALU.add, ALU.subtract).then_inc(g.k_lo, 1)
                    for b in range(B):
                        v.wait_ge(g.kv_ps, layer * (KD + B) + KD + b + 1)
                        for r in range(2):
                            q = slice(r * SK, (r + 1) * SK)
                            hd = slice(r * DH, (r + 1) * DH)
                            ins = v.tensor_tensor(vall[q, b, :, hd],
                                                  bank[4 + b % 2][q, 0:D].rearrange("p (n c) -> p n c", c=2 * DH)[:, :, hd],
                                                  brow[q, layer, 0, :].rearrange("p (n c) -> p n c", c=2 * DH)[:, :, hd], ALU.add)
                        ins.then_inc(g.v_done, 1)

                    def q_lo(n):
                        for c in range(KD):
                            v.wait_ge(g.q_hi, n * KD + (c + 1))
                            v.scalar_tensor_tensor(ql[:, c, :], bank[c][:], bcol[:, layer, 0, c:c + 1], asf(qh[:, c, :]),
                                                   ALU.add, ALU.subtract).then_inc(g.q_lo, 1)

                    def maxes(n):
                        for u in range(TJ * KD):
                            j, c = u // KD, u % KD
                            v.wait_ge(g.s_ps, n * TJ * KD + (u + 1))
                            v.tensor_reduce(mx[:, j, c * HH:(c + 1) * HH], bank[2 + c][:].rearrange("p (h k) -> p h k", k=SK),
                                            AX.X, ALU.max).then_inc(g.max_done, 1)
                        v.wait_ge(g.max_done, n * TJ * KD + (TJ * KD + 2))
                        v.tensor_copy(mx[:, :, 32:32 + H], mx[:, :, 0:H]).then_inc(g.max_twice, 1)

                    def m_lo(n):
                        v.wait_ge(g.m_hi, n + 1)
                        v.scalar_tensor_tensor(mm[32:64, :], bank[2][32:64, :], -1.0, asf(mm[32:64, :]),
                                               ALU.mult, ALU.subtract).then_inc(g.m_lo, 1)

                    def ctx_f(n, h):
                        v.wait_ge(g.rec_done, n * KD + (h + 1))
                        v.tensor_tensor(cf[:, h, :], bank[6][:], rec[:], ALU.mult).then_inc(g.ctx_f, 1)

                    def ctx_lo(n, h):
                        v.wait_ge(g.ctx_hi, n * KD + (h + 1))
                        v.tensor_tensor(cl[:, h, :], cf[:, h, :], asf(ch[:, h, :]), ALU.subtract).then_inc(g.ctx_lo, 1)

                    def x_up(n, b):
                        v.wait_ge(g.x_bo, n + 1)
                        for u in range(2):
                            v.wait_ge(g.o_ps, n * 2 + (u + 1))
                            xb = x[:, ds(b * TJ + 2 * u, 2), :]
                            v.tensor_tensor(xb, bank[u][:].rearrange("p (t d) -> p t d", t=2), xb, ALU.add).then_inc(g.x_new, 1)

                    def first(n):
                        if layer == 0:
                            v.wait_ge(g.x0_in, 16)
                        norm_a(n + layer * B, 0)
                        norm_b(n + layer * B, 0)
                        xT_lo(n + layer * B)
                        q_lo(n)
                        maxes(n)
                        m_lo(n)

                    def step(n, b, par, nxt):
                        l = n + (1 + layer * B)
                        if nxt:
                            norm_a(l, b + 1)
                            norm_b(l, b + 1)
                        ctx_f(n, 0)
                        if nxt:
                            xT_lo(l)
                        ctx_lo(n, 0)
                        ctx_f(n, 1)
                        if nxt:
                            q_lo(n + 1)
                        ctx_lo(n, 1)
                        if nxt:
                            maxes(n + 1)
                        x_up(n, b)
                        if nxt:
                            m_lo(n + 1)

                    if layer == 0:
                        v.wait_ge(g.x_in, (B - 1) * 16)
                    pipeline(v, first, step, layer)

                    if layer == 0:
                        with v.Fori(0, B) as b:
                            l = b + B
                            v.wait_ge(g.x_new, B * 2 + 1)
                            norm_a(l, b)
                            norm_b(l, b)
                            xT_lo(l)
                            for j in range(TJ):
                                v.wait_ge(g.gelu, b * TJ + (j + 1))
                                ins = v.tensor_copy(sc[:, j:j + 1], bank[2 + j][:, D:D + 1])
                            ins.then_inc(g.score, 1)
                            v.wait_ge(g.srow, b + 1)
                            for j in range(TJ):
                                w = (j + 1) * P
                                ins = v.tensor_scalar(cmp1[:, j, 0:w], srow[:, 0:w], sc[:, j:j + 1], None, ALU.is_lt)
                                if j < TJ - 1:
                                    ins = v.tensor_scalar(cmp1[:, j, w:S], srow[:, w:S], sc[:, j:j + 1], None, ALU.is_le)
                                ins = v.scalar_tensor_tensor(cmp2[:, j, :], srow[:, w - P:w], sc[:, j:j + 1],
                                                             const[:, C_TRI:C_TRI + P], ALU.is_equal, ALU.mult)
                            ins.then_inc(g.cmp, 1)
                            v.wait_ge(g.cnt_ps, b + 1)
                            v.tensor_scalar(keep[:, 0, :], bank[7][:, 0:TJ], float(KEEP), None, ALU.is_lt)
                            v.tensor_scalar(keep[:, 1, :], bank[7][:, 0:TJ], float(KEEP), None, ALU.is_ge).then_inc(g.keep_ok, 1)
                            v.wait_ge(g.keep_ok, b + 1)
                            xs = lambda j: x[:, ds(b * TJ + j, 1), :].rearrange("p o d -> p (o d)")
                            for j in range(TJ):
                                ins = v.scalar_tensor_tensor(xs(j), xn[:, j, 0:D], keep[:, 1, j:j + 1], xs(j), ALU.mult, ALU.add)
                            ins.then_inc(g.ffn_t, 1)
                            v.wait_ge(g.ffn_t, b + 1)
                            for j in range(TJ):
                                ins = v.scalar_tensor_tensor(xs(j), gl[:, j, :], keep[:, 0, j:j + 1], xs(j), ALU.mult, ALU.add)
                            ins.then_inc(g.ffn_x, 1)
                        v.wait_ge(g.ffn_x, B + 1)

                tri8 = const[:, C_TRI8:C_TRI8 + E * E].rearrange("p (e f) -> p e f", f=E)
                k = 15
                with v.Fori(0, B) as b:
                    c = [0]

                    def dep(ins):
                        c[0] += 1
                        ins.then_inc(g.route, 1)
                        v.wait_ge(g.route, b * k + c[0])

                    l = b + 3 * B
                    v.wait_ge(g.x_new, B * 4 + 1)
                    norm_a(l, b)
                    v.wait_ge(g.row_free, b + 1)
                    norm_b(l, b)
                    v.wait_ge(g.lg_ps, b + 1)
                    dep(v.tensor_copy(lg[:].rearrange("p t e -> p (t e)"), bank[2][:, 0:TJ * E]))
                    dep(v.tensor_reduce(m1[:], lg[:], AX.X, ALU.max))
                    v.tensor_tensor(es[:], lg[:], m1[:].unsqueeze(2).to_broadcast([P, TJ, E]), ALU.subtract).then_inc(g.lg_sb, 1)
                    lf = lg[:].unsqueeze(2).to_broadcast([P, TJ, E, E])
                    le = lg[:].unsqueeze(3).to_broadcast([P, TJ, E, E])
                    v.tensor_tensor(r1[:], lf, le, ALU.is_gt)
                    dep(v.tensor_tensor(r2[:], lf, le, ALU.is_equal))
                    dep(v.tensor_tensor(r2[:], r2[:], tri8.unsqueeze(1).to_broadcast([P, TJ, E, E]), ALU.mult))
                    dep(v.tensor_tensor(r1[:], r1[:], r2[:], ALU.add))
                    dep(v.tensor_reduce(rank[:], r1[:], AX.X, ALU.add))
                    v.tensor_scalar(pickb[:], rank[:], float(TOPK), None, ALU.is_lt).then_inc(g.sel_b, 1)
                    dep(v.tensor_scalar(pick[:], rank[:], float(TOPK), None, ALU.is_lt))
                    v.wait_ge(g.exps, b + 1)
                    dep(v.tensor_tensor(es[:], ex[:], pick[:], ALU.mult))
                    dep(v.tensor_reduce(sm[:, 0, :], es[:], AX.X, ALU.add))
                    dep(v.reciprocal(sm[:, 1, :], sm[:, 0, :]))
                    v.tensor_tensor(xn[:, :, D:D + E], es[:], sm[:, 1, :].unsqueeze(2).to_broadcast([P, TJ, E]), ALU.mult)
                    v.tensor_copy(xn[:, :, D + E].bitcast(i32), tokid[:, ds(b * TJ, TJ)]).then_inc(g.xrow_ok, 1)
                    v.wait_ge(g.pos_ps, b + 1)
                    dep(v.tensor_tensor(slot[:], bank[3][:, 0:TJ * E].rearrange("p (t e) -> p t e", e=E),
                                        run[:].unsqueeze(1).to_broadcast([P, TJ, E]), ALU.add))
                    dep(v.tensor_tensor(run[:], run[:], bank[3][:, TJ * E:(TJ + 1) * E], ALU.add))
                    for kk in range(TOPK):
                        ins = v.scalar_tensor_tensor(s2[:, kk, :, :], rank[:], float(kk), slot[:], ALU.is_equal, ALU.mult)
                    dep(ins)
                    dep(v.tensor_reduce(sf[:], s2[:], AX.X, ALU.add))
                    v.tensor_copy(si[:], sf[:]).then_inc(g.slot_ok, 1)
                    dep(v.engine_nop())
                    assert c[0] == k, c
                t = [0]

                def dep(ins):
                    t[0] += 1
                    ins.then_inc(g.counts, 1)
                    v.wait_ge(g.counts, t[0])

                v.tensor_copy(ci[:, 1, 0:E], run[:])
                dep(v.tensor_tensor(cn[:, 0, 0:E], run[:], const[:, C_BASE:C_BASE + E], ALU.subtract))
                dep(v.tensor_scalar(cn[:, 1, 0:E], cn[:, 0, 0:E], float(TT - 1), None, ALU.add))
                dep(v.tensor_copy(ci[:, 0, 0:E], cn[:, 1, 0:E]))
                dep(v.tensor_scalar(ci[:, 0, 0:E], ci[:, 0, 0:E], TT.bit_length() - 1, None, ALU.logical_shift_right))
                dep(v.tensor_copy(cn[:, 2, 0:E], ci[:, 0, 0:E]))
                dep(v.tensor_scalar(cn[:, 2, 0:E], cn[:, 2, 0:E], float(MINT), None, ALU.max))
                dep(v.tensor_tensor(r1[:].rearrange("p a b c -> p (a b c)")[:, 0:(E + 1) * E].rearrange("p (e f) -> p e f", f=E),
                                    cn[:, 2, 0:E].unsqueeze(1).to_broadcast([P, E + 1, E]),
                                    const[:, C_TRI8:C_TRI8 + (E + 1) * E].rearrange("p (e f) -> p e f", f=E), ALU.mult))
                dep(v.tensor_reduce(cn[:, 3, :], r1[:].rearrange("p a b c -> p (a b c)")[:, 0:(E + 1) * E].rearrange("p (e f) -> p e f", f=E),
                                    AX.X, ALU.add))
                v.tensor_copy(bounds[0:1, 0:E + 1], cn[0:1, 3, :])
                v.tensor_copy(bounds[0:1, E + 1:2 * E + 1], ci[0:1, 1, 0:E]).then_inc(g.bounds_ok, 1)
        moe(nc, sb, sem, bank, ident, bounds, slots, gu_in, dn_in, out)


def moe(nc, sb, sem, bank, ident, bounds, slots, gu_in, dn_in, out):
    f32, f32r, i32 = mybir.dt.float32, mybir.dt.float32r, mybir.dt.int32
    ALU, ACT = mybir.AluOpType, mybir.ActivationFunctionType
    ds = bass.ds
    SJ = TT // P
    GC = 2 * F // FC
    NB = 4
    with ExitStack() as m:
        a = lambda name, shape, dt: sb(name, shape, dt, m)
        graw = a("graw", [P, KD, 2 * F], f32)
        draw = a("draw", [P, FC, D], f32)
        gw = [[a(f"gw{p}{h}", [P, KD, 2 * F], f32r) for h in "hl"] for p in range(2)]
        dw = [[a(f"dw{p}{h}", [P, FC, D], f32r) for h in "hl"] for p in range(2)]
        xs = a("xs", [P, SJ, ROW], f32)
        xh = a("mxh", [P, KD * TT], f32r)
        xl = a("mxl", [P, KD * TT], f32r)
        sg = [a(f"sg{i}", [P, TT], f32) for i in range(2)]
        hf = [a(f"hf{i}", [P, TT], f32) for i in range(4)]
        hh = a("hh", [P, FC, TT], f32r)
        hl = a("hl", [P, FC, TT], f32r)
        meta = [a(f"meta{i}", [P, SJ, E + 1], f32) for i in range(2)]
        wt = a("wt", [P, SJ, 1], f32)
        tk = a("tk", [P, SJ, 1], i32)
        y = a("y", [P, SJ, D], f32)
        g = type("Sems", (), {k: sem("e_" + k) for k in (
            "w_in w_hi w_lo x_in x_read xT_ps xT_hi xT_lo gu_ps silu h_f h_hi h_lo y_ps y_ok meta wt_ok added y_free passed").split()})
        block = m.enter_context(nc.Block())

        def experts(eng, tile, before=None):
            def expert(e, par, more):
                lo = eng.value_load(bounds[0:1, ds(e, 1)], min_val=0, max_val=NTMAX - MINT)
                hi = eng.value_load(bounds[0:1, ds(e + 1, 1)], min_val=MINT, max_val=NTMAX)
                if before:
                    before(e)
                tile(lo, e, lo, par, more)
                with eng.Fori(lo + 1, hi) as t:
                    tile(t, e, lo, par, False)

            with eng.Fori(0, E // 2 - 1) as e2:
                expert(e2 * 2, 0, True)
                expert(e2 * 2 + 1, 1, True)
            expert(E - 2, 0, True)
            expert(E - 1, 1, False)

        @block.sync
        def _(sp):
            sp.dma_start(graw[:], gu_in[0]).then_inc(g.w_in, 16)
            sp.dma_start(draw[:], dn_in[0]).then_inc(g.w_in, 16)

            def tile(t, e, lo, par, more):
                sp.wait_ge(g.x_read, t + 1)
                row = nc.s_assert_within(e * CAP + (t - lo) * TT, 0, E * CAP - TT,
                                         skip_runtime_bounds_check_because="an expert has at most CAP / TT tiles")
                sp.dma_start(xs[:], slots[ds(row, TT), :].rearrange("(s p) r -> p s r", p=P)).then_inc(g.x_in, 16)

            experts(sp, tile)
            last = sp.value_load(bounds[0:1, E:E + 1], min_val=MINT, max_val=NTMAX)
            sp.wait_ge(g.x_read, last + 1)
            sp.dma_start(xs[:], slots[0:TT, :].rearrange("(s p) r -> p s r", p=P)).then_inc(g.x_in, 16)

        @block.gpsimd
        def _(pool):
            pool.sem_inc(g.y_free, 1)
            last = pool.value_load(bounds[0:1, E:E + 1], min_val=MINT, max_val=NTMAX)
            with pool.Fori(0, last) as t:
                pool.wait_ge(g.y_ok, t + 2)
                pool.sem_inc(g.passed, 1)
                for s in range(SJ):
                    pool.indirect_dma_start(out, bass.IndirectOffsetOnAxis(ap=tk[:, s, :], axis=0),
                                            y[:, s, :], None, compute_op=ALU.add).then_inc(g.added, 16)
                pool.wait_ge(g.added, t * (SJ * 16) + SJ * 16)
                pool.sem_inc(g.y_free, 1)

        @block.scalar
        def _(act):
            def piece(c, par):
                act.activation(gw[par][0][:, :, c * GC:(c + 1) * GC], graw[:, :, c * GC:(c + 1) * GC], ACT.Copy)
                act.activation(dw[par][0][:, c, :], draw[:, c, :], ACT.Copy).then_inc(g.w_hi, 1)

            def load(e):
                act.dma_start(graw[:], gu_in[ds(e, 1)].rearrange("o p k f -> p (o k) f")).then_inc(g.w_in, 16)
                act.dma_start(draw[:], dn_in[ds(e, 1)].rearrange("o p k f -> p (o k) f")).then_inc(g.w_in, 16)

            def xT(t):
                act.wait_ge(g.xT_ps, t + 1)
                act.activation(xh[:], bank[0][:], ACT.Copy).then_inc(g.xT_hi, 1)

            def silu(t, f):
                act.wait_ge(g.gu_ps, t * FC + (f + 1))
                act.activation(sg[f % 2][:], bank[2 + f % NB][:, 0:TT], ACT.Silu).then_inc(g.silu, 1)

            def h_hi(t, f):
                act.wait_ge(g.h_f, t * FC + (f + 1 + NB))
                act.activation(hh[:, f, :], hf[f % 4][:], ACT.Copy).then_inc(g.h_hi, 1)

            def tile(t, e, lo, par, more):
                if more:
                    act.wait_ge(g.w_in, e * 32 + 64)
                for f in range(FC):
                    silu(t, f)
                    if f:
                        h_hi(t, f - 1)
                    if more and f % 2:
                        piece(f // 2, 1 - par)
                h_hi(t, FC - 1)
                xT(t + 1)
                if more:
                    for c in range(FC // 2, FC):
                        piece(c, 1 - par)
                    act.wait_ge(g.w_lo, e * FC + 2 * FC)
                    if not isinstance(e, int):
                        load(e + 2)

            act.wait_ge(g.w_in, 32)
            for c in range(FC):
                piece(c, 0)
            act.wait_ge(g.w_lo, FC)
            act.dma_start(graw[:], gu_in[1]).then_inc(g.w_in, 16)
            act.dma_start(draw[:], dn_in[1]).then_inc(g.w_in, 16)
            xT(0)
            experts(act, tile)

        @block.tensor
        def _(pe):
            def tr(t):
                pe.wait_ge(g.x_in, t * 16 + 16)
                for k in range(KD):
                    for s in range(SJ):
                        ins = pe.transpose(bank[0][:, k * TT + s * P:k * TT + (s + 1) * P], xs[:, s, k * P:(k + 1) * P], ident[:])
                ins.then_inc(g.xT_ps, 1)

            def before(e):
                pe.wait_ge(g.w_lo, e * FC + FC)

            def tile(t, e, lo, par, more):
                (gh, gl), (dh, dl) = gw[par], dw[par]
                pe.wait_ge(g.xT_lo, t + 1)
                for f in range(FC):
                    pe.wait_ge(g.h_f, t * FC + (f + 1))
                    for side in range(2):
                        c = slice(side * F + f * P, side * F + (f + 1) * P)
                        o = bank[2 + f % NB][:, side * TT:(side + 1) * TT]
                        for k in range(KD):
                            kx = slice(k * TT, (k + 1) * TT)
                            pe.matmul(o, gh[:, k, c], xh[:, kx], start=k == 0, stop=False)
                            pe.matmul(o, gh[:, k, c], xl[:, kx], start=False, stop=False)
                            ins = pe.matmul(o, gl[:, k, c], xh[:, kx], start=False, stop=k == KD - 1)
                    ins.then_inc(g.gu_ps, 1)
                tr(t + 1)
                pe.wait_ge(g.y_ok, t + 1)
                for s in range(SJ):
                    for f in range(FC):
                        if s == 0:
                            pe.wait_ge(g.h_lo, t * FC + (f + 1))
                        h1, h2 = hh[:, f, s * P:(s + 1) * P], hl[:, f, s * P:(s + 1) * P]
                        o = bank[6][:, s * D:(s + 1) * D]
                        pe.matmul(o, h1, dh[:, f, :], start=f == 0, stop=False)
                        pe.matmul(o, h1, dl[:, f, :], start=False, stop=False)
                        ins = pe.matmul(o, h2, dh[:, f, :], start=False, stop=f == FC - 1)
                ins.then_inc(g.y_ps, 1)

            tr(0)
            experts(pe, tile, before)

        @block.vector
        def _(v):
            v.sem_inc(g.x_read, 1)
            v.sem_inc(g.y_ok, 1)
            v.sem_inc(g.h_f, NB)

            def piece(n, c, par):
                v.wait_ge(g.w_hi, n + (c + 1))
                gc = slice(c * GC, (c + 1) * GC)
                v.tensor_tensor(gw[par][1][:, :, gc], graw[:, :, gc], gw[par][0][:, :, gc].bitcast(f32), ALU.subtract)
                v.tensor_tensor(dw[par][1][:, c, :], draw[:, c, :], dw[par][0][:, c, :].bitcast(f32), ALU.subtract).then_inc(g.w_lo, 1)

            def xT(t):
                v.wait_ge(g.xT_hi, t + 1)
                v.tensor_tensor(xl[:], bank[0][:], xh[:].bitcast(f32), ALU.subtract).then_inc(g.xT_lo, 1)
                v.tensor_copy(meta[0][:], xs[:, :, D:ROW]).then_inc(g.x_read, 1)

            def h_f(t, f):
                v.wait_ge(g.silu, t * FC + (f + 1))
                v.tensor_tensor(hf[f % 4][:], bank[2 + f % NB][:, TT:2 * TT], sg[f % 2][:], ALU.mult).then_inc(g.h_f, 1)

            def h_lo(t, f):
                v.wait_ge(g.h_hi, t * FC + (f + 1))
                v.tensor_tensor(hl[:, f, :], hf[f % 4][:], hh[:, f, :].bitcast(f32), ALU.subtract).then_inc(g.h_lo, 1)

            def tile(t, e, lo, par, more):
                v.wait_ge(g.x_read, t + 2)
                v.tensor_copy(meta[1][:], meta[0][:]).then_inc(g.meta, 1)
                for f in range(FC):
                    h_f(t, f)
                    if f:
                        h_lo(t, f - 1)
                    if more and f % 2:
                        piece(e * FC + FC, f // 2, 1 - par)
                h_lo(t, FC - 1)
                xT(t + 1)
                if more:
                    for c in range(FC // 2, FC):
                        piece(e * FC + FC, c, 1 - par)
                v.wait_ge(g.meta, t + 1)
                v.wait_ge(g.y_free, t + 1)
                v.tensor_copy(tk[:], meta[1][:, :, E:E + 1].bitcast(i32))
                v.tensor_copy(wt[:], meta[1][:, :, ds(e, 1)]).then_inc(g.wt_ok, 1)
                v.wait_ge(g.wt_ok, t + 1)
                v.wait_ge(g.y_ps, t + 1)
                for s in range(SJ):
                    ins = v.tensor_scalar(y[:, s, :], bank[6][:, s * D:(s + 1) * D], wt[:, s, :], None, ALU.mult)
                ins.then_inc(g.y_ok, 1)

            for c in range(FC):
                piece(0, c, 0)
            xT(0)
            experts(v, tile)


def _constants():
    c = np.zeros((P, C_N), np.float32)
    p = np.arange(P)
    c[:, C_ID:C_ID + P] = np.eye(P)
    c[:, C_TRI:C_TRI + P] = p[:, None] < p[None, :]
    for r in range(2 * 32):
        if r % 32 < H:
            n, h = (r % 32) // 2, (r % 32) % 2
            c[r, C_SEL + n * P + h * SK:C_SEL + n * P + (h + 1) * SK] = 1
    c[0, C_MROW:C_MROW + P] = c[32, C_MROW:C_MROW + P] = 1
    c[:, C_BD:C_BD + HH] = (p[:, None] // DH) == np.arange(HH)[None, :]
    e = np.arange(E + 1)
    c[:, C_TRI8:C_TRI8 + (E + 1) * E] = (np.arange(E)[None, :] < e[:, None]).reshape(1, -1)
    c[:, C_BASE:C_BASE + E] = np.arange(E) * CAP
    tok = (np.arange(T // P)[None, :] * P + p[:, None]).astype(np.int32)
    pad = np.zeros((PAD, ROW), np.float32)
    pad[:, ROW - 1] = (T + np.arange(PAD)).astype(np.int32).view(np.float32)
    return c, tok, pad, np.zeros((PAD, D), np.float32)


def kernel(**inputs):
    import concourse.bacc as bacc
    from concourse.bass_utils import run_bass_kernel_spmd

    i = {k: np.asarray(v) for k, v in inputs.items()}

    def rows(w):
        return np.ascontiguousarray(w.reshape(-1, P, w.shape[-1]).transpose(1, 0, 2))

    w = [[rows(i[f"L0_xattn_w{n}"].T) for n in "qkvo"], [rows(i[f"L1_xattn_W{n}"]) for n in "qkvo"]]
    bias = lambda n: np.stack([i[f"L{l}_xattn_b{n}"] for l in range(2)])
    bcol = np.stack([bias("q"), bias("k")], 1).reshape(2, 2, KD, P).transpose(3, 0, 1, 2)
    brow = np.broadcast_to(np.stack([bias("v"), bias("o")], 1)[None], (P, 2, 2, D))
    ctxT = rows(i["ctx_1024"].reshape(B * SK, D).T).reshape(P, KD, B, 1, SK).repeat(2, axis=3)
    mask = i["mask_Bx1x1xS2_ff0"].reshape(B, SK)
    router = np.stack([i["L0_ffn_w_router"], np.zeros(D, np.float32)], 1)
    wb = rows(np.concatenate([i["L0_ffn_w_block"], router], 1))
    gu = i["L1_ffn_gate_up_proj"].transpose(0, 2, 1).reshape(E, KD, P, 2 * F).transpose(0, 2, 1, 3)
    dn = i["L1_ffn_down_proj"].transpose(0, 2, 1).reshape(E, FC, P, D).transpose(0, 2, 1, 3)
    const, tok, pad, zero = _constants()
    arrays = dict(
        x_in=i["x"].reshape(T, D), ctxT_in=ctxT, maskr_in=mask.reshape(1, B * SK), maskc_in=np.concatenate([mask.T, mask.T]),
        w_in=np.stack([np.stack(l, 1) for l in w]), bcol_in=bcol, brow_in=brow, wb_in=wb, gate_in=rows(i["L1_ffn_gate_w"].T),
        gu_in=gu, dn_in=dn, const_in=const, tok_in=tok, pad_in=pad, zero_in=zero)
    arrays = {k: np.ascontiguousarray(v) for k, v in arrays.items()}
    nc = bacc.Bacc("TRN2", target_bir_lowering=False, num_devices=1)
    aps = {k: nc.dram_tensor(k, list(v.shape), mybir.dt.from_np(v.dtype), kind="ExternalInput").ap() for k, v in arrays.items()}
    aps["out"] = nc.dram_tensor("out", [T + PAD, D], mybir.dt.float32, kind="ExternalOutput").ap()
    build(nc, **aps)
    r = run_bass_kernel_spmd(nc, [arrays], core_ids=[0])
    return r.results[0]["out"][:T].reshape(B, S, D)
```

```python
from contextlib import ExitStack

import numpy as np

import concourse.bass as bass
from concourse import mybir

P = 128
B, S, D = 8, 512, 256
SK = 64
H, DH = 16, 16
T = B * S
TJ = S // P
KD = D // P
HH = H // KD
NPAIR = H // 2
PH = NPAIR // 2
KEEP = int(S * 0.75)
E, F = 8, 1024
FC = F // P
TOPK = 2
TT = 256
MINT = 2
PAD = MINT * TT
CAP = T + PAD
NTMAX = T * TOPK // TT + MINT * E
ROW = D + E + 1
NEG = -1.0e9
EPS = 1e-5
SCALE = float(DH) ** -0.5

C_ID = 0
C_TRI = C_ID + P
C_BD = C_TRI + P
C_HALF = C_BD + HH
C_TRI8 = C_HALF + 2
C_BASE = C_TRI8 + (E + 1) * E
C_N = C_BASE + E


def build(nc, x_in, ctxT_in, maskr_in, maskc_in, w_in, bcol_in, bv_in, bo_in, wb_in, wr_in, gate_in, gu_in, dn_in,
          const_in, sel_in, tok_in, pad_in, zero_in, out):
    f32, f32r, bf16, i32 = mybir.dt.float32, mybir.dt.float32r, mybir.dt.bfloat16, mybir.dt.int32
    ALU, ACT, AX = mybir.AluOpType, mybir.ActivationFunctionType, mybir.AxisListType
    slots = nc.dram_tensor("slots", [E * CAP, ROW], f32).ap()
    ctx = ExitStack()
    ds = bass.ds
    NB2 = 2 * B

    def sb(name, shape, dt, c=None):
        return (c or ctx).enter_context(nc.sbuf_tensor(name, shape, dt))

    def sem(name):
        return ctx.enter_context(nc.semaphore(name))

    def asf(ap):
        return ap.bitcast(f32)

    with ctx:
        bank = [ctx.enter_context(nc.psum_tensor(f"bank{i}", [P, 512], f32)) for i in range(8)]
        ident = sb("ident", [P, P], f32)
        bounds = sb("bounds", [1, E + 1 + E], i32)
        w_lay, k_lay = [None, None], [None, None]
        with ExitStack() as early:
            w_lay[0] = [sb(f"w0{p}", [P, 4, KD, D], f32r, early) for p in "hl"]
            k_lay[0] = [sb(f"k0{p}", [P, KD, B * SK], f32r, early) for p in "hl"]
        graw = sb("graw", [P, KD, 2 * F], f32)
        draw = sb("draw", [P, FC, D], f32)

        att = ExitStack()
        with att:
            a = lambda name, shape, dt, c=att: sb(name, shape, dt, c)
            x = a("x", [P, T // P, D], f32)
            const = a("const", [P, C_N], f32)
            tokid = a("tokid", [P, T // P], i32)
            sel = a("sel", [P, (NPAIR + 1) * P], f32r)
            mrow = sel[:, NPAIR * P:]
            trib = a("trib", [P, P], bf16)
            oneb = a("oneb", [P, P], bf16)
            oblk = a("oblk", [P, 2 * DH], f32)
            epst = a("epst", [P, 1], f32)
            w_lay[1] = [a(f"w1{p}", [P, 4, KD, D], f32r) for p in "hl"]
            k_lay[1] = [a(f"k1{p}", [P, KD, B * SK], f32r) for p in "hl"]
            v_lay = [a(f"v{l}", [P, B, NPAIR, DH], f32) for l in range(2)]
            bcol = a("bcol", [P, 2, 2, KD], f32)
            bo = a("bo", [P, 2, D], f32)
            kb = [a(f"kb{p}", [P, 2, KD, HH * SK], f32r) for p in range(2)]
            vb = [a(f"vb{p}", [P, NPAIR, 2 * DH], f32) for p in range(2)]
            mkr = a("mkr", [P, B * SK], f32r)
            mkc = a("mkc", [P, B], f32)
            mkb = [a(f"mkb{p}", [P, 1], f32) for p in range(2)]
            xn = a("xn", [P, TJ, D], f32)
            x2 = [a(f"x2{p}", [P, TJ, ROW], f32) for p in range(2)]
            st = a("st", [P, 2 * TJ, 6], f32)
            mv = a("mv", [P, 2 * TJ, 2], f32)
            rs = a("rs", [P, 5, 2 * TJ], f32)
            mx = a("mx", [P, TJ, P], f32)
            mm = a("mm", [P, S], f32r)
            wbh = a("wbh", [P, KD, D], f32r)
            wbl = a("wbl", [P, KD, D], f32r)
            wrh = a("wrh", [P, KD, P], f32r)
            wrl = a("wrl", [P, KD, P], f32r)
            gt = a("gt", [P, KD, E], f32)
            keep = a("keep", [P, 2, TJ], f32)
            sc = a("sc", [P, TJ, 1], f32)
            lg = a("lg", [P, TJ, E], f32)
            m1 = a("m1", [P, TJ], f32)
            rank = a("rank", [P, TJ, E], f32)
            pick = a("pick", [P, TJ, E], f32)
            pickb = a("pickb", [P, TJ, E], bf16)
            es = a("es", [P, TJ, E], f32)
            ex = a("ex", [P, TJ, E], f32)
            sm = a("sm", [P, 2, TJ], f32)
            run = a("run", [P, E], f32)
            slot = a("slot", [P, TJ, E], f32)
            s2 = a("s2", [P, TOPK, TJ, E], f32)
            sf = a("sf", [P, TOPK, TJ], f32)
            si = [a(f"si{p}", [P, TOPK, TJ], i32) for p in range(2)]
            cn = a("cn", [P, 4, E + 1], f32)
            ci = a("ci", [P, 2, E + 1], i32)
            with ExitStack() as raw:
                craw = a("craw", [P, KD * B * 2 * SK], f32, raw)
                wraw = [a(f"wraw{l}", [P, 4, KD, D], f32, raw) for l in range(2)]
                selraw = a("selraw", [P, (NPAIR + 1) * P], f32, raw)
                mraw = a("mraw", [P, B * SK], f32, raw)
                bv = a("bv", [P, 2, D], f32, raw)
                wbraw = a("wbraw", [P, KD, D], f32, raw)
                wrraw = a("wrraw", [P, KD, P], f32, raw)
            pr = a("pr", [P, NPAIR, S], f32)
            lnd = a("lnd", [P, S], f32)
            rec = a("rec", [P, S], f32)
            cf = a("cf", [P, KD, S], f32)
            ch = a("ch", [P, KD, S], f32r)
            cl = a("cl", [P, KD, S], f32r)
            with ExitStack() as routing:
                x2T = a("x2T", [P, KD, S], f32, routing)
                r1 = a("r1", [P, TJ, E, E], f32, routing)
                r2 = a("r2", [P, TJ, E, E], f32, routing)
            gl = a("gl", [P, TJ, D], f32)
            srow = a("srow", [P, S], f32)
            cmp1 = a("cmp1", [P, TJ, S], bf16)
            cmp2 = a("cmp2", [P, TJ, P], bf16)
            with ExitStack() as cx:
                chi = a("chi", [P, KD * B * 2 * SK], f32r, cx)
                clo = a("clo", [P, KD * B * 2 * SK], f32r, cx)
            xh = a("xh", [P, KD, S], f32r)
            xl = a("xl", [P, KD, S], f32r)
            qh = a("qh", [P, KD, S], f32r)
            ql = a("ql", [P, KD, S], f32r)

            g = type("Sems", (), {k: sem(k) for k in (
                "x0_in x_in const_in w0_in w1_in w2_in pool_ready setup v_ready mask_ready c_hi w_hi "
                "w_lo kv_ps k_hi k_lo v_done bn stats ln_act rstd_act newton rstd xn_ready x2_ready "
                "xT_ps xT_hi xT_lo x2T_ps x2T_hi x2T_lo q_ps q_hi q_lo s_ps max_done max_twice mT_ps m_hi m_lo "
                "st_ps exp_done pv_ps ln_done rec_done ctx_f ctx_hi ctx_lo o_ps x_bo x_new kblk passed_v passed_a "
                "passed_p f_ps gelu srow_ps srow sc_ps score cmp cnt_ps keep_ok x_skip1 x_skip ffn_x lg_ps lg_sb exps "
                "sel_b pos_ps slot_read slot_ok xrow_ok rows_left scattered0 scattered1 x_out pads bounds_ok route counts "
                "graw_in").split()})
            scattered = [g.scattered0, g.scattered1]
            block = att.enter_context(nc.Block())

            def pipeline(eng, step):
                def loop(n0, layer, side, upd):
                    with eng.Fori(0, 2) as i:
                        for par in range(2):
                            step(i * 2 + (n0 + par), par, layer, layer, side, upd)

                step(0, 0, 0, 0, None, False)
                step(1, 1, 0, 0, "ffn", False)
                loop(2, 0, "ffn", True)
                step(6, 0, 0, 0, "ffn", True)
                step(7, 1, 0, 1, "ffn", True)
                step(8, 0, 1, 1, "ffn", True)
                step(9, 1, 1, 1, "moe", True)
                loop(10, 1, "moe", False)
                step(14, 0, 1, 1, "moe", False)
                step(15, 1, 1, None, "moe", False)

            def tiles(n, layer, j=0, w=TJ):
                return ds(n * TJ + (j - layer * B * TJ), w)

            def xt(n, layer, j):
                return x[:, tiles(n, layer, j, 1), :].rearrange("p o d -> p (o d)")

            def layer_of(side):
                return 0 if side == "ffn" else 1

            @block.sync
            def _(sp):
                sp.dma_start(x[:, 0:TJ, :], x_in[0:S, :].rearrange("(t p) d -> p t d", p=P)).then_inc(g.x0_in, 16)
                sp.dma_start(wraw[0][:], w_in[0]).then_inc(g.w0_in, 16)
                sp.dma_start(bcol[:], bcol_in).then_inc(g.w0_in, 16)
                sp.dma_start(wraw[1][:], w_in[1]).then_inc(g.w2_in, 16)
                sp.dma_start(wbraw[:], wb_in).then_inc(g.w1_in, 16)
                sp.dma_start(wrraw[:], wr_in).then_inc(g.w1_in, 16)
                sp.dma_start(bo[:], bo_in).then_inc(g.w1_in, 16)
                sp.dma_start(gt[:], gate_in).then_inc(g.w1_in, 16)
                sp.dma_start(tokid[:], tok_in).then_inc(g.w1_in, 16)
                for b in range(1, B):
                    sp.dma_start(x[:, b * TJ:(b + 1) * TJ, :],
                                 x_in[b * S:(b + 1) * S, :].rearrange("(t p) d -> p t d", p=P)).then_inc(g.x_in, 16)
                sp.dma_start(out[T:T + PAD, :], zero_in).then_inc(g.x_out, 16)
                sp.wait_ge(g.o_ps, 2 * B)
                sp.wait_ge(g.kblk, B)
                sp.dma_start(graw[:], gu_in[0]).then_inc(g.graw_in, 16)
                sp.dma_start(draw[:], dn_in[0]).then_inc(g.graw_in, 16)
                with sp.Fori(0, B) as b:
                    sp.wait_ge(g.x_new, (b + B) * 2 + 3)
                    sp.dma_start(out[ds(b * S, S), :].rearrange("(t p) d -> p t d", p=P),
                                 x[:, ds(b * TJ, TJ), :]).then_inc(g.x_out, 16)
                sp.wait_ge(g.bounds_ok, 1)
                for s in scattered:
                    sp.wait_ge(s, B // 2 * TOPK * TJ * 16)
                with sp.Fori(0, E) as e:
                    r = sp.value_load(bounds[0:1, ds(e + (E + 1), 1)], min_val=0, max_val=E * CAP - PAD)
                    sp.dma_start(slots[ds(r, PAD), :], pad_in).then_inc(g.pads, 16)
                sp.wait_ge(g.pads, E * 16)
                sp.wait_ge(g.x_out, (B + 1) * 16)

            @block.gpsimd
            def _(pool):
                pool.memset(mm[:].bitcast(i32), 0)
                pool.memset(mkr[:].bitcast(i32), 0)
                pool.memset(mx[:], 0.0)
                pool.memset(oneb[:], 1.0)
                pool.memset(epst[:], EPS).then_inc(g.pool_ready, 1)

                def keys(n, par, layer):
                    if isinstance(n, int) and n == 0:
                        pool.wait_ge(g.k_lo, 2 * KD)
                        pool.wait_ge(g.v_done, 2 * B)
                        pool.wait_ge(g.const_in, 96)
                    else:
                        pool.wait_ge(g.mT_ps, n)
                    for part in range(2):
                        for c in range(KD):
                            pool.tensor_tensor(
                                kb[par][:, part, c, :].rearrange("p (h k) -> p h k", h=HH),
                                asf(k_lay[layer][part][:, c, ds(n * SK - layer * B * SK, SK)]).unsqueeze(1).to_broadcast([P, HH, SK]),
                                const[:, C_BD:C_BD + HH].unsqueeze(2).to_broadcast([P, HH, SK]), ALU.mult)
                    if layer:
                        pool.tensor_copy(mkb[par][:], mkc[:, ds(n - B, 1)])
                    pool.tensor_tensor(vb[par][:].rearrange("p a (r d) -> p a r d", r=2),
                                       v_lay[layer][:, ds(n - layer * B, 1), :, :].rearrange("p o a d -> p (o a) d").unsqueeze(2).to_broadcast([P, NPAIR, 2, DH]),
                                       const[:, C_HALF:C_HALF + 2].unsqueeze(1).unsqueeze(3).to_broadcast([P, NPAIR, 2, DH]),
                                       ALU.mult).then_inc(g.kblk, 1)

                def add_bo(n, layer):
                    pool.wait_ge(g.xn_ready, n + 1)
                    xb = x[:, tiles(n, layer), :]
                    pool.tensor_tensor(xb, xb, bo[:, layer, :].unsqueeze(1).to_broadcast([P, TJ, D]), ALU.add).then_inc(g.x_bo, 1)

                def ctx_lo(n, h):
                    pool.wait_ge(g.ctx_hi, n * KD + (h + 1))
                    pool.tensor_tensor(cl[:, h, :], cf[:, h, :], asf(ch[:, h, :]), ALU.subtract).then_inc(g.ctx_lo, 1)

                def skipped(m, par):
                    pool.wait_ge(g.keep_ok, m + 1)
                    o = x2[par][:, :, 0:D]
                    pool.tensor_tensor(o, o, keep[:, 1, :].unsqueeze(2).to_broadcast([P, TJ, D]), ALU.mult).then_inc(g.x_skip1, 1)
                    pool.wait_ge(g.x_skip1, m + 1)
                    xb = x[:, tiles(m, 0), :]
                    pool.tensor_tensor(xb, xb, o, ALU.add).then_inc(g.x_skip, 1)

                def scatter(m, par):
                    pool.wait_ge(g.slot_ok, m - (B - 1))
                    pool.wait_ge(g.xrow_ok, m - (B - 1))
                    if not (isinstance(m, int) and m == B):
                        pool.wait_ge(scattered[1 - par], (m - 1 - (B + 1 - par)) * (TOPK * TJ * 8) + TOPK * TJ * 16)
                        pool.sem_inc(g.rows_left, 1)
                    pool.sem_inc(g.passed_p, 1)
                    for kk in range(TOPK):
                        for j in range(TJ):
                            pool.indirect_dma_start(slots, bass.IndirectOffsetOnAxis(ap=si[par][:, kk, j:j + 1], axis=0),
                                                    x2[par][:, j, :], None).then_inc(scattered[par], 16)

                pool.wait_ge(g.w1_in, 5 * 16)
                add_bo(0, 0)
                keys(0, 0, 0)

                def step(n, par, cur, nxt, side, upd):
                    if upd:
                        skipped(n - 2, par)
                    if nxt is not None:
                        keys(n + 1, 1 - par, nxt)
                        add_bo(n + 1, nxt)
                    ctx_lo(n, 0)
                    ctx_lo(n, 1)
                    if side == "moe":
                        scatter(n - 1, 1 - par)

                pipeline(pool, step)
                scatter(NB2 - 1, 1)
                for s in scattered:
                    pool.wait_ge(s, B // 2 * TOPK * TJ * 16)

            @block.scalar
            def _(act):
                act.preload_act_table_set("natural_log_exp_and_others")
                act.dma_start(craw[:], ctxT_in).then_inc(g.w0_in, 16)
                act.dma_start(const[:], const_in).then_inc(g.const_in, 16)
                act.dma_start(selraw[:], sel_in).then_inc(g.const_in, 16)
                act.dma_start(bv[:], bv_in).then_inc(g.const_in, 16)
                for r in (0, 32):
                    act.dma_start(mraw[r:r + 1, :], maskr_in).then_inc(g.const_in, 16)
                act.dma_start(mkc[:], maskc_in).then_inc(g.const_in, 16)

                def rstd(c, t):
                    act.wait_ge(g.stats, c + 1)
                    act.activation(rs[:, 0, t], mv[:, t, 1], ACT.Ln, bias=epst[:, 0:1]).then_inc(g.ln_act, 1)
                    act.wait_ge(g.ln_act, c + 1)
                    act.activation(rs[:, 1, t], rs[:, 0, t], ACT.Exp, scale=-0.5).then_inc(g.rstd_act, 1)

                def normed(n, c, layer):
                    act.wait_ge(g.rstd, c + 1)
                    act.sem_inc(g.passed_a, 1)
                    for j in range(TJ):
                        ins = act.activation(xn[:, j, :], xt(n, layer, j), ACT.Identity, bias=rs[:, 4, j:j + 1], scale=rs[:, 3, j:j + 1])
                    ins.then_inc(g.xn_ready, 1)

                def xT(n):
                    for c in range(KD):
                        act.wait_ge(g.xT_ps, n * KD + (c + 1))
                        act.activation(xh[:, c, :], bank[c][:], ACT.Copy).then_inc(g.xT_hi, 1)

                def x2T_hi(m, side):
                    if side == "moe":
                        act.wait_ge(g.ffn_x, B)
                    for c in range(KD):
                        act.wait_ge(g.x2T_ps, m * KD + (c + 1))
                        act.activation(xh[:, c, :] if side == "ffn" else x2T[:, c, :], bank[2 + c][:], ACT.Copy).then_inc(g.x2T_hi, 1)

                def q_hi(n, layer):
                    for c in range(KD):
                        act.wait_ge(g.q_ps, n * KD + (c + 1))
                        act.activation(qh[:, c, :], bank[c][:], ACT.Identity, bias=bcol[:, layer, 0, c:c + 1]).then_inc(g.q_hi, 1)

                def m_hi(n):
                    act.wait_ge(g.mT_ps, n + 1)
                    act.activation(mm[0:64, :], bank[2][0:64, :], ACT.Copy, scale=-1.0).then_inc(g.m_hi, 1)

                def exps(n, par, layer, pairs):
                    for p in pairs:
                        act.wait_ge(g.st_ps, n * NPAIR + (p + 1))
                        act.activation(pr[:, p, :], bank[4 + p % 2][:], ACT.Exp, scale=SCALE,
                                       bias=mkb[par][:, 0:1] if layer else 0.0).then_inc(g.exp_done, 1)

                def recip(n, h):
                    act.wait_ge(g.pv_ps, n * KD + (h + 1))
                    act.activation(lnd[:], bank[7][:], ACT.Ln).then_inc(g.ln_done, 1)
                    act.wait_ge(g.ln_done, n * KD + (h + 1))
                    act.activation(rec[:], lnd[:], ACT.Exp, scale=-1.0).then_inc(g.rec_done, 1)

                def ctx_hi(n, h):
                    act.wait_ge(g.ctx_f, n * KD + (h + 2))
                    act.activation(ch[:, h, :], cf[:, h, :], ACT.Copy).then_inc(g.ctx_hi, 1)

                def gelu(m):
                    for u in range(2):
                        act.wait_ge(g.f_ps, m * 2 + (u + 1))
                        act.activation(gl[:, 2 * u:2 * u + 2, :].rearrange("p t d -> p (t d)"), bank[2 + u][:],
                                       ACT.Gelu_apprx_tanh).then_inc(g.gelu, 1)
                    act.preload_act_table_set("natural_log_exp_and_others")

                def srow_copy(m):
                    act.wait_ge(g.srow_ps, m + 1)
                    act.activation(srow[:], bank[2][:], ACT.Copy).then_inc(g.srow, 1)

                def ex_(m):
                    act.wait_ge(g.lg_sb, m - (B - 1))
                    act.activation(ex[:], es[:], ACT.Exp).then_inc(g.exps, 1)

                act.wait_ge(g.w0_in, 48)
                act.activation(chi[:], craw[:], ACT.Copy).then_inc(g.c_hi, 1)
                act.activation(w_lay[0][0][:], wraw[0][:], ACT.Copy).then_inc(g.w_hi, 1)
                act.wait_ge(g.pool_ready, 1)
                rstd(0, slice(0, TJ))
                act.wait_ge(g.w2_in, 16)
                act.activation(w_lay[1][0][:], wraw[1][:], ACT.Copy).then_inc(g.w_hi, 1)
                normed(0, 0, 0)
                for layer in range(2):
                    for c in range(KD):
                        act.wait_ge(g.kv_ps, layer * (KD + B) + c + 1)
                        act.activation(k_lay[layer][0][:, c, :], bank[c][:], ACT.Identity,
                                       bias=bcol[:, layer, 1, c:c + 1]).then_inc(g.k_hi, 1)
                xT(0)
                q_hi(0, 0)
                m_hi(0)
                act.sem_inc(g.exp_done, 2)
                act.wait_ge(g.mask_ready, 1)

                def step(n, par, cur, nxt, side, upd):
                    exps(n, par, cur, (0, 1))
                    if side and nxt is not None:
                        rstd(n + 1, slice(0, 2 * TJ))
                    elif nxt is not None:
                        rstd(n + 1, slice(0, TJ))
                    else:
                        rstd(n + 1, slice(TJ, 2 * TJ))
                    if nxt is not None:
                        normed(n + 1, n + 1, nxt)
                    exps(n, par, cur, (2, 3))
                    if side:
                        x2T_hi(n - 1, side)
                    exps(n, par, cur, (4, 5))
                    recip(n, 0)
                    if side == "ffn":
                        gelu(n - 1)
                    exps(n, par, cur, (6, 7))
                    if nxt is not None:
                        xT(n + 1)
                    ctx_hi(n, 0)
                    recip(n, 1)
                    if side == "ffn":
                        srow_copy(n - 1)
                    if nxt is not None:
                        q_hi(n + 1, nxt)
                    if side == "moe":
                        ex_(n - 1)
                    ctx_hi(n, 1)
                    if nxt is not None:
                        m_hi(n + 1)

                pipeline(act, step)
                rstd(NB2 + 1, slice(TJ, 2 * TJ))
                x2T_hi(NB2 - 1, "moe")
                ex_(NB2 - 1)

            @block.tensor
            def _(pe):
                def three(o, ahi, alo, bhi, blo, last=True):
                    n = len(ahi)
                    for c in range(n):
                        pe.matmul(o, ahi[c], bhi[c], start=c == 0, stop=False)
                        pe.matmul(o, ahi[c], blo[c], start=False, stop=False)
                        ins = pe.matmul(o, alo[c], bhi[c], start=False, stop=last and c == n - 1)
                    return ins

                def chunks(t, *rest):
                    return [t[(slice(None), k) + rest] for k in range(KD)]

                def wts(layer, i, cols=slice(None)):
                    return [[w_lay[layer][p][:, i, k, cols] for k in range(KD)] for p in range(2)]

                def transposes(src, b0, done):
                    for c in range(KD):
                        for j in range(TJ):
                            ins = pe.transpose(bank[b0 + c][:, j * P:(j + 1) * P], src[:, j, c * P:(c + 1) * P], ident[:])
                        ins.then_inc(done, 1)

                def tr(n):
                    pe.wait_ge(g.xn_ready, n + 1)
                    transposes(xn, 0, g.xT_ps)

                def tr2(m, par):
                    pe.wait_ge(g.x2_ready, m + 1)
                    transposes(x2[par], 2, g.x2T_ps)

                def q_proj(n, layer):
                    pe.wait_ge(g.xT_lo, n * KD + KD)
                    for c in range(KD):
                        wh, wl = wts(layer, 0, slice(c * P, (c + 1) * P))
                        three(bank[c][:], wh, wl, chunks(xh), chunks(xl)).then_inc(g.q_ps, 1)

                def maxima(n, par, layer):
                    pe.wait_ge(g.q_hi, n * KD + KD)
                    pe.wait_ge(g.kblk, n + 1)
                    for u in range(TJ * KD):
                        j, c = u // KD, u % KD
                        pe.wait_ge(g.max_done, n * TJ * KD + (u + 1))
                        ins = pe.matmul(bank[2 + c][:], qh[:, c, j * P:(j + 1) * P], kb[par][:, 0, c, :],
                                        start=True, stop=not layer)
                        if layer:
                            ins = pe.matmul(bank[2 + c][:], mrow, mkr[:, ds(n * SK - B * SK, SK)].unsqueeze(1).to_broadcast([P, HH, SK]),
                                            start=False, stop=True)
                        ins.then_inc(g.s_ps, 1)

                def maxima_T(n):
                    pe.wait_ge(g.max_twice, n + 1)
                    for j in range(TJ):
                        ins = pe.transpose(bank[2][:, j * P:(j + 1) * P], mx[:, j, :], ident[:])
                    ins.then_inc(g.mT_ps, 1)

                def scores(n, par, pairs):
                    for p in pairs:
                        c, o = p // PH, (p % PH) * P
                        pe.wait_ge(g.exp_done, n * NPAIR + (p + 1))
                        k_ = kb[par]
                        three(bank[4 + p % 2][:], [k_[:, 0, c, o:o + P]], [k_[:, 1, c, o:o + P]],
                              [qh[:, c, :]], [ql[:, c, :]], last=False)
                    if pairs[0] == 0:
                        pe.wait_ge(g.m_lo, n + 1)
                    for p in pairs:
                        pe.matmul(bank[4 + p % 2][:], sel[:, p * P:(p + 1) * P], mm[:], start=False, stop=True).then_inc(g.st_ps, 1)

                def values(n, par, h):
                    pe.wait_ge(g.exp_done, n * NPAIR + (PH * (h + 1) + 2))
                    pe.wait_ge(g.ctx_f, n * KD + (h + 1))
                    for dst in (6, 7):
                        for j in range(PH):
                            p = h * PH + j
                            ins = pe.matmul(bank[dst][32 * j:32 * j + 32, :], vb[par][:, p, :] if dst == 6 else oblk[:],
                                            pr[:, p, :], start=True, stop=True)
                    ins.then_inc(g.pv_ps, 1)

                def out_proj(n, layer):
                    pe.wait_ge(g.ctx_lo, n * KD + KD)
                    wh, wl = wts(layer, 3)
                    for u in range(2):
                        for t in range(2):
                            j = slice((2 * u + t) * P, (2 * u + t + 1) * P)
                            ins = three(bank[u][:, t * D:(t + 1) * D], chunks(ch, j), chunks(cl, j), wh, wl)
                        ins.then_inc(g.o_ps, 1)

                def ffn_mm(m):
                    pe.wait_ge(g.x2T_lo, m * KD + KD)
                    for u in range(2):
                        for t in range(2):
                            j = slice((2 * u + t) * P, (2 * u + t + 1) * P)
                            ins = three(bank[2 + u][:, t * D:(t + 1) * D], chunks(xh, j), chunks(xl, j), chunks(wbh), chunks(wbl))
                        ins.then_inc(g.f_ps, 1)

                def router(m):
                    pe.wait_ge(g.gelu, m * 2 + 2)
                    three(bank[2][:], chunks(wrh), chunks(wrl), chunks(xh), chunks(xl)).then_inc(g.srow_ps, 1)

                def router_T(m):
                    pe.wait_ge(g.srow, m + 1)
                    for j in range(TJ):
                        ins = pe.transpose(bank[3][:, j * P:(j + 1) * P], srow[:, j * P:(j + 1) * P], ident[:])
                    ins.then_inc(g.sc_ps, 1)

                def count(m):
                    pe.wait_ge(g.cmp, m + 1)
                    for i in range(TJ):
                        for j in range(TJ):
                            pe.matmul(bank[3][:, i:i + 1], cmp1[:, j, i * P:(i + 1) * P], oneb[:, 0:1], start=j == 0, stop=False)
                        ins = pe.matmul(bank[3][:, i:i + 1], cmp2[:, i, :], oneb[:, 0:1], start=False, stop=True)
                    ins.then_inc(g.cnt_ps, 1)

                def gates(m):
                    pe.wait_ge(g.x2T_hi, m * KD + KD)
                    for j in range(TJ):
                        for k in range(KD):
                            ins = pe.matmul(bank[2][:, j * E:(j + 1) * E], x2T[:, k, j * P:(j + 1) * P], gt[:, k, :],
                                            start=k == 0, stop=k == KD - 1)
                    ins.then_inc(g.lg_ps, 1)

                def positions(m):
                    pe.wait_ge(g.sel_b, m - (B - 1))
                    for j in range(TJ):
                        for i in range(j):
                            pe.matmul(bank[3][:, j * E:(j + 1) * E], oneb[:], pickb[:, i, :], start=i == 0, stop=False)
                        pe.matmul(bank[3][:, j * E:(j + 1) * E], trib[:], pickb[:, j, :], start=j == 0, stop=True)
                    for i in range(TJ):
                        ins = pe.matmul(bank[3][:, TJ * E:(TJ + 1) * E], oneb[:], pickb[:, i, :], start=i == 0, stop=i == TJ - 1)
                    ins.then_inc(g.pos_ps, 1)

                for layer in range(2):
                    pe.wait_ge(g.w_lo, layer + 1)
                    if layer:
                        pe.wait_ge(g.k_lo, KD)
                    cview = lambda t: [t[:, k * B * 2 * SK:(k + 1) * B * 2 * SK].rearrange("p (b r s) -> p b r s", r=2, s=SK)[:, :, 0, :] for k in range(KD)]
                    for c in range(KD):
                        wh, wl = wts(layer, 1, slice(c * P, (c + 1) * P))
                        three(bank[c][:], wh, wl, cview(chi), cview(clo)).then_inc(g.kv_ps, 1)
                    wh, wl = wts(layer, 2)
                    for b in range(B):
                        if layer or b >= 4:
                            pe.wait_ge(g.v_done, layer * B + b - 3)
                        dup = lambda t: [t[:, (k * B + b) * 2 * SK:(k * B + b + 1) * 2 * SK] for k in range(KD)]
                        three(bank[4 + b % 4][:, 0:D], dup(chi), dup(clo), wh, wl).then_inc(g.kv_ps, 1)
                pe.wait_ge(g.k_lo, 2 * KD)
                tr(0)
                q_proj(0, 0)
                maxima(0, 0, 0)
                maxima_T(0)
                pe.wait_ge(g.v_done, 2 * B)

                def step(n, par, cur, nxt, side, upd):
                    pe.wait_ge(g.q_lo, n * KD + KD)
                    scores(n, par, (0, 1))
                    scores(n, par, (2, 3))
                    if side:
                        if upd:
                            pe.wait_ge(g.keep_ok, n - 1)
                        tr2(n - 1, 1 - par)
                    scores(n, par, (4, 5))
                    values(n, par, 0)
                    if side == "ffn":
                        ffn_mm(n - 1)
                    if side == "moe":
                        gates(n - 1)
                    scores(n, par, (6, 7))
                    if nxt is not None:
                        pe.wait_ge(g.x_new, n * 2 + 1)
                        if side == "ffn":
                            router(n - 1)
                        tr(n + 1)
                    elif side == "ffn":
                        router(n - 1)
                    values(n, par, 1)
                    if nxt is not None:
                        q_proj(n + 1, nxt)
                    if side == "ffn":
                        router_T(n - 1)
                    if side == "moe":
                        positions(n - 1)
                    pe.wait_ge(g.q_lo, (n + 1) * KD + KD if nxt is not None else n * KD + KD)
                    out_proj(n, cur)
                    if nxt is not None:
                        if side == "ffn":
                            pe.wait_ge(g.score, n)
                        if side == "moe":
                            pe.wait_ge(g.slot_read, n - B)
                        maxima(n + 1, 1 - par, nxt)
                        maxima_T(n + 1)
                    if side == "ffn":
                        count(n - 1)

                pipeline(pe, step)
                pe.wait_ge(g.slot_read, B - 1)
                tr2(NB2 - 1, 1)
                gates(NB2 - 1)
                positions(NB2 - 1)

            @block.vector
            def _(v):
                tri8 = const[:, C_TRI8:C_TRI8 + E * E].rearrange("p (e f) -> p e f", f=E)
                NROUTE = 13

                def stats(c, groups):
                    for n, layer, t0 in groups:
                        for j in range(TJ):
                            ins = v.bn_stats(st[:, t0 + j, :], xt(n, layer, j))
                    ins.then_inc(g.bn, 1)
                    v.wait_ge(g.bn, c + 1)
                    v.sem_inc(g.passed_v, 1)
                    for _, _, t0 in groups:
                        for j in range(TJ):
                            ins = v.bn_aggr(mv[:, t0 + j, :], st[:, t0 + j, :])
                    ins.then_inc(g.stats, 1)

                def newton(c, t):
                    v.wait_ge(g.rstd_act, c + 1)
                    v.tensor_tensor(rs[:, 2, t], rs[:, 1, t], rs[:, 1, t], ALU.mult).then_inc(g.newton, 1)
                    v.wait_ge(g.newton, c * 4 + 1)
                    v.scalar_tensor_tensor(rs[:, 2, t], mv[:, t, 1], EPS, rs[:, 2, t], ALU.add, ALU.mult).then_inc(g.newton, 1)
                    v.wait_ge(g.newton, c * 4 + 2)
                    v.tensor_scalar(rs[:, 2, t], rs[:, 2, t], -0.5, 1.5, ALU.mult, ALU.add).then_inc(g.newton, 1)
                    v.wait_ge(g.newton, c * 4 + 3)
                    v.tensor_tensor(rs[:, 3, t], rs[:, 1, t], rs[:, 2, t], ALU.mult).then_inc(g.newton, 1)
                    v.wait_ge(g.newton, c * 4 + 4)
                    v.scalar_tensor_tensor(rs[:, 4, t], mv[:, t, 0], -1.0, rs[:, 3, t], ALU.mult, ALU.mult).then_inc(g.rstd, 1)

                def normed2(m, par, layer):
                    for j in range(TJ):
                        ins = v.tensor_scalar(x2[par][:, j, 0:D], xt(m, layer, j), mv[:, TJ + j, 0:1], rs[:, 3, TJ + j:TJ + j + 1],
                                              ALU.subtract, ALU.mult)
                    ins.then_inc(g.x2_ready, 1)

                def free_rows(m):
                    v.wait_ge(g.rows_left, m - (B - 1))

                def lo(b0, hi, low, src, i, done):
                    for c in range(KD):
                        v.wait_ge(src, i * KD + (c + 1))
                        v.tensor_tensor(low[:, c, :], bank[b0 + c][:], asf(hi[:, c, :]), ALU.subtract).then_inc(done, 1)

                def q_lo(n, layer):
                    for c in range(KD):
                        v.wait_ge(g.q_hi, n * KD + (c + 1))
                        v.scalar_tensor_tensor(ql[:, c, :], bank[c][:], bcol[:, layer, 0, c:c + 1], asf(qh[:, c, :]),
                                               ALU.add, ALU.subtract).then_inc(g.q_lo, 1)

                def maxes(n):
                    for u in range(TJ * KD):
                        j, c = u // KD, u % KD
                        v.wait_ge(g.s_ps, n * TJ * KD + (u + 1))
                        v.tensor_reduce(mx[:, j, c * HH:(c + 1) * HH], bank[2 + c][:].rearrange("p (h k) -> p h k", k=SK),
                                        AX.X, ALU.max).then_inc(g.max_done, 1)
                    v.wait_ge(g.max_done, n * TJ * KD + (TJ * KD + 2))
                    v.tensor_copy(mx[:, :, 32:32 + H], mx[:, :, 0:H]).then_inc(g.max_twice, 1)

                def m_lo(n):
                    v.wait_ge(g.m_hi, n + 1)
                    v.scalar_tensor_tensor(mm[32:64, :], bank[2][32:64, :], -1.0, asf(mm[32:64, :]),
                                           ALU.mult, ALU.subtract).then_inc(g.m_lo, 1)

                def ctx_f(n, h):
                    v.wait_ge(g.rec_done, n * KD + (h + 1))
                    v.tensor_tensor(cf[:, h, :], bank[6][:], rec[:], ALU.mult).then_inc(g.ctx_f, 1)

                def x_up(n, layer):
                    v.wait_ge(g.x_bo, n + 1)
                    for u in range(2):
                        v.wait_ge(g.o_ps, n * 2 + (u + 1))
                        xb = x[:, tiles(n, layer, 2 * u, 2), :]
                        v.tensor_tensor(xb, bank[u][:].rearrange("p (t d) -> p t d", t=2), xb, ALU.add).then_inc(g.x_new, 1)

                def compare(m):
                    v.wait_ge(g.sc_ps, m + 1)
                    v.tensor_copy(sc[:], bank[3][:].rearrange("p (t c) -> p t c", c=P)[:, :, 0:1]).then_inc(g.score, 1)
                    v.wait_ge(g.score, m + 1)
                    for j in range(TJ):
                        w = (j + 1) * P
                        v.tensor_scalar(cmp1[:, j, 0:w], srow[:, 0:w], sc[:, j, :], None, ALU.is_lt)
                        if j < TJ - 1:
                            v.tensor_scalar(cmp1[:, j, w:S], srow[:, w:S], sc[:, j, :], None, ALU.is_le)
                        ins = v.scalar_tensor_tensor(cmp2[:, j, :], srow[:, w - P:w], sc[:, j, :],
                                                     const[:, C_TRI:C_TRI + P], ALU.is_equal, ALU.mult)
                    ins.then_inc(g.cmp, 1)

                def keeps(m):
                    v.wait_ge(g.cnt_ps, m + 1)
                    v.tensor_scalar(keep[:, 0, :], bank[3][:, 0:TJ], float(KEEP), None, ALU.is_lt)
                    v.tensor_scalar(keep[:, 1, :], bank[3][:, 0:TJ], float(KEEP), None, ALU.is_ge).then_inc(g.keep_ok, 1)

                def kept(m):
                    v.wait_ge(g.x_skip, m + 1)
                    for j in range(TJ):
                        ins = v.scalar_tensor_tensor(xt(m, 0, j), gl[:, j, :], keep[:, 0, j:j + 1], xt(m, 0, j), ALU.mult, ALU.add)
                    ins.then_inc(g.ffn_x, 1)

                def dep(ins, m, i):
                    ins.then_inc(g.route, 1)
                    v.wait_ge(g.route, m * NROUTE + (i - B * NROUTE))

                def gating(m, par):
                    v.wait_ge(g.lg_ps, m - (B - 1))
                    dep(v.tensor_copy(lg[:].rearrange("p t e -> p (t e)"), bank[2][:, 0:TJ * E]), m, 1)
                    dep(v.tensor_reduce(m1[:], lg[:], AX.X, ALU.max), m, 2)
                    v.tensor_tensor(es[:], lg[:], m1[:].unsqueeze(2).to_broadcast([P, TJ, E]), ALU.subtract).then_inc(g.lg_sb, 1)
                    lf = lg[:].unsqueeze(2).to_broadcast([P, TJ, E, E])
                    le = lg[:].unsqueeze(3).to_broadcast([P, TJ, E, E])
                    v.tensor_tensor(r1[:], lf, le, ALU.is_gt)
                    dep(v.tensor_tensor(r2[:], lf, le, ALU.is_equal), m, 3)
                    dep(v.tensor_tensor(r2[:], r2[:], tri8.unsqueeze(1).to_broadcast([P, TJ, E, E]), ALU.mult), m, 4)
                    dep(v.tensor_tensor(r1[:], r1[:], r2[:], ALU.add), m, 5)
                    dep(v.tensor_reduce(rank[:], r1[:], AX.X, ALU.add), m, 6)
                    v.tensor_scalar(pickb[:], rank[:], float(TOPK), None, ALU.is_lt).then_inc(g.sel_b, 1)
                    dep(v.tensor_scalar(pick[:], rank[:], float(TOPK), None, ALU.is_lt), m, 7)

                def weights(m, par):
                    v.wait_ge(g.exps, m - (B - 1))
                    dep(v.tensor_tensor(es[:], ex[:], pick[:], ALU.mult), m, 11)
                    dep(v.tensor_reduce(sm[:, 0, :], es[:], AX.X, ALU.add), m, 12)
                    dep(v.reciprocal(sm[:, 1, :], sm[:, 0, :]), m, 13)
                    v.tensor_tensor(x2[par][:, :, D:D + E], es[:], sm[:, 1, :].unsqueeze(2).to_broadcast([P, TJ, E]), ALU.mult)
                    v.tensor_copy(x2[par][:, :, D + E].bitcast(i32), tokid[:, tiles(m, 1)]).then_inc(g.xrow_ok, 1)

                def slots_of(m, par):
                    v.wait_ge(g.pos_ps, m - (B - 1))
                    dep(v.tensor_tensor(slot[:], bank[3][:, 0:TJ * E].rearrange("p (t e) -> p t e", e=E),
                                        run[:].unsqueeze(1).to_broadcast([P, TJ, E]), ALU.add), m, 8)
                    v.tensor_tensor(run[:], run[:], bank[3][:, TJ * E:(TJ + 1) * E], ALU.add).then_inc(g.slot_read, 1)
                    for kk in range(TOPK):
                        ins = v.scalar_tensor_tensor(s2[:, kk, :, :], rank[:], float(kk), slot[:], ALU.is_equal, ALU.mult)
                    dep(ins, m, 9)
                    dep(v.tensor_reduce(sf[:], s2[:], AX.X, ALU.add), m, 10)
                    v.tensor_copy(si[par][:], sf[:]).then_inc(g.slot_ok, 1)

                v.sem_inc(g.ctx_f, 1)
                v.sem_inc(g.x_new, 1)
                v.sem_inc(g.max_done, 2)
                v.sem_inc(g.rows_left, 2)
                v.wait_ge(g.x0_in, 16)
                stats(0, [(0, 0, 0)])
                v.wait_ge(g.c_hi, 1)
                v.tensor_tensor(clo[:], craw[:], asf(chi[:]), ALU.subtract)
                v.wait_ge(g.w_hi, 1)
                v.tensor_tensor(w_lay[0][1][:], wraw[0][:], asf(w_lay[0][0][:]), ALU.subtract).then_inc(g.w_lo, 1)
                v.wait_ge(g.pool_ready, 1)
                newton(0, slice(0, TJ))
                v.wait_ge(g.const_in, 96)
                v.tensor_copy(ident[:], const[:, C_ID:C_ID + P])
                v.tensor_copy(trib[:], const[:, C_TRI:C_TRI + P])
                v.tensor_copy(oblk[:].rearrange("p (r d) -> p r d", r=2), const[:, C_HALF:C_HALF + 2].unsqueeze(2).to_broadcast([P, 2, DH]))
                v.tensor_copy(run[:], const[:, C_BASE:C_BASE + E]).then_inc(g.v_ready, 1)
                v.wait_ge(g.w_hi, 2)
                v.tensor_tensor(w_lay[1][1][:], wraw[1][:], asf(w_lay[1][0][:]), ALU.subtract).then_inc(g.w_lo, 1)
                for layer in range(2):
                    for c in range(KD):
                        v.wait_ge(g.k_hi, layer * KD + c + 1)
                        v.scalar_tensor_tensor(k_lay[layer][1][:, c, :], bank[c][:], bcol[:, layer, 1, c:c + 1],
                                               asf(k_lay[layer][0][:, c, :]), ALU.add, ALU.subtract).then_inc(g.k_lo, 1)
                    for b in range(B):
                        v.wait_ge(g.kv_ps, layer * (KD + B) + KD + b + 1)
                        for r in range(2):
                            q, hd = slice(r * SK, (r + 1) * SK), slice(r * DH, (r + 1) * DH)
                            ins = v.tensor_tensor(v_lay[layer][q, b, :, :],
                                                  bank[4 + b % 4][q, 0:D].rearrange("p (n c) -> p n c", c=2 * DH)[:, :, hd],
                                                  bv[q, layer, :].rearrange("p (n c) -> p n c", c=2 * DH)[:, :, hd], ALU.add)
                        ins.then_inc(g.v_done, 1)
                lo(0, xh, xl, g.xT_hi, 0, g.xT_lo)
                q_lo(0, 0)
                v.wait_ge(g.w1_in, 80)
                v.tensor_copy(sel[:], selraw[:])
                v.tensor_copy(wbh[:], wbraw[:])
                v.tensor_copy(wrh[:], wrraw[:])
                for r in (0, 32):
                    v.tensor_scalar(mraw[r:r + 1, :], mraw[r:r + 1, :], NEG, 1.0 / SCALE, ALU.mult, ALU.mult)
                v.tensor_scalar(mkc[:], mkc[:], NEG, None, ALU.mult).then_inc(g.setup, 1)
                v.wait_ge(g.setup, 1)
                v.tensor_tensor(wbl[:], wbraw[:], asf(wbh[:]), ALU.subtract)
                v.tensor_tensor(wrl[:], wrraw[:], asf(wrh[:]), ALU.subtract)
                for r in (0, 32):
                    last = v.tensor_copy(mkr[r:r + 1, :], mraw[r:r + 1, :])
                last.then_inc(g.setup, 1)
                v.wait_ge(g.setup, 2)
                v.tensor_tensor(mkr[32:33, :], mraw[32:33, :], asf(mkr[32:33, :]), ALU.subtract).then_inc(g.mask_ready, 1)
                maxes(0)
                m_lo(0)
                v.wait_ge(g.x_in, (B - 1) * 16)

                def step(n, par, cur, nxt, side, upd):
                    other = layer_of(side)
                    groups = ([(n + 1, nxt, 0)] if nxt is not None else []) + ([(n - 1, other, TJ)] if side else [])
                    if upd:
                        keeps(n - 2)
                    if side:
                        v.wait_ge(g.x_new, n * 2 + 1)
                    stats(n + 1, groups)
                    newton(n + 1, slice(0 if nxt is not None else TJ, 2 * TJ if side else TJ))
                    if side:
                        if side == "moe":
                            free_rows(n - 1)
                        normed2(n - 1, 1 - par, other)
                    if upd:
                        kept(n - 2)
                    if side == "ffn":
                        lo(2, xh, xl, g.x2T_hi, n - 1, g.x2T_lo)
                    ctx_f(n, 0)
                    if side == "moe":
                        gating(n - 1, 1 - par)
                    if nxt is not None:
                        lo(0, xh, xl, g.xT_hi, n + 1, g.xT_lo)
                    ctx_f(n, 1)
                    if nxt is not None:
                        q_lo(n + 1, nxt)
                    if side == "ffn":
                        compare(n - 1)
                    if side == "moe":
                        slots_of(n - 1, 1 - par)
                        weights(n - 1, 1 - par)
                    if nxt is not None:
                        maxes(n + 1)
                    x_up(n, cur)
                    if nxt is not None:
                        m_lo(n + 1)

                pipeline(v, step)
                v.wait_ge(g.x_new, NB2 * 2 + 1)
                stats(NB2 + 1, [(NB2 - 1, 1, TJ)])
                newton(NB2 + 1, slice(TJ, 2 * TJ))
                free_rows(NB2 - 1)
                normed2(NB2 - 1, 1, 1)
                gating(NB2 - 1, 1)
                slots_of(NB2 - 1, 1)
                weights(NB2 - 1, 1)

                t = [0]

                def dep1(ins):
                    t[0] += 1
                    ins.then_inc(g.counts, 1)
                    v.wait_ge(g.counts, t[0])

                r1f = r1[:].rearrange("p a b c -> p (a b c)")[:, 0:(E + 1) * E].rearrange("p (e f) -> p e f", f=E)
                v.wait_ge(g.slot_read, B)
                v.tensor_copy(ci[:, 1, 0:E], run[:])
                dep1(v.tensor_tensor(cn[:, 0, 0:E], run[:], const[:, C_BASE:C_BASE + E], ALU.subtract))
                dep1(v.tensor_scalar(cn[:, 1, 0:E], cn[:, 0, 0:E], float(TT - 1), None, ALU.add))
                dep1(v.tensor_copy(ci[:, 0, 0:E], cn[:, 1, 0:E]))
                dep1(v.tensor_scalar(ci[:, 0, 0:E], ci[:, 0, 0:E], TT.bit_length() - 1, None, ALU.logical_shift_right))
                dep1(v.tensor_copy(cn[:, 2, 0:E], ci[:, 0, 0:E]))
                dep1(v.tensor_scalar(cn[:, 2, 0:E], cn[:, 2, 0:E], float(MINT), None, ALU.max))
                dep1(v.tensor_tensor(r1f, cn[:, 2, 0:E].unsqueeze(1).to_broadcast([P, E + 1, E]),
                                     const[:, C_TRI8:C_TRI8 + (E + 1) * E].rearrange("p (e f) -> p e f", f=E), ALU.mult))
                dep1(v.tensor_reduce(cn[:, 3, :], r1f, AX.X, ALU.add))
                v.tensor_copy(bounds[0:1, 0:E + 1], cn[0:1, 3, :])
                v.tensor_copy(bounds[0:1, E + 1:2 * E + 1], ci[0:1, 1, 0:E]).then_inc(g.bounds_ok, 1)
        moe(nc, sb, sem, bank, ident, bounds, graw, draw, g.graw_in, slots, gu_in, dn_in, out)


def moe(nc, sb, sem, bank, ident, bounds, graw, draw, graw_in, slots, gu_in, dn_in, out):
    f32, f32r, i32 = mybir.dt.float32, mybir.dt.float32r, mybir.dt.int32
    ALU, ACT = mybir.AluOpType, mybir.ActivationFunctionType
    ds = bass.ds
    SJ = TT // P
    NB = 4
    with ExitStack() as m:
        a = lambda name, shape, dt: sb(name, shape, dt, m)
        gw = [[a(f"gw{p}{h}", [P, KD, 2 * F], f32r) for h in "hl"] for p in range(2)]
        dw = [[a(f"dw{p}{h}", [P, FC, D], f32r) for h in "hl"] for p in range(2)]
        xs = a("xs", [P, SJ, ROW], f32)
        xh = a("mxh", [P, KD * TT], f32r)
        xl = a("mxl", [P, KD * TT], f32r)
        sg = [a(f"sg{i}", [P, TT], f32) for i in range(2)]
        hf = [a(f"hf{i}", [P, TT], f32) for i in range(4)]
        hh = a("hh", [P, FC, TT], f32r)
        hl = a("hl", [P, FC, TT], f32r)
        meta = [a(f"meta{i}", [P, SJ, E + 1], f32) for i in range(2)]
        wt = a("wt", [P, SJ, 1], f32)
        tk = a("tk", [P, SJ, 1], i32)
        y = a("y", [P, SJ, D], f32)
        g = type("Sems", (), {k: sem("e_" + k) for k in (
            "w_in w_hi w_lo x_in x_read xT_ps xT_hi xT_lo gu_ps silu h_f h_hi h_lo y_ps y_ok meta wt_ok added y_free passed").split()})
        block = m.enter_context(nc.Block())

        def inner(w, c):
            return w[:].rearrange("p k (s f) -> p (k s) f", s=2)[:, :, c * P:(c + 1) * P]

        def experts(eng, tile):
            def expert(e, par, more):
                lo = eng.value_load(bounds[0:1, ds(e, 1)], min_val=0, max_val=NTMAX - MINT)
                hi = eng.value_load(bounds[0:1, ds(e + 1, 1)], min_val=MINT, max_val=NTMAX)
                tile(lo, e, lo, par, more)
                with eng.Fori(lo + 1, hi) as t:
                    tile(t, e, lo, par, False)

            with eng.Fori(0, E // 2 - 1) as e2:
                expert(e2 * 2, 0, True)
                expert(e2 * 2 + 1, 1, True)
            expert(E - 2, 0, True)
            expert(E - 1, 1, False)

        @block.sync
        def _(sp):
            def tile(t, e, lo, par, more):
                sp.wait_ge(g.x_read, t + 1)
                row = nc.s_assert_within(e * CAP + (t - lo) * TT, 0, E * CAP - TT,
                                         skip_runtime_bounds_check_because="an expert has at most CAP / TT tiles")
                sp.dma_start(xs[:], slots[ds(row, TT), :].rearrange("(s p) r -> p s r", p=P)).then_inc(g.x_in, 16)

            experts(sp, tile)
            last = sp.value_load(bounds[0:1, E:E + 1], min_val=MINT, max_val=NTMAX)
            sp.wait_ge(g.x_read, last + 1)
            sp.dma_start(xs[:], slots[0:TT, :].rearrange("(s p) r -> p s r", p=P)).then_inc(g.x_in, 16)

        @block.gpsimd
        def _(pool):
            pool.sem_inc(g.y_free, 1)
            last = pool.value_load(bounds[0:1, E:E + 1], min_val=MINT, max_val=NTMAX)
            with pool.Fori(0, last) as t:
                pool.wait_ge(g.y_ok, t + 2)
                pool.sem_inc(g.passed, 1)
                for s in range(SJ):
                    pool.indirect_dma_start(out, bass.IndirectOffsetOnAxis(ap=tk[:, s, :], axis=0),
                                            y[:, s, :], None, compute_op=ALU.add).then_inc(g.added, 16)
                pool.wait_ge(g.added, t * (SJ * 16) + SJ * 16)
                pool.sem_inc(g.y_free, 1)

        @block.scalar
        def _(act):
            def piece(c, par):
                act.activation(inner(gw[par][0], c), inner(graw, c), ACT.Copy)
                act.activation(dw[par][0][:, c, :], draw[:, c, :], ACT.Copy).then_inc(g.w_hi, 1)

            def load(e):
                act.dma_start(graw[:], gu_in[ds(e, 1)].rearrange("o p k f -> p (o k) f")).then_inc(g.w_in, 16)
                act.dma_start(draw[:], dn_in[ds(e, 1)].rearrange("o p k f -> p (o k) f")).then_inc(g.w_in, 16)

            def xT(t):
                act.wait_ge(g.xT_ps, t + 1)
                act.activation(xh[:], bank[0][:], ACT.Copy).then_inc(g.xT_hi, 1)

            def silu(t, f):
                act.wait_ge(g.gu_ps, t * FC + (f + 1))
                act.activation(sg[f % 2][:], bank[2 + f % NB][:, 0:TT], ACT.Silu).then_inc(g.silu, 1)

            def h_hi(t, f):
                act.wait_ge(g.h_f, t * FC + (f + 1 + NB))
                act.activation(hh[:, f, :], hf[f % 4][:], ACT.Copy).then_inc(g.h_hi, 1)

            def tile(t, e, lo, par, more):
                if more:
                    act.wait_ge(g.w_in, e * 32 + 32)
                for f in range(FC):
                    silu(t, f)
                    if f:
                        h_hi(t, f - 1)
                    if more and f % 2:
                        piece(f // 2, 1 - par)
                h_hi(t, FC - 1)
                xT(t + 1)
                if more:
                    for c in range(FC // 2, FC):
                        piece(c, 1 - par)
                    act.wait_ge(g.w_lo, e * FC + 2 * FC)
                    if not isinstance(e, int):
                        load(e + 2)

            act.wait_ge(graw_in, 32)
            for c in range(FC):
                piece(c, 0)
            act.wait_ge(g.w_lo, FC)
            act.dma_start(graw[:], gu_in[1]).then_inc(g.w_in, 16)
            act.dma_start(draw[:], dn_in[1]).then_inc(g.w_in, 16)
            xT(0)
            experts(act, tile)

        @block.tensor
        def _(pe):
            def tr(t):
                pe.wait_ge(g.x_in, t * 16 + 16)
                for k in range(KD):
                    for s in range(SJ):
                        ins = pe.transpose(bank[0][:, k * TT + s * P:k * TT + (s + 1) * P], xs[:, s, k * P:(k + 1) * P], ident[:])
                ins.then_inc(g.xT_ps, 1)

            def tile(t, e, lo, par, more):
                (gh, gl), (dh, dl) = gw[par], dw[par]
                pe.wait_ge(g.xT_lo, t + 1)
                for f in range(FC):
                    if t is lo:
                        pe.wait_ge(g.w_lo, e * FC + (f + 1))
                    pe.wait_ge(g.h_f, t * FC + (f + 1))
                    for side in range(2):
                        c = slice(side * F + f * P, side * F + (f + 1) * P)
                        o = bank[2 + f % NB][:, side * TT:(side + 1) * TT]
                        for k in range(KD):
                            kx = slice(k * TT, (k + 1) * TT)
                            pe.matmul(o, gh[:, k, c], xh[:, kx], start=k == 0, stop=False)
                            pe.matmul(o, gh[:, k, c], xl[:, kx], start=False, stop=False)
                            ins = pe.matmul(o, gl[:, k, c], xh[:, kx], start=False, stop=k == KD - 1)
                    ins.then_inc(g.gu_ps, 1)
                tr(t + 1)
                pe.wait_ge(g.y_ok, t + 1)
                for s in range(SJ):
                    for f in range(FC):
                        if s == 0:
                            pe.wait_ge(g.h_lo, t * FC + (f + 1))
                        h1, h2 = hh[:, f, s * P:(s + 1) * P], hl[:, f, s * P:(s + 1) * P]
                        o = bank[6][:, s * D:(s + 1) * D]
                        pe.matmul(o, h1, dh[:, f, :], start=f == 0, stop=False)
                        pe.matmul(o, h1, dl[:, f, :], start=False, stop=False)
                        ins = pe.matmul(o, h2, dh[:, f, :], start=False, stop=f == FC - 1)
                ins.then_inc(g.y_ps, 1)

            tr(0)
            experts(pe, tile)

        @block.vector
        def _(v):
            v.sem_inc(g.x_read, 1)
            v.sem_inc(g.y_ok, 1)
            v.sem_inc(g.h_f, NB)

            def piece(n, c, par):
                v.wait_ge(g.w_hi, n + (c + 1))
                v.tensor_tensor(inner(gw[par][1], c), inner(graw, c), inner(gw[par][0], c).bitcast(f32), ALU.subtract)
                v.tensor_tensor(dw[par][1][:, c, :], draw[:, c, :], dw[par][0][:, c, :].bitcast(f32), ALU.subtract).then_inc(g.w_lo, 1)

            def xT(t):
                v.wait_ge(g.xT_hi, t + 1)
                v.tensor_tensor(xl[:], bank[0][:], xh[:].bitcast(f32), ALU.subtract).then_inc(g.xT_lo, 1)
                v.tensor_copy(meta[0][:], xs[:, :, D:ROW]).then_inc(g.x_read, 1)

            def h_f(t, f):
                v.wait_ge(g.silu, t * FC + (f + 1))
                v.tensor_tensor(hf[f % 4][:], bank[2 + f % NB][:, TT:2 * TT], sg[f % 2][:], ALU.mult).then_inc(g.h_f, 1)

            def h_lo(t, f):
                v.wait_ge(g.h_hi, t * FC + (f + 1))
                v.tensor_tensor(hl[:, f, :], hf[f % 4][:], hh[:, f, :].bitcast(f32), ALU.subtract).then_inc(g.h_lo, 1)

            def tile(t, e, lo, par, more):
                v.wait_ge(g.x_read, t + 2)
                v.tensor_copy(meta[1][:], meta[0][:]).then_inc(g.meta, 1)
                for f in range(FC):
                    h_f(t, f)
                    if f:
                        h_lo(t, f - 1)
                    if more and f % 2:
                        piece(e * FC + FC, f // 2, 1 - par)
                h_lo(t, FC - 1)
                xT(t + 1)
                if more:
                    for c in range(FC // 2, FC):
                        piece(e * FC + FC, c, 1 - par)
                v.wait_ge(g.meta, t + 1)
                v.wait_ge(g.y_free, t + 1)
                v.tensor_copy(tk[:], meta[1][:, :, E:E + 1].bitcast(i32))
                v.tensor_copy(wt[:], meta[1][:, :, ds(e, 1)]).then_inc(g.wt_ok, 1)
                v.wait_ge(g.wt_ok, t + 1)
                v.wait_ge(g.y_ps, t + 1)
                for s in range(SJ):
                    ins = v.tensor_scalar(y[:, s, :], bank[6][:, s * D:(s + 1) * D], wt[:, s, :], None, ALU.mult)
                ins.then_inc(g.y_ok, 1)

            for c in range(FC):
                piece(0, c, 0)
            xT(0)
            experts(v, tile)


def _constants():
    c = np.zeros((P, C_N), np.float32)
    p = np.arange(P)
    c[:, C_ID:C_ID + P] = np.eye(P)
    c[:, C_TRI:C_TRI + P] = p[:, None] < p[None, :]
    c[:, C_BD:C_BD + HH] = (p[:, None] // DH) == np.arange(HH)[None, :]
    c[:, C_HALF:C_HALF + 2] = (p[:, None] // SK) == np.arange(2)[None, :]
    sel = np.zeros((P, NPAIR + 1, P), np.float32)
    for r in range(2 * 32):
        if r % 32 < H:
            n, h = (r % 32) // 2, (r % 32) % 2
            sel[r, n, h * SK:(h + 1) * SK] = 1
    sel[0, NPAIR] = sel[32, NPAIR] = 1
    e = np.arange(E + 1)
    c[:, C_TRI8:C_TRI8 + (E + 1) * E] = (np.arange(E)[None, :] < e[:, None]).reshape(1, -1)
    c[:, C_BASE:C_BASE + E] = np.arange(E) * CAP
    tok = (np.arange(T // P)[None, :] * P + p[:, None]).astype(np.int32)
    pad = np.zeros((PAD, ROW), np.float32)
    pad[:, ROW - 1] = (T + np.arange(PAD)).astype(np.int32).view(np.float32)
    return c, sel.reshape(P, -1), tok, pad, np.zeros((PAD, D), np.float32)


def kernel(**inputs):
    import concourse.bacc as bacc
    from concourse.bass_utils import run_bass_kernel_spmd

    i = {k: np.asarray(v) for k, v in inputs.items()}

    def rows(w):
        return np.ascontiguousarray(w.reshape(-1, P, w.shape[-1]).transpose(1, 0, 2))

    w = [[rows(i[f"L0_xattn_w{n}"].T) for n in "qkvo"], [rows(i[f"L1_xattn_W{n}"]) for n in "qkvo"]]
    bias = lambda n: np.stack([i[f"L{l}_xattn_b{n}"] for l in range(2)])
    bcol = np.stack([bias("q"), bias("k")], 1).reshape(2, 2, KD, P).transpose(3, 0, 1, 2)
    every = lambda v: np.broadcast_to(v[None], (P,) + v.shape)
    ctxT = rows(i["ctx_1024"].reshape(B * SK, D).T).reshape(P, KD, B, 1, SK).repeat(2, axis=3).reshape(P, -1)
    mask = i["mask_Bx1x1xS2_ff0"].reshape(B, SK)
    router = rows(np.broadcast_to(i["L0_ffn_w_router"][:, None], (D, P)))
    gu = i["L1_ffn_gate_up_proj"].transpose(0, 2, 1).reshape(E, KD, P, 2 * F).transpose(0, 2, 1, 3)
    dn = i["L1_ffn_down_proj"].transpose(0, 2, 1).reshape(E, FC, P, D).transpose(0, 2, 1, 3)
    const, sel, tok, pad, zero = _constants()
    arrays = dict(
        x_in=i["x"].reshape(T, D), ctxT_in=ctxT, maskr_in=mask.reshape(1, B * SK), maskc_in=np.concatenate([mask.T, mask.T]),
        w_in=np.stack([np.stack(l, 1) for l in w]), bcol_in=bcol, bv_in=every(bias("v")), bo_in=every(bias("o")),
        wb_in=rows(i["L0_ffn_w_block"]), wr_in=router, gate_in=rows(i["L1_ffn_gate_w"].T),
        gu_in=gu, dn_in=dn, const_in=const, sel_in=sel, tok_in=tok, pad_in=pad, zero_in=zero)
    arrays = {k: np.ascontiguousarray(v) for k, v in arrays.items()}
    nc = bacc.Bacc("TRN2", target_bir_lowering=False, num_devices=1)
    aps = {k: nc.dram_tensor(k, list(v.shape), mybir.dt.from_np(v.dtype), kind="ExternalInput").ap() for k, v in arrays.items()}
    aps["out"] = nc.dram_tensor("out", [T + PAD, D], mybir.dt.float32, kind="ExternalOutput").ap()
    build(nc, **aps)
    r = run_bass_kernel_spmd(nc, [arrays], core_ids=[0])
    return r.results[0]["out"][:T].reshape(B, S, D)
```

```python
from contextlib import ExitStack

import numpy as np

import concourse.bass as bass
from concourse import mybir

P = 128
B, S, D = 8, 512, 256
SK = 64
H, DH = 16, 16
T = B * S
TJ = S // P
KD = D // P
HH = H // KD
QH = HH // 2
NPAIR = H // 2
PH = NPAIR // 2
GP = 2
NG = NPAIR // GP
KEEP = int(S * 0.75)
E, F = 8, 1024
FC = F // P
TOPK = 2
TT = 256
MINT = 2
PAD = TT
CAP = T + MINT * TT
NTMAX = T * TOPK // TT + MINT * E
ROW = D + E + 1
NEG = -1.0e9
EPS = 1e-5
SCALE = float(DH) ** -0.5

C_ID = 0
C_TRI = C_ID + P
C_BD = C_TRI + P
C_HALF = C_BD + QH
C_TRI8 = C_HALF + 2
C_BASE = C_TRI8 + (E + 1) * E
C_N = C_BASE + E


def build(nc, x_in, ctxT_in, maskr_in, maskc_in, w_in, bcol_in, bv_in, bo_in, wb_in, wr_in, gate_in, gu_in, dn_in,
          const_in, sel_in, tok_in, pad_in, zero_in, out):
    f32, f32r, bf16, i32 = mybir.dt.float32, mybir.dt.float32r, mybir.dt.bfloat16, mybir.dt.int32
    ALU, ACT, AX = mybir.AluOpType, mybir.ActivationFunctionType, mybir.AxisListType
    slots = nc.dram_tensor("slots", [E * CAP, ROW], f32).ap()
    ctx = ExitStack()
    ds = bass.ds
    NB2 = 2 * B

    def sb(name, shape, dt, c=None):
        return (c or ctx).enter_context(nc.sbuf_tensor(name, shape, dt))

    def sem(name):
        return ctx.enter_context(nc.semaphore(name))

    def asf(ap):
        return ap.bitcast(f32)

    with ctx:
        bank = [ctx.enter_context(nc.psum_tensor(f"bank{i}", [P, 512], f32)) for i in range(8)]
        ident = sb("ident", [P, P], f32)
        bounds = sb("bounds", [1, E + 1 + E], i32)
        w_lay, k_lay = [None, None], [None, None]
        with ExitStack() as early:
            w_lay[0] = [sb(f"w0{p}", [P, 4, KD, D], f32r, early) for p in "hl"]
            k_lay[0] = [sb(f"k0{p}", [P, KD, B * SK], f32r, early) for p in "hl"]
        graw = sb("graw", [P, KD, 2 * F], f32)
        draw = sb("draw", [P, FC, D], f32)

        att = ExitStack()
        with att:
            a = lambda name, shape, dt, c=att: sb(name, shape, dt, c)
            x = a("x", [P, T // P, D], f32)
            const = a("const", [P, C_N], f32)
            tokid = a("tokid", [P, T // P], i32)
            sel = a("sel", [P, (NPAIR + 1) * P], f32r)
            mrow = sel[:, NPAIR * P:]
            trib = a("trib", [P, P], bf16)
            oneb = a("oneb", [P, P], bf16)
            epst = a("epst", [P, 1], f32)
            w_lay[1] = [a(f"w1{p}", [P, 4, KD, D], f32r) for p in "hl"]
            k_lay[1] = [a(f"k1{p}", [P, KD, B * SK], f32r) for p in "hl"]
            v_lay = [a(f"v{l}", [P, B, NPAIR, DH], f32) for l in range(2)]
            bcol = a("bcol", [P, 2, 2, KD], f32)
            kt = a("kt", [P, 2, KD, QH * SK], f32r)
            kb = [a(f"kb{p}", [P, 2, KD, 2, QH * SK], f32r) for p in range(2)]
            vb = [a(f"vb{p}", [P, NPAIR, 2, DH + 1], f32) for p in range(2)]
            mkr = a("mkr", [P, B * SK], f32r)
            bo = a("bo", [P, 2, D], f32)
            mkc = a("mkc", [P, B], f32)
            mkb = [a(f"mkb{p}", [P, 1], f32) for p in range(2)]
            xn = a("xn", [P, TJ, D], f32)
            x2 = [a(f"x2{p}", [P, TJ, ROW], f32) for p in range(2)]
            st = a("st", [P, 2 * TJ, 6], f32)
            mv = a("mv", [P, 2 * TJ, 2], f32)
            rs = a("rs", [P, 5, 2 * TJ], f32)
            mx = a("mx", [P, TJ + 1, P // 2], f32)
            mm = a("mm", [P, S], f32r)
            wbh = a("wbh", [P, KD, D], f32r)
            wbl = a("wbl", [P, KD, D], f32r)
            wrh = a("wrh", [P, KD, P], f32r)
            wrl = a("wrl", [P, KD, P], f32r)
            gt = a("gt", [P, KD, E], f32)
            keep = a("keep", [P, 2, TJ], f32)
            sc = a("sc", [P, TJ, 1], f32)
            lg = a("lg", [P, TJ, E], f32)
            m1 = a("m1", [P, TJ], f32)
            rank = a("rank", [P, TJ, E], f32)
            pick = a("pick", [P, TJ, E], f32)
            pickb = a("pickb", [P, TJ, E], bf16)
            es = a("es", [P, TJ, E], f32)
            ex = a("ex", [P, TJ, E], f32)
            sm = a("sm", [P, 2, TJ], f32)
            run = a("run", [P, E], f32)
            slot = a("slot", [P, TJ, E], f32)
            sf = a("sf", [P, TOPK, TJ], f32)
            si = [a(f"si{p}", [P, TOPK, TJ], i32) for p in range(2)]
            cn = a("cn", [P, 4, E + 1], f32)
            ci = a("ci", [P, 2, E + 1], i32)
            with ExitStack() as raw:
                craw = a("craw", [P, KD * B * 2 * SK], f32, raw)
                wraw = [a(f"wraw{l}", [P, 4, KD, D], f32, raw) for l in range(2)]
                selraw = a("selraw", [P, (NPAIR + 1) * P], f32, raw)
                mraw = a("mraw", [P, B * SK], f32, raw)
                bv = a("bv", [P, 2, D], f32, raw)
                wbraw = a("wbraw", [P, KD, D], f32, raw)
                wrraw = a("wrraw", [P, KD, P], f32, raw)
            pr = a("pr", [P, NPAIR, S], f32)
            rec = a("rec", [P, 2, TJ, 2 * GP], f32)
            cf = a("cf", [P, TJ, D], f32)
            ch = a("ch", [P, KD, S], f32r)
            cl = a("cl", [P, KD, S], f32r)
            with ExitStack() as routing:
                x2T = a("x2T", [P, KD, S], f32, routing)
                r1 = a("r1", [P, TJ, E, E], f32, routing)
                r2 = a("r2", [P, TJ, E, E], f32, routing)
                s2 = a("s2", [P, TOPK, TJ, E], f32, routing)
            gl = a("gl", [P, TJ, D], f32)
            srow = a("srow", [P, S], f32)
            cmp1 = a("cmp1", [P, TJ, S], bf16)
            cmp2 = a("cmp2", [P, TJ, P], bf16)
            with ExitStack() as cx:
                chi = a("chi", [P, KD * B * 2 * SK], f32r, cx)
                clo = a("clo", [P, KD * B * 2 * SK], f32r, cx)
            xh = a("xh", [P, KD, S], f32r)
            xl = a("xl", [P, KD, S], f32r)
            qq = [a(f"qq{p}", [P, KD, 2, S], f32r) for p in range(2)]

            g = type("Sems", (), {k: sem(k) for k in (
                "x0_in x_in const_in w0_in w1_in w2_in pool_ready setup mask_ready c_hi w_hi "
                "w_lo kv_ps k_hi k_lo v_done bn stats ln_act rstd_act newton rstd xn_ready x2_ready "
                "xT_ps xT_hi xT_lo x2T_ps x2T_hi x2T_lo q_ps q_hi q_lo s_ps max_done max_twice mT_ps m_hi m_lo "
                "st_ps exp_done pv_ps rec_done ctx_f cT_ps ctx_hi ctx_lo o_ps x_bo x_new kb_in kblk passed_v passed_a "
                "passed_p f_ps gelu srow_ps srow sc_ps score cmp cnt_ps keep_ok x_skip1 x_skip ffn_x lg_ps lg_sb exps "
                "sel_b pos_ps slot_read slot_ok xrow_ok rows_left scattered0 scattered1 x_out bounds_ok route counts "
                "wb_hi graw_in padded pads").split()})
            scattered = [g.scattered0, g.scattered1]
            block = att.enter_context(nc.Block())

            def pipeline(eng, step):
                def loop(n0, layer, side):
                    with eng.Fori(0, 2) as i:
                        for par in range(2):
                            step(i * 2 + (n0 + par), par, layer, layer, layer, side, side)

                step(0, 0, 0, 0, 0, None, None)
                step(1, 1, 0, 0, 0, "ffn", None)
                loop(2, 0, "ffn")
                step(6, 0, 0, 0, 1, "ffn", "ffn")
                step(7, 1, 0, 1, 1, "ffn", "ffn")
                step(8, 0, 1, 1, 1, "ffn", "ffn")
                step(9, 1, 1, 1, 1, "moe", "ffn")
                loop(10, 1, "moe")
                step(14, 0, 1, 1, None, "moe", "moe")
                step(15, 1, 1, None, None, "moe", "moe")

            def tiles(n, layer, j=0, w=TJ):
                return ds(n * TJ + (j - layer * B * TJ), w)

            def xt(n, layer, j):
                return x[:, tiles(n, layer, j, 1), :].rearrange("p o d -> p (o d)")

            LO, HI = slice(0, P // 2), slice(P // 2, P)
            QUARTERS = ((LO, 0, LO, HI), (HI, 1, HI, LO))

            def layer_of(side):
                return 0 if side == "ffn" else 1

            def pad_slots(eng, half):
                eng.wait_ge(g.bounds_ok, 1)
                with eng.Fori(0, E // 2) as e:
                    r = eng.value_load(bounds[0:1, ds(e * 2 + (E + 1 + half), 1)], min_val=0, max_val=E * CAP - PAD)
                    eng.dma_start(slots[ds(r, PAD), :], pad_in[0:PAD, :]).then_inc(g.pads, 16)

            @block.sync
            def _(sp):
                sp.dma_start(wraw[0][:], w_in[0]).then_inc(g.w0_in, 16)
                sp.dma_start(bcol[:], bcol_in).then_inc(g.w0_in, 16)
                for b in range(2):
                    sp.dma_start(x[:, b * TJ:(b + 1) * TJ, :],
                                 x_in[b * S:(b + 1) * S, :].rearrange("(t p) d -> p t d", p=P)).then_inc(g.x0_in, 16)
                sp.dma_start(wraw[1][:], w_in[1]).then_inc(g.w2_in, 16)
                sp.dma_start(wbraw[:], wb_in).then_inc(g.w1_in, 16)
                sp.dma_start(wrraw[:], wr_in).then_inc(g.w1_in, 16)
                sp.dma_start(bo[:], bo_in).then_inc(g.w1_in, 16)
                sp.dma_start(gt[:], gate_in).then_inc(g.w1_in, 16)
                sp.dma_start(tokid[:], tok_in).then_inc(g.w1_in, 16)
                for b in range(2, B):
                    sp.dma_start(x[:, b * TJ:(b + 1) * TJ, :],
                                 x_in[b * S:(b + 1) * S, :].rearrange("(t p) d -> p t d", p=P)).then_inc(g.x_in, 16)
                sp.dma_start(out[T:T + MINT * TT, :], zero_in).then_inc(g.x_out, 16)
                with sp.Fori(0, E) as e:
                    sp.dma_start(slots[ds(e * CAP + PAD, (MINT - 1) * TT), :], pad_in[PAD:MINT * TT, :]).then_inc(g.padded, 16)

                def keys_in(n, par):
                    sp.wait_ge(g.kblk, n + 1)
                    for q, src in enumerate((LO, HI)):
                        for dst in (LO, HI):
                            sp.dma_start(asf(kb[par][dst, :, :, q, :]), asf(kt[src, :, :, :])).then_inc(g.kb_in, 16)

                def x_to_out(n):
                    sp.wait_ge(g.x_new, n * 2 + 3)
                    sp.dma_start(out[ds(n * S - B * S, S), :].rearrange("(t p) d -> p t d", p=P),
                                 x[:, tiles(n, 1), :]).then_inc(g.x_out, 16)

                keys_in(0, 0)

                def step(n, par, cur, nxt, nn, side, prev):
                    if nxt is not None:
                        keys_in(n + 1, 1 - par)
                    if side == "moe":
                        x_to_out(n - 1)
                    if side == "moe" and prev == "ffn":
                        sp.wait_ge(g.o_ps, 2 * B)
                        sp.dma_start(graw[:], gu_in[0]).then_inc(g.graw_in, 16)
                        sp.dma_start(draw[:], dn_in[0]).then_inc(g.graw_in, 16)

                pipeline(sp, step)
                x_to_out(NB2 - 1)
                pad_slots(sp, 0)
                sp.wait_ge(g.x_out, (B + 1) * 16)

            @block.gpsimd
            def _(pool):
                pool.sem_inc(g.x_skip, 1)
                pool.memset(mm[:].bitcast(i32), 0)
                pool.memset(mkr[:].bitcast(i32), 0)
                pool.memset(mx[:], 0.0)
                pool.memset(oneb[:], 1.0)
                pool.memset(epst[:], EPS).then_inc(g.pool_ready, 1)

                def keys(n, par, layer):
                    if isinstance(n, int) and n == 0:
                        pool.wait_ge(g.k_lo, KD)
                        pool.wait_ge(g.v_done, B)
                        pool.wait_ge(g.const_in, 96)
                    else:
                        pool.wait_ge(g.mT_ps, n)
                        pool.wait_ge(g.kb_in, n * 64)
                        pool.sem_inc(g.passed_p, 1)
                    if isinstance(n, int) and n < 2:
                        pool.tensor_copy(vb[par][:, :, :, DH:DH + 1], const[:, C_HALF:C_HALF + 2].unsqueeze(1).unsqueeze(3).to_broadcast([P, NPAIR, 2, 1]))
                    for part in range(2):
                        for c in range(KD):
                            pool.tensor_tensor(
                                kt[:, part, c, :].rearrange("p (h k) -> p h k", h=QH),
                                asf(k_lay[layer][part][:, c, ds(n * SK - layer * B * SK, SK)]).unsqueeze(1).to_broadcast([P, QH, SK]),
                                const[:, C_BD:C_BD + QH].unsqueeze(2).to_broadcast([P, QH, SK]), ALU.mult)
                    if layer:
                        pool.tensor_copy(mkb[par][:], mkc[:, ds(n - B, 1)])
                    pool.tensor_tensor(vb[par][:, :, :, 0:DH],
                                       v_lay[layer][:, ds(n - layer * B, 1), :, :].rearrange("p o a d -> p (o a) d").unsqueeze(2).to_broadcast([P, NPAIR, 2, DH]),
                                       const[:, C_HALF:C_HALF + 2].unsqueeze(1).unsqueeze(3).to_broadcast([P, NPAIR, 2, DH]),
                                       ALU.mult).then_inc(g.kblk, 1)

                def update(m, par):
                    xb, n2 = x[:, tiles(m, 0), :], x2[par][:, :, 0:D]
                    pool.wait_ge(g.keep_ok, m + 1)
                    pool.wait_ge(g.gelu, m * 2 + 2)
                    pool.tensor_tensor(n2, n2, keep[:, 1, :].unsqueeze(2).to_broadcast([P, TJ, D]), ALU.mult).then_inc(g.x_skip1, 1)
                    pool.tensor_tensor(gl[:], gl[:], keep[:, 0, :].unsqueeze(2).to_broadcast([P, TJ, D]), ALU.mult).then_inc(g.x_skip1, 1)
                    pool.wait_ge(g.x_skip1, m * 2 + 1)
                    pool.sem_inc(g.passed_p, 1)
                    pool.tensor_tensor(xb, xb, n2, ALU.add).then_inc(g.x_skip, 1)
                    pool.wait_ge(g.x_skip, m + 2)
                    pool.sem_inc(g.passed_p, 1)
                    pool.tensor_tensor(xb, xb, gl[:], ALU.add).then_inc(g.ffn_x, 1)

                def add_bo(n, layer):
                    pool.wait_ge(g.xn_ready, n + 1)
                    xb = x[:, tiles(n, layer), :]
                    pool.sem_inc(g.passed_p, 1)
                    pool.tensor_tensor(xb, xb, bo[:, layer, :].unsqueeze(1).to_broadcast([P, TJ, D]), ALU.add).then_inc(g.x_bo, 1)

                def scatter(m, par):
                    pool.wait_ge(g.slot_ok, m - (B - 1))
                    pool.wait_ge(g.xrow_ok, m - (B - 1))
                    pool.sem_inc(g.passed_p, 1)
                    for kk in range(TOPK):
                        for j in range(TJ):
                            pool.indirect_dma_start(slots, bass.IndirectOffsetOnAxis(ap=si[par][:, kk, j:j + 1], axis=0),
                                                    x2[par][:, j, :], None).then_inc(scattered[par], 16)
                    pool.wait_ge(scattered[par], (m - (B + par)) * (TOPK * TJ * 8) + TOPK * TJ * 16)
                    pool.sem_inc(g.rows_left, 1)

                pool.wait_ge(g.wb_hi, 1)
                pool.tensor_tensor(wbl[:], wbraw[:], asf(wbh[:]), ALU.subtract)
                pool.tensor_tensor(wrl[:], wrraw[:], asf(wrh[:]), ALU.subtract)
                keys(0, 0, 0)
                add_bo(0, 0)
                add_bo(1, 0)

                def step(n, par, cur, nxt, nn, side, prev):
                    if nxt is not None:
                        keys(n + 1, 1 - par, nxt)
                    if prev == "ffn":
                        update(n - 2, par)
                    if prev == "moe":
                        pool.wait_ge(g.padded, E * 16)
                        scatter(n - 2, par)
                    if nn is not None:
                        add_bo(n + 2, nn)

                pipeline(pool, step)
                scatter(NB2 - 2, 0)
                scatter(NB2 - 1, 1)

            @block.scalar
            def _(act):
                act.preload_act_table_set("natural_log_exp_and_others")
                act.dma_start(craw[:], ctxT_in).then_inc(g.w0_in, 16)
                act.dma_start(const[:], const_in).then_inc(g.const_in, 16)
                act.dma_start(selraw[:], sel_in).then_inc(g.const_in, 16)
                act.dma_start(bv[:], bv_in).then_inc(g.const_in, 16)
                for r in (0, 32):
                    act.dma_start(mraw[r:r + 1, :], maskr_in).then_inc(g.const_in, 16)
                act.dma_start(mkc[:], maskc_in).then_inc(g.const_in, 16)

                def rstd(c, t):
                    act.wait_ge(g.stats, c + 1)
                    act.activation(rs[:, 0, t], mv[:, t, 1], ACT.Ln, bias=epst[:, 0:1]).then_inc(g.ln_act, 1)
                    act.wait_ge(g.ln_act, c + 1)
                    act.activation(rs[:, 1, t], rs[:, 0, t], ACT.Exp, scale=-0.5).then_inc(g.rstd_act, 1)

                def normed(n, c, layer, t0=0):
                    act.wait_ge(g.rstd, c + 1)
                    act.sem_inc(g.passed_a, 1)
                    for j in range(TJ):
                        ins = act.activation(xn[:, j, :], xt(n, layer, j), ACT.Identity, bias=rs[:, 4, t0 + j:t0 + j + 1],
                                             scale=rs[:, 3, t0 + j:t0 + j + 1])
                    ins.then_inc(g.xn_ready, 1)

                def normed2(m, par, side, c, first):
                    act.wait_ge(g.rstd, c + 1)
                    if side == "moe":
                        act.wait_ge(g.rows_left, m - (B - 1))
                        act.wait_ge(g.x_skip, B if first else B + 1)
                    elif not first:
                        act.wait_ge(g.x_skip, m)
                    act.sem_inc(g.passed_a, 1)
                    for j in range(TJ):
                        t = slice(TJ + j, TJ + j + 1)
                        ins = act.activation(x2[par][:, j, 0:D], xt(m, layer_of(side), j), ACT.Identity, bias=rs[:, 4, t], scale=rs[:, 3, t])
                    ins.then_inc(g.x2_ready, 1)

                def xT(n):
                    for c in range(KD):
                        act.wait_ge(g.xT_ps, n * KD + (c + 1))
                        act.activation(xh[:, c, :], bank[c][:], ACT.Copy).then_inc(g.xT_hi, 1)

                def x2T_hi(m, side):
                    if side == "moe":
                        act.wait_ge(g.ffn_x, B)
                    for c in range(KD):
                        act.wait_ge(g.x2T_ps, m * KD + (c + 1))
                        act.activation(xh[:, c, :] if side == "ffn" else x2T[:, c, :], bank[4 + c][:], ACT.Copy).then_inc(g.x2T_hi, 1)

                def q_hi(n, par, layer):
                    for c in range(KD):
                        act.wait_ge(g.q_ps, n * KD + (c + 1))
                        for rows, q, hi, lo in QUARTERS:
                            ins = act.activation(qq[par][hi, c, q, :], bank[c][rows, :], ACT.Identity, bias=bcol[rows, layer, 0, c:c + 1])
                        ins.then_inc(g.q_hi, 1)

                def m_hi(n):
                    act.wait_ge(g.mT_ps, n + 1)
                    act.activation(mm[0:64, :], bank[2][0:64, :], ACT.Copy, scale=-1.0).then_inc(g.m_hi, 1)

                def exps(n, par, layer, pairs):
                    for p in pairs:
                        act.wait_ge(g.st_ps, n * NPAIR + (p + 1))
                        act.activation(pr[:, p, :], bank[4 + p % 2][:], ACT.Exp, scale=SCALE,
                                       bias=mkb[par][:, 0:1] if layer else 0.0).then_inc(g.exp_done, 1)

                def ctx_hi(n):
                    for c in range(KD):
                        act.wait_ge(g.cT_ps, n * KD + (c + 1))
                        act.activation(ch[:, c, :], bank[6 + c][:], ACT.Copy).then_inc(g.ctx_hi, 1)

                def gelu(m, first):
                    if not first:
                        act.wait_ge(g.ffn_x, m)
                    for i, u in enumerate((1, 0)):
                        act.wait_ge(g.f_ps, m * 2 + (i + 1))
                        act.activation(gl[:, 2 * u:2 * u + 2, :].rearrange("p t d -> p (t d)"), bank[2 + u][:],
                                       ACT.Gelu_apprx_tanh).then_inc(g.gelu, 1)
                    act.preload_act_table_set("natural_log_exp_and_others")

                def srow_copy(m):
                    act.wait_ge(g.srow_ps, m + 1)
                    act.activation(srow[:], bank[2][:], ACT.Copy).then_inc(g.srow, 1)

                def ex_(m):
                    act.wait_ge(g.lg_sb, m - (B - 1))
                    act.activation(ex[:], es[:], ACT.Exp).then_inc(g.exps, 1)

                act.wait_ge(g.w0_in, 48)
                act.activation(chi[:], craw[:], ACT.Copy).then_inc(g.c_hi, 1)
                act.activation(w_lay[0][0][:], wraw[0][:], ACT.Copy).then_inc(g.w_hi, 1)
                act.wait_ge(g.w2_in, 16)
                act.activation(w_lay[1][0][:], wraw[1][:], ACT.Copy).then_inc(g.w_hi, 1)
                act.wait_ge(g.pool_ready, 1)
                rstd(0, slice(0, 2 * TJ))
                normed(0, 0, 0)
                for layer in range(2):
                    if layer:
                        act.wait_ge(g.const_in, 96)
                        act.activation(sel[:], selraw[:], ACT.Copy)
                        act.wait_ge(g.w1_in, 80)
                        act.activation(wrh[:], wrraw[:], ACT.Copy)
                        act.activation(wbh[:], wbraw[:], ACT.Copy).then_inc(g.wb_hi, 1)
                    for c in range(KD):
                        act.wait_ge(g.kv_ps, layer * (KD + B) + c + 1)
                        act.activation(k_lay[layer][0][:, c, :], bank[c][:], ACT.Identity,
                                       bias=bcol[:, layer, 1, c:c + 1]).then_inc(g.k_hi, 1)
                xT(0)
                normed(1, 0, 0, TJ)
                q_hi(0, 0, 0)
                m_hi(0)
                act.sem_inc(g.exp_done, 2)
                act.wait_ge(g.mask_ready, 1)

                def step(n, par, cur, nxt, nn, side, prev):
                    exps(n, par, cur, (0, 1))
                    if nxt is not None:
                        xT(n + 1)
                    exps(n, par, cur, (2, 3))
                    rstd(n + 1, slice(0 if nn is not None else TJ, 2 * TJ if side else TJ))
                    if nxt is not None:
                        q_hi(n + 1, 1 - par, nxt)
                    if prev == "moe":
                        ex_(n - 2)
                    exps(n, par, cur, (4, 5))
                    exps(n, par, cur, (6, 7))
                    if side:
                        normed2(n - 1, 1 - par, side, n + 1, prev != side)
                    if nn is not None:
                        normed(n + 2, n + 1, nn)
                    ctx_hi(n)
                    if side:
                        x2T_hi(n - 1, side)
                    if nxt is not None:
                        m_hi(n + 1)
                    elif side == "moe":
                        ex_(n - 1)
                    if side == "ffn":
                        srow_copy(n - 1)
                        gelu(n - 1, prev is None)

                pipeline(act, step)
                rstd(NB2 + 1, slice(TJ, 2 * TJ))
                normed2(NB2 - 1, 1, "moe", NB2 + 1, False)
                x2T_hi(NB2 - 1, "moe")
                ex_(NB2 - 1)
                pad_slots(act, 1)

            @block.tensor
            def _(pe):
                def three(o, ahi, alo, bhi, blo):
                    n = len(ahi)
                    for c in range(n):
                        pe.matmul(o, ahi[c], bhi[c], start=c == 0, stop=False)
                        pe.matmul(o, ahi[c], blo[c], start=False, stop=False)
                        ins = pe.matmul(o, alo[c], bhi[c], start=False, stop=c == n - 1)
                    return ins

                def chunks(t, *rest):
                    return [t[(slice(None), k) + rest] for k in range(KD)]

                def wts(layer, i, cols=slice(None)):
                    return [[w_lay[layer][p][:, i, k, cols] for k in range(KD)] for p in range(2)]

                def transposes(src, b0, done):
                    for c in range(KD):
                        for j in range(TJ):
                            ins = pe.transpose(bank[b0 + c][:, j * P:(j + 1) * P], src[:, j, c * P:(c + 1) * P], ident[:])
                        ins.then_inc(done, 1)

                def tr(n):
                    pe.wait_ge(g.xn_ready, n + 1)
                    transposes(xn, 0, g.xT_ps)

                def tr2(m, par):
                    pe.wait_ge(g.x2_ready, m + 1)
                    transposes(x2[par], 4, g.x2T_ps)

                def q_proj(n, layer):
                    pe.wait_ge(g.xT_lo, n * KD + KD)
                    for c in range(KD):
                        wh, wl = wts(layer, 0, slice(c * P, (c + 1) * P))
                        three(bank[c][:], wh, wl, chunks(xh), chunks(xl)).then_inc(g.q_ps, 1)

                def maxima(n, par, layer, units):
                    for u in units:
                        j, c = u // KD, u % KD
                        pe.wait_ge(g.max_done, n * TJ * KD + (u + 1))
                        if layer:
                            pe.matmul(bank[2 + c][:], mrow, mkr[:, ds(n * SK - B * SK, SK)].unsqueeze(1).to_broadcast([P, HH, SK]),
                                      start=True, stop=False)
                        for q in range(2):
                            ins = pe.matmul(bank[2 + c][:, q * QH * SK:(q + 1) * QH * SK], qq[par][:, c, q, j * P:(j + 1) * P],
                                            kb[par][:, 0, c, q, :], start=not layer, stop=not layer or q == 1)
                        ins.then_inc(g.s_ps, 1)

                def maxima_T(n):
                    pe.wait_ge(g.max_twice, n + 1)
                    for j in range(TJ):
                        ins = pe.transpose(bank[2][:, j * P:(j + 1) * P], mx[:, j:j + 2, :].rearrange("p a b -> p (a b)"), ident[:])
                    ins.then_inc(g.mT_ps, 1)

                def scores(n, par, pairs):
                    for p in pairs:
                        c, q, o = p // PH, p % PH // 2, p % 2 * P
                        pe.wait_ge(g.exp_done, n * NPAIR + (p + 1))
                        for part in range(2):
                            pe.matmul(bank[4 + p % 2][:], kb[par][:, part, c, q, o:o + P], qq[par][:, c, q, :], start=part == 0, stop=False)
                    if pairs[0] == 0:
                        pe.wait_ge(g.m_lo, n + 1)
                    for p in pairs:
                        pe.matmul(bank[4 + p % 2][:], sel[:, p * P:(p + 1) * P], mm[:], start=False, stop=True).then_inc(g.st_ps, 1)

                def values(n, par, i):
                    pe.wait_ge(g.exp_done, n * NPAIR + (GP * (i + 1) + 2))
                    if i >= 2:
                        pe.wait_ge(g.ctx_f, n * NG + (i - 1))
                    W = 2 * (DH + 1)
                    for t in range(TJ):
                        for j in range(GP):
                            p = i * GP + j
                            ins = pe.matmul(bank[6 + i % 2][:, (t * GP + j) * W:(t * GP + j + 1) * W], pr[:, p, t * P:(t + 1) * P],
                                            vb[par][:, p, :, :], start=True, stop=True)
                    ins.then_inc(g.pv_ps, 1)

                def ctx_T(n):
                    pe.wait_ge(g.ctx_f, n * NG + NG)
                    transposes(cf, 6, g.cT_ps)

                def out_proj(n, layer):
                    pe.wait_ge(g.ctx_lo, n * KD + KD)
                    wh, wl = wts(layer, 3)
                    for u in range(2):
                        for t in range(2):
                            j = slice((2 * u + t) * P, (2 * u + t + 1) * P)
                            ins = three(bank[u][:, t * D:(t + 1) * D], chunks(ch, j), chunks(cl, j), wh, wl)
                        ins.then_inc(g.o_ps, 1)

                def ffn_mm(m):
                    for u in (1, 0):
                        if u == 0:
                            pe.wait_ge(g.srow, m + 1)
                        for t in range(2):
                            j = slice((2 * u + t) * P, (2 * u + t + 1) * P)
                            ins = three(bank[2 + u][:, t * D:(t + 1) * D], chunks(xh, j), chunks(xl, j), chunks(wbh), chunks(wbl))
                        ins.then_inc(g.f_ps, 1)

                def router(m):
                    pe.wait_ge(g.x2T_lo, m * KD + KD)
                    three(bank[2][:], chunks(wrh), chunks(wrl), chunks(xh), chunks(xl)).then_inc(g.srow_ps, 1)

                def router_T(m):
                    pe.wait_ge(g.srow, m + 1)
                    for j in range(TJ):
                        ins = pe.transpose(bank[6][:, j * P:(j + 1) * P], srow[:, j * P:(j + 1) * P], ident[:])
                    ins.then_inc(g.sc_ps, 1)

                def count(m):
                    pe.wait_ge(g.gelu, m * 2 + 2)
                    pe.wait_ge(g.cmp, m * 2 + 2)
                    for i in range(TJ):
                        for j in range(TJ):
                            pe.matmul(bank[3][:, i:i + 1], cmp1[:, j, i * P:(i + 1) * P], oneb[:, 0:1], start=j == 0, stop=False)
                        ins = pe.matmul(bank[3][:, i:i + 1], cmp2[:, i, :], oneb[:, 0:1], start=False, stop=True)
                    ins.then_inc(g.cnt_ps, 1)

                def gates(m):
                    pe.wait_ge(g.x2T_hi, m * KD + KD)
                    for j in range(TJ):
                        for k in range(KD):
                            ins = pe.matmul(bank[2][:, j * E:(j + 1) * E], x2T[:, k, j * P:(j + 1) * P], gt[:, k, :],
                                            start=k == 0, stop=k == KD - 1)
                    ins.then_inc(g.lg_ps, 1)

                def positions(m):
                    pe.wait_ge(g.sel_b, m - (B - 1))
                    for j in range(TJ):
                        for i in range(j):
                            pe.matmul(bank[3][:, j * E:(j + 1) * E], oneb[:], pickb[:, i, :], start=i == 0, stop=False)
                        pe.matmul(bank[3][:, j * E:(j + 1) * E], trib[:], pickb[:, j, :], start=j == 0, stop=True)
                    for i in range(TJ):
                        ins = pe.matmul(bank[3][:, TJ * E:(TJ + 1) * E], oneb[:], pickb[:, i, :], start=i == 0, stop=i == TJ - 1)
                    ins.then_inc(g.pos_ps, 1)

                for layer in range(2):
                    pe.wait_ge(g.w_lo, layer + 1)
                    if layer:
                        pe.wait_ge(g.k_lo, KD)
                    cview = lambda t: [t[:, k * B * 2 * SK:(k + 1) * B * 2 * SK].rearrange("p (b r s) -> p b r s", r=2, s=SK)[:, :, 0, :] for k in range(KD)]
                    for c in range(KD):
                        wh, wl = wts(layer, 1, slice(c * P, (c + 1) * P))
                        three(bank[c][:], wh, wl, cview(chi), cview(clo)).then_inc(g.kv_ps, 1)
                    wh, wl = wts(layer, 2)
                    for b in range(B):
                        if layer or b >= 4:
                            pe.wait_ge(g.v_done, layer * B + b - 3)
                        dup = lambda t: [t[:, (k * B + b) * 2 * SK:(k * B + b + 1) * 2 * SK] for k in range(KD)]
                        three(bank[4 + b % 4][:, 0:D], dup(chi), dup(clo), wh, wl).then_inc(g.kv_ps, 1)
                pe.wait_ge(g.k_lo, 2 * KD)
                tr(0)
                q_proj(0, 0)
                pe.wait_ge(g.q_lo, KD)
                pe.wait_ge(g.kblk, 1)
                pe.wait_ge(g.kb_in, 64)
                maxima(0, 0, 0, range(TJ * KD))
                maxima_T(0)
                pe.wait_ge(g.v_done, 2 * B)

                def step(n, par, cur, nxt, nn, side, prev):
                    pe.wait_ge(g.q_lo, n * KD + KD)
                    scores(n, par, (0, 1))
                    pe.wait_ge(g.x_new, n * 2 + 1)
                    if nxt is not None:
                        tr(n + 1)
                    scores(n, par, (2, 3))
                    if prev == "ffn":
                        pe.wait_ge(g.score, n - 1)
                    values(n, par, 0)
                    if prev == "moe" and nn is None:
                        positions(n - 2)
                    if nxt is not None:
                        q_proj(n + 1, nxt)
                    scores(n, par, (4, 5))
                    values(n, par, 1)
                    if prev == "ffn":
                        count(n - 2)
                    if prev == "moe" and nn is not None:
                        positions(n - 2)
                    scores(n, par, (6, 7))
                    if nxt is not None:
                        pe.wait_ge(g.q_lo, (n + 1) * KD + KD)
                        pe.wait_ge(g.kblk, n + 2)
                        pe.wait_ge(g.kb_in, n * 64 + 128)
                        if prev == "ffn":
                            pe.wait_ge(g.keep_ok, n - 1)
                        if prev == "moe":
                            pe.wait_ge(g.slot_read, n - B - 1)
                        maxima(n + 1, 1 - par, nxt, (0, 1))
                    values(n, par, 2)
                    if nxt is not None:
                        maxima(n + 1, 1 - par, nxt, (2, 3))
                    values(n, par, 3)
                    if nxt is not None:
                        maxima(n + 1, 1 - par, nxt, (4, 5))
                    ctx_T(n)
                    if nxt is not None:
                        maxima(n + 1, 1 - par, nxt, (6, 7))
                    if side:
                        tr2(n - 1, 1 - par)
                    if side == "moe" and nxt is None:
                        gates(n - 1)
                    if nxt is not None:
                        maxima_T(n + 1)
                        pe.wait_ge(g.q_lo, (n + 1) * KD + KD)
                    if side == "moe" and nxt is None:
                        positions(n - 1)
                    out_proj(n, cur)
                    if side and nxt is not None:
                        pe.wait_ge(g.m_lo, n + 2)
                    if side == "ffn":
                        router(n - 1)
                        ffn_mm(n - 1)
                        router_T(n - 1)
                    if side == "moe" and nxt is not None:
                        gates(n - 1)

                pipeline(pe, step)
                tr2(NB2 - 1, 1)
                gates(NB2 - 1)
                pe.wait_ge(g.slot_read, B - 1)
                positions(NB2 - 1)

            @block.vector
            def _(v):
                tri8 = const[:, C_TRI8:C_TRI8 + E * E].rearrange("p (e f) -> p e f", f=E)
                NROUTE = 13

                def stats(c, groups):
                    for n, layer, t0 in groups:
                        for j in range(TJ):
                            ins = v.bn_stats(st[:, t0 + j, :], xt(n, layer, j))
                    ins.then_inc(g.bn, 1)
                    v.wait_ge(g.bn, c + 1)
                    v.sem_inc(g.passed_v, 1)
                    for _, _, t0 in groups:
                        for j in range(TJ):
                            ins = v.bn_aggr(mv[:, t0 + j, :], st[:, t0 + j, :])
                    ins.then_inc(g.stats, 1)

                def newton(c, t):
                    v.wait_ge(g.rstd_act, c + 1)
                    v.tensor_tensor(rs[:, 2, t], rs[:, 1, t], rs[:, 1, t], ALU.mult).then_inc(g.newton, 1)
                    v.wait_ge(g.newton, c * 4 + 1)
                    v.scalar_tensor_tensor(rs[:, 2, t], mv[:, t, 1], EPS, rs[:, 2, t], ALU.add, ALU.mult).then_inc(g.newton, 1)
                    v.wait_ge(g.newton, c * 4 + 2)
                    v.tensor_scalar(rs[:, 2, t], rs[:, 2, t], -0.5, 1.5, ALU.mult, ALU.add).then_inc(g.newton, 1)
                    v.wait_ge(g.newton, c * 4 + 3)
                    v.tensor_tensor(rs[:, 3, t], rs[:, 1, t], rs[:, 2, t], ALU.mult).then_inc(g.newton, 1)
                    v.wait_ge(g.newton, c * 4 + 4)
                    v.scalar_tensor_tensor(rs[:, 4, t], mv[:, t, 0], -1.0, rs[:, 3, t], ALU.mult, ALU.mult).then_inc(g.rstd, 1)

                def lo(b0, hi, low, src, i, done):
                    for c in range(KD):
                        v.wait_ge(src, i * KD + (c + 1))
                        v.tensor_tensor(low[:, c, :], bank[b0 + c][:], asf(hi[:, c, :]), ALU.subtract).then_inc(done, 1)

                def q_lo(n, par, layer):
                    for c in range(KD):
                        v.wait_ge(g.q_hi, n * KD + (c + 1))
                        for rows, q, hi, lo in QUARTERS:
                            ins = v.scalar_tensor_tensor(qq[par][lo, c, q, :], bank[c][rows, :], bcol[rows, layer, 0, c:c + 1],
                                                         asf(qq[par][hi, c, q, :]), ALU.add, ALU.subtract)
                        ins.then_inc(g.q_lo, 1)

                def maxes(n, units):
                    for u in units:
                        j, c = u // KD, u % KD
                        v.wait_ge(g.s_ps, n * TJ * KD + (u + 1))
                        v.tensor_reduce(mx[:, j, c * HH:(c + 1) * HH], bank[2 + c][:].rearrange("p (h k) -> p h k", k=SK),
                                        AX.X, ALU.max).then_inc(g.max_done, 1)

                def maxes_twice(n):
                    v.wait_ge(g.max_done, n * TJ * KD + (TJ * KD + 2))
                    v.tensor_copy(mx[:, 0:TJ, 32:32 + H], mx[:, 0:TJ, 0:H]).then_inc(g.max_twice, 1)

                def m_lo(n):
                    v.wait_ge(g.m_hi, n + 1)
                    v.scalar_tensor_tensor(mm[32:64, :], bank[2][32:64, :], -1.0, asf(mm[32:64, :]),
                                           ALU.mult, ALU.subtract).then_inc(g.m_lo, 1)

                def ctx_f(n, i):
                    v.wait_ge(g.pv_ps, n * NG + (i + 1))
                    o = bank[6 + i % 2][:, 0:TJ * GP * 2 * (DH + 1)].rearrange("p (t h c) -> p t h c", h=2 * GP, c=DH + 1)
                    v.reciprocal(rec[:, i % 2, :, :], o[:, :, :, DH]).then_inc(g.rec_done, 1)
                    v.wait_ge(g.rec_done, n * NG + (i + 1))
                    w = 2 * GP * DH
                    v.tensor_tensor(cf[:, :, i * w:(i + 1) * w].rearrange("p t (h c) -> p t h c", c=DH), o[:, :, :, 0:DH],
                                    rec[:, i % 2, :, :].unsqueeze(3).to_broadcast([P, TJ, 2 * GP, DH]), ALU.mult).then_inc(g.ctx_f, 1)

                def x_up(n, layer):
                    v.wait_ge(g.x_bo, n + 1)
                    for u in range(2):
                        v.wait_ge(g.o_ps, n * 2 + (u + 1))
                        xb = x[:, tiles(n, layer, 2 * u, 2), :]
                        v.tensor_tensor(xb, bank[u][:].rearrange("p (t d) -> p t d", t=2), xb, ALU.add).then_inc(g.x_new, 1)

                def score(m):
                    v.wait_ge(g.sc_ps, m + 1)
                    v.tensor_copy(sc[:], bank[6][:].rearrange("p (t c) -> p t c", c=P)[:, :, 0:1]).then_inc(g.score, 1)

                def compare(m, js):
                    v.wait_ge(g.score, m + 1)
                    for j in js:
                        w = (j + 1) * P
                        v.tensor_scalar(cmp1[:, j, 0:w], srow[:, 0:w], sc[:, j, :], None, ALU.is_lt)
                        if j < TJ - 1:
                            v.tensor_scalar(cmp1[:, j, w:S], srow[:, w:S], sc[:, j, :], None, ALU.is_le)
                        ins = v.scalar_tensor_tensor(cmp2[:, j, :], srow[:, w - P:w], sc[:, j, :],
                                                     const[:, C_TRI:C_TRI + P], ALU.is_equal, ALU.mult)
                    ins.then_inc(g.cmp, 1)

                def keeps(m):
                    v.wait_ge(g.cnt_ps, m + 1)
                    v.tensor_scalar(keep[:, 0, :], bank[3][:, 0:TJ], float(KEEP), None, ALU.is_lt)
                    v.tensor_scalar(keep[:, 1, :], bank[3][:, 0:TJ], float(KEEP), None, ALU.is_ge).then_inc(g.keep_ok, 1)

                def dep(ins, m, i):
                    ins.then_inc(g.route, 1)
                    v.wait_ge(g.route, m * NROUTE + (i - B * NROUTE))

                def gating(m, par):
                    v.wait_ge(g.lg_ps, m - (B - 1))
                    dep(v.tensor_copy(lg[:].rearrange("p t e -> p (t e)"), bank[2][:, 0:TJ * E]), m, 1)
                    dep(v.tensor_reduce(m1[:], lg[:], AX.X, ALU.max), m, 2)
                    v.tensor_tensor(es[:], lg[:], m1[:].unsqueeze(2).to_broadcast([P, TJ, E]), ALU.subtract).then_inc(g.lg_sb, 1)
                    lf = lg[:].unsqueeze(2).to_broadcast([P, TJ, E, E])
                    le = lg[:].unsqueeze(3).to_broadcast([P, TJ, E, E])
                    v.tensor_tensor(r1[:], lf, le, ALU.is_gt)
                    dep(v.tensor_tensor(r2[:], lf, le, ALU.is_equal), m, 3)
                    dep(v.tensor_tensor(r2[:], r2[:], tri8.unsqueeze(1).to_broadcast([P, TJ, E, E]), ALU.mult), m, 4)
                    dep(v.tensor_tensor(r1[:], r1[:], r2[:], ALU.add), m, 5)
                    dep(v.tensor_reduce(rank[:], r1[:], AX.X, ALU.add), m, 6)
                    v.tensor_scalar(pickb[:], rank[:], float(TOPK), None, ALU.is_lt).then_inc(g.sel_b, 1)
                    dep(v.tensor_scalar(pick[:], rank[:], float(TOPK), None, ALU.is_lt), m, 7)

                def weights(m, par):
                    v.wait_ge(g.exps, m - (B - 1))
                    dep(v.tensor_tensor(es[:], ex[:], pick[:], ALU.mult), m, 11)
                    dep(v.tensor_reduce(sm[:, 0, :], es[:], AX.X, ALU.add), m, 12)
                    dep(v.reciprocal(sm[:, 1, :], sm[:, 0, :]), m, 13)
                    v.tensor_tensor(x2[par][:, :, D:D + E], es[:], sm[:, 1, :].unsqueeze(2).to_broadcast([P, TJ, E]), ALU.mult)
                    v.tensor_copy(x2[par][:, :, D + E].bitcast(i32), tokid[:, tiles(m, 1)]).then_inc(g.xrow_ok, 1)

                def slots_of(m, par):
                    v.wait_ge(g.pos_ps, m - (B - 1))
                    dep(v.tensor_tensor(slot[:], bank[3][:, 0:TJ * E].rearrange("p (t e) -> p t e", e=E),
                                        run[:].unsqueeze(1).to_broadcast([P, TJ, E]), ALU.add), m, 8)
                    v.tensor_tensor(run[:], run[:], bank[3][:, TJ * E:(TJ + 1) * E], ALU.add).then_inc(g.slot_read, 1)
                    for kk in range(TOPK):
                        ins = v.scalar_tensor_tensor(s2[:, kk, :, :], rank[:], float(kk), slot[:], ALU.is_equal, ALU.mult)
                    dep(ins, m, 9)
                    dep(v.tensor_reduce(sf[:], s2[:], AX.X, ALU.add), m, 10)
                    v.tensor_copy(si[par][:], sf[:]).then_inc(g.slot_ok, 1)

                v.sem_inc(g.x_new, 1)
                v.sem_inc(g.max_done, 2)
                v.sem_inc(g.rows_left, 2)
                v.wait_ge(g.c_hi, 1)
                v.tensor_tensor(clo[:], craw[:], asf(chi[:]), ALU.subtract)
                v.wait_ge(g.w_hi, 1)
                v.tensor_tensor(w_lay[0][1][:], wraw[0][:], asf(w_lay[0][0][:]), ALU.subtract).then_inc(g.w_lo, 1)
                v.wait_ge(g.x0_in, 32)
                stats(0, [(0, 0, 0), (1, 0, TJ)])
                v.wait_ge(g.pool_ready, 1)
                newton(0, slice(0, 2 * TJ))
                v.wait_ge(g.const_in, 96)
                v.tensor_copy(ident[:], const[:, C_ID:C_ID + P])
                v.tensor_copy(trib[:], const[:, C_TRI:C_TRI + P])
                v.tensor_copy(run[:], const[:, C_BASE:C_BASE + E])
                v.wait_ge(g.w_hi, 2)
                v.tensor_tensor(w_lay[1][1][:], wraw[1][:], asf(w_lay[1][0][:]), ALU.subtract).then_inc(g.w_lo, 1)
                for layer in range(2):
                    for c in range(KD):
                        v.wait_ge(g.k_hi, layer * KD + c + 1)
                        v.scalar_tensor_tensor(k_lay[layer][1][:, c, :], bank[c][:], bcol[:, layer, 1, c:c + 1],
                                               asf(k_lay[layer][0][:, c, :]), ALU.add, ALU.subtract).then_inc(g.k_lo, 1)
                    for b in range(B):
                        v.wait_ge(g.kv_ps, layer * (KD + B) + KD + b + 1)
                        for r in range(2):
                            q, hd = slice(r * SK, (r + 1) * SK), slice(r * DH, (r + 1) * DH)
                            ins = v.tensor_tensor(v_lay[layer][q, b, :, :],
                                                  bank[4 + b % 4][q, 0:D].rearrange("p (n c) -> p n c", c=2 * DH)[:, :, hd],
                                                  bv[q, layer, :].rearrange("p (n c) -> p n c", c=2 * DH)[:, :, hd], ALU.add)
                        ins.then_inc(g.v_done, 1)
                lo(0, xh, xl, g.xT_hi, 0, g.xT_lo)
                v.wait_ge(g.w1_in, 80)
                for r in (0, 32):
                    v.tensor_scalar(mraw[r:r + 1, :], mraw[r:r + 1, :], NEG, 1.0 / SCALE, ALU.mult, ALU.mult)
                v.tensor_scalar(mkc[:], mkc[:], NEG, None, ALU.mult).then_inc(g.setup, 1)
                v.wait_ge(g.setup, 1)
                for r in (0, 32):
                    last = v.tensor_copy(mkr[r:r + 1, :], mraw[r:r + 1, :])
                last.then_inc(g.setup, 1)
                v.wait_ge(g.setup, 2)
                v.tensor_tensor(mkr[32:33, :], mraw[32:33, :], asf(mkr[32:33, :]), ALU.subtract).then_inc(g.mask_ready, 1)
                q_lo(0, 0, 0)
                maxes(0, range(TJ * KD))
                maxes_twice(0)
                m_lo(0)
                v.wait_ge(g.x_in, (B - 2) * 16)

                def step(n, par, cur, nxt, nn, side, prev):
                    if side:
                        v.wait_ge(g.x_new, n * 2 + 1)
                    stats(n + 1, ([(n + 2, nn, 0)] if nn is not None else []) + ([(n - 1, layer_of(side), TJ)] if side else []))
                    if prev == "ffn":
                        score(n - 2)
                        compare(n - 2, (0, 1))
                    if prev == "moe" and nn is None:
                        gating(n - 2, par)
                    if nxt is not None:
                        lo(0, xh, xl, g.xT_hi, n + 1, g.xT_lo)
                    newton(n + 1, slice(0 if nn is not None else TJ, 2 * TJ if side else TJ))
                    ctx_f(n, 0)
                    if prev == "ffn":
                        compare(n - 2, (2, 3))
                    if prev == "moe" and nn is not None:
                        gating(n - 2, par)
                    elif prev == "moe":
                        slots_of(n - 2, par)
                    if nxt is not None:
                        q_lo(n + 1, 1 - par, nxt)
                    ctx_f(n, 1)
                    if prev == "ffn":
                        keeps(n - 2)
                    if prev == "moe":
                        if nn is not None:
                            slots_of(n - 2, par)
                        weights(n - 2, par)
                    if nxt is not None:
                        maxes(n + 1, (0, 1))
                    ctx_f(n, 2)
                    if nxt is not None:
                        maxes(n + 1, (2, 3))
                    ctx_f(n, 3)
                    if nxt is not None:
                        maxes(n + 1, (4, 5, 6, 7))
                        maxes_twice(n + 1)
                    if side == "moe" and nxt is None:
                        gating(n - 1, 1 - par)
                    lo(6, ch, cl, g.ctx_hi, n, g.ctx_lo)
                    if side == "moe" and nxt is None:
                        slots_of(n - 1, 1 - par)
                        weights(n - 1, 1 - par)
                    if nxt is not None:
                        m_lo(n + 1)
                    if side == "ffn":
                        lo(4, xh, xl, g.x2T_hi, n - 1, g.x2T_lo)
                    x_up(n, cur)

                pipeline(v, step)
                v.wait_ge(g.x_new, NB2 * 2 + 1)
                stats(NB2 + 1, [(NB2 - 1, 1, TJ)])
                newton(NB2 + 1, slice(TJ, 2 * TJ))
                gating(NB2 - 1, 1)
                slots_of(NB2 - 1, 1)
                weights(NB2 - 1, 1)

                t = [0]

                def dep1(ins):
                    t[0] += 1
                    ins.then_inc(g.counts, 1)
                    v.wait_ge(g.counts, t[0])

                r1f = r1[:].rearrange("p a b c -> p (a b c)")[:, 0:(E + 1) * E].rearrange("p (e f) -> p e f", f=E)
                v.wait_ge(g.slot_read, B)
                v.tensor_copy(ci[:, 1, 0:E], run[:])
                dep1(v.tensor_tensor(cn[:, 0, 0:E], run[:], const[:, C_BASE:C_BASE + E], ALU.subtract))
                dep1(v.tensor_scalar(cn[:, 1, 0:E], cn[:, 0, 0:E], float(TT - 1), None, ALU.add))
                dep1(v.tensor_copy(ci[:, 0, 0:E], cn[:, 1, 0:E]))
                dep1(v.tensor_scalar(ci[:, 0, 0:E], ci[:, 0, 0:E], TT.bit_length() - 1, None, ALU.logical_shift_right))
                dep1(v.tensor_copy(cn[:, 2, 0:E], ci[:, 0, 0:E]))
                dep1(v.tensor_scalar(cn[:, 2, 0:E], cn[:, 2, 0:E], float(MINT), None, ALU.max))
                dep1(v.tensor_tensor(r1f, cn[:, 2, 0:E].unsqueeze(1).to_broadcast([P, E + 1, E]),
                                     const[:, C_TRI8:C_TRI8 + (E + 1) * E].rearrange("p (e f) -> p e f", f=E), ALU.mult))
                dep1(v.tensor_reduce(cn[:, 3, :], r1f, AX.X, ALU.add))
                v.tensor_copy(bounds[0:1, 0:E + 1], cn[0:1, 3, :])
                v.tensor_copy(bounds[0:1, E + 1:2 * E + 1], ci[0:1, 1, 0:E]).then_inc(g.bounds_ok, 1)
        moe(nc, sb, sem, bank, ident, bounds, graw, draw, g.graw_in, scattered, g.pads, slots, gu_in, dn_in, out)


def moe(nc, sb, sem, bank, ident, bounds, graw, draw, graw_in, scattered, pads, slots, gu_in, dn_in, out):
    f32, f32r, i32 = mybir.dt.float32, mybir.dt.float32r, mybir.dt.int32
    ALU, ACT = mybir.AluOpType, mybir.ActivationFunctionType
    ds = bass.ds
    SJ = TT // P
    SPLIT = (3, 5, 7)
    XT_AT = 5
    NB = 4
    with ExitStack() as m:
        a = lambda name, shape, dt: sb(name, shape, dt, m)
        gw = [[a(f"gw{p}{h}", [P, KD, 2 * F], f32r) for h in "hl"] for p in range(2)]
        dw = [[a(f"dw{p}{h}", [P, FC, D], f32r) for h in "hl"] for p in range(2)]
        xs = a("xs", [P, SJ, ROW], f32)
        xh = a("mxh", [P, KD * TT], f32r)
        xl = a("mxl", [P, KD * TT], f32r)
        sg = [a(f"sg{i}", [P, TT], f32) for i in range(2)]
        hf = [a(f"hf{i}", [P, TT], f32) for i in range(4)]
        hh = a("hh", [P, FC, TT], f32r)
        hl = a("hl", [P, FC, TT], f32r)
        meta = [a(f"meta{i}", [P, SJ, E + 1], f32) for i in range(2)]
        wt = a("wt", [P, SJ, 1], f32)
        tk = a("tk", [P, SJ, 1], i32)
        y = a("y", [P, SJ, D], f32)
        g = type("Sems", (), {k: sem("e_" + k) for k in (
            "w_in w_hi w_lo x_in x_read xT_ps xT_hi xT_lo gu_ps silu h_f h_hi h_lo y_ps y_ok meta wt_ok added y_free passed").split()})
        block = m.enter_context(nc.Block())

        def inner(w, c):
            return w[:].rearrange("p k (s f) -> p (k s) f", s=2)[:, :, c * P:(c + 1) * P]

        def experts(eng, tile):
            def expert(e, par, more):
                lo = eng.value_load(bounds[0:1, ds(e, 1)], min_val=0, max_val=NTMAX - MINT)
                hi = eng.value_load(bounds[0:1, ds(e + 1, 1)], min_val=MINT, max_val=NTMAX)
                tile(lo, e, lo, par, more)
                with eng.Fori(lo + 1, hi) as t:
                    tile(t, e, lo, par, False)

            with eng.Fori(0, E // 2 - 1) as e2:
                expert(e2 * 2, 0, True)
                expert(e2 * 2 + 1, 1, True)
            expert(E - 2, 0, True)
            expert(E - 1, 1, False)

        @block.sync
        def _(sp):
            for s in scattered:
                sp.wait_ge(s, B // 2 * TOPK * TJ * 16)
            sp.wait_ge(pads, E * 16)

            def tile(t, e, lo, par, more):
                sp.wait_ge(g.x_read, t + 1)
                row = nc.s_assert_within(e * CAP + (t - lo) * TT, 0, E * CAP - TT,
                                         skip_runtime_bounds_check_because="an expert has at most CAP / TT tiles")
                sp.dma_start(xs[:], slots[ds(row, TT), :].rearrange("(s p) r -> p s r", p=P)).then_inc(g.x_in, 16)

            experts(sp, tile)
            last = sp.value_load(bounds[0:1, E:E + 1], min_val=MINT, max_val=NTMAX)
            sp.wait_ge(g.x_read, last + 1)
            sp.dma_start(xs[:], slots[0:TT, :].rearrange("(s p) r -> p s r", p=P)).then_inc(g.x_in, 16)

        @block.gpsimd
        def _(pool):
            pool.sem_inc(g.y_free, 1)
            last = pool.value_load(bounds[0:1, E:E + 1], min_val=MINT, max_val=NTMAX)
            with pool.Fori(0, last) as t:
                pool.wait_ge(g.y_ok, t + 2)
                pool.sem_inc(g.passed, 1)
                for s in range(SJ):
                    pool.indirect_dma_start(out, bass.IndirectOffsetOnAxis(ap=tk[:, s, :], axis=0),
                                            y[:, s, :], None, compute_op=ALU.add).then_inc(g.added, 16)
                pool.wait_ge(g.added, t * (SJ * 16) + SJ * 16)
                pool.sem_inc(g.y_free, 1)

        @block.scalar
        def _(act):
            def piece(c, par):
                act.activation(inner(gw[par][0], c), inner(graw, c), ACT.Copy)
                act.activation(dw[par][0][:, c, :], draw[:, c, :], ACT.Copy).then_inc(g.w_hi, 1)

            def load(e):
                act.dma_start(graw[:], gu_in[ds(e, 1)].rearrange("o p k f -> p (o k) f")).then_inc(g.w_in, 16)
                act.dma_start(draw[:], dn_in[ds(e, 1)].rearrange("o p k f -> p (o k) f")).then_inc(g.w_in, 16)

            def xT(t):
                act.wait_ge(g.xT_ps, t + 1)
                act.activation(xh[:], bank[0][:], ACT.Copy).then_inc(g.xT_hi, 1)

            def silu(t, f):
                act.wait_ge(g.gu_ps, t * FC + (f + 1))
                act.activation(sg[f % 2][:], bank[2 + f % NB][:, 0:TT], ACT.Silu).then_inc(g.silu, 1)

            def h_hi(t, f):
                act.wait_ge(g.h_f, t * FC + (f + 1 + NB))
                act.activation(hh[:, f, :], hf[f % 4][:], ACT.Copy).then_inc(g.h_hi, 1)

            def tile(t, e, lo, par, more):
                for f in range(FC):
                    silu(t, f)
                    if f:
                        h_hi(t, f - 1)
                    if more and f in SPLIT:
                        if f == SPLIT[0]:
                            act.wait_ge(g.w_in, e * 32 + 32)
                        piece(SPLIT.index(f), 1 - par)
                h_hi(t, FC - 1)
                xT(t + 1)
                if more:
                    for c in range(len(SPLIT), FC):
                        piece(c, 1 - par)
                    act.wait_ge(g.w_lo, e * FC + 2 * FC)
                    if not isinstance(e, int):
                        load(e + 2)

            act.wait_ge(graw_in, 32)
            for c in range(FC):
                piece(c, 0)
                if c == XT_AT:
                    xT(0)
            act.wait_ge(g.w_lo, FC)
            act.dma_start(graw[:], gu_in[1]).then_inc(g.w_in, 16)
            act.dma_start(draw[:], dn_in[1]).then_inc(g.w_in, 16)
            experts(act, tile)

        @block.tensor
        def _(pe):
            def tr(t):
                pe.wait_ge(g.x_in, t * 16 + 16)
                for k in range(KD):
                    for s in range(SJ):
                        ins = pe.transpose(bank[0][:, k * TT + s * P:k * TT + (s + 1) * P], xs[:, s, k * P:(k + 1) * P], ident[:])
                ins.then_inc(g.xT_ps, 1)

            def tile(t, e, lo, par, more):
                (gh, gl), (dh, dl) = gw[par], dw[par]
                pe.wait_ge(g.xT_lo, t + 1)
                for f in range(FC):
                    if t is lo:
                        pe.wait_ge(g.w_lo, e * FC + (f + 1))
                    pe.wait_ge(g.h_f, t * FC + (f + 1))
                    for side in range(2):
                        c = slice(side * F + f * P, side * F + (f + 1) * P)
                        o = bank[2 + f % NB][:, side * TT:(side + 1) * TT]
                        for k in range(KD):
                            kx = slice(k * TT, (k + 1) * TT)
                            pe.matmul(o, gh[:, k, c], xh[:, kx], start=k == 0, stop=False)
                            pe.matmul(o, gh[:, k, c], xl[:, kx], start=False, stop=False)
                            ins = pe.matmul(o, gl[:, k, c], xh[:, kx], start=False, stop=k == KD - 1)
                    ins.then_inc(g.gu_ps, 1)
                tr(t + 1)
                pe.wait_ge(g.y_ok, t + 1)
                for s in range(SJ):
                    for f in range(FC):
                        if s == 0:
                            pe.wait_ge(g.h_lo, t * FC + (f + 1))
                        h1, h2 = hh[:, f, s * P:(s + 1) * P], hl[:, f, s * P:(s + 1) * P]
                        o = bank[6][:, s * D:(s + 1) * D]
                        pe.matmul(o, h1, dh[:, f, :], start=f == 0, stop=False)
                        pe.matmul(o, h1, dl[:, f, :], start=False, stop=False)
                        ins = pe.matmul(o, h2, dh[:, f, :], start=False, stop=f == FC - 1)
                ins.then_inc(g.y_ps, 1)

            tr(0)
            experts(pe, tile)

        @block.vector
        def _(v):
            v.sem_inc(g.x_read, 1)
            v.sem_inc(g.y_ok, 1)
            v.sem_inc(g.h_f, NB)

            def piece(n, c, par):
                v.wait_ge(g.w_hi, n + (c + 1))
                v.tensor_tensor(inner(gw[par][1], c), inner(graw, c), inner(gw[par][0], c).bitcast(f32), ALU.subtract)
                v.tensor_tensor(dw[par][1][:, c, :], draw[:, c, :], dw[par][0][:, c, :].bitcast(f32), ALU.subtract).then_inc(g.w_lo, 1)

            def xT(t):
                v.wait_ge(g.xT_hi, t + 1)
                v.tensor_tensor(xl[:], bank[0][:], xh[:].bitcast(f32), ALU.subtract).then_inc(g.xT_lo, 1)
                v.tensor_copy(meta[0][:], xs[:, :, D:ROW]).then_inc(g.x_read, 1)

            def h_f(t, f):
                v.wait_ge(g.silu, t * FC + (f + 1))
                v.tensor_tensor(hf[f % 4][:], bank[2 + f % NB][:, TT:2 * TT], sg[f % 2][:], ALU.mult).then_inc(g.h_f, 1)

            def h_lo(t, f):
                v.wait_ge(g.h_hi, t * FC + (f + 1))
                v.tensor_tensor(hl[:, f, :], hf[f % 4][:], hh[:, f, :].bitcast(f32), ALU.subtract).then_inc(g.h_lo, 1)

            def tile(t, e, lo, par, more):
                v.wait_ge(g.x_read, t + 2)
                v.tensor_copy(meta[1][:], meta[0][:]).then_inc(g.meta, 1)
                for f in range(FC):
                    h_f(t, f)
                    if f:
                        h_lo(t, f - 1)
                    if more and f in SPLIT:
                        piece(e * FC + FC, SPLIT.index(f), 1 - par)
                h_lo(t, FC - 1)
                xT(t + 1)
                if more:
                    for c in range(len(SPLIT), FC):
                        piece(e * FC + FC, c, 1 - par)
                v.wait_ge(g.meta, t + 1)
                v.wait_ge(g.y_free, t + 1)
                v.tensor_copy(tk[:], meta[1][:, :, E:E + 1].bitcast(i32))
                v.tensor_copy(wt[:], meta[1][:, :, ds(e, 1)]).then_inc(g.wt_ok, 1)
                v.wait_ge(g.wt_ok, t + 1)
                v.wait_ge(g.y_ps, t + 1)
                for s in range(SJ):
                    ins = v.tensor_scalar(y[:, s, :], bank[6][:, s * D:(s + 1) * D], wt[:, s, :], None, ALU.mult)
                ins.then_inc(g.y_ok, 1)

            for c in range(FC):
                piece(0, c, 0)
                if c == XT_AT:
                    xT(0)
            experts(v, tile)


def _constants():
    c = np.zeros((P, C_N), np.float32)
    p = np.arange(P)
    c[:, C_ID:C_ID + P] = np.eye(P)
    c[:, C_TRI:C_TRI + P] = p[:, None] < p[None, :]
    c[:, C_BD:C_BD + QH] = (p[:, None] // DH) % QH == np.arange(QH)[None, :]
    c[:, C_HALF:C_HALF + 2] = (p[:, None] // SK) == np.arange(2)[None, :]
    sel = np.zeros((P, NPAIR + 1, P), np.float32)
    for r in range(2 * 32):
        if r % 32 < H:
            n, h = (r % 32) // 2, (r % 32) % 2
            sel[r, n, h * SK:(h + 1) * SK] = 1
    sel[0, NPAIR] = sel[32, NPAIR] = 1
    e = np.arange(E + 1)
    c[:, C_TRI8:C_TRI8 + (E + 1) * E] = (np.arange(E)[None, :] < e[:, None]).reshape(1, -1)
    c[:, C_BASE:C_BASE + E] = np.arange(E) * CAP
    tok = (np.arange(T // P)[None, :] * P + p[:, None]).astype(np.int32)
    pad = np.zeros((MINT * TT, ROW), np.float32)
    pad[:, ROW - 1] = (T + np.arange(MINT * TT)).astype(np.int32).view(np.float32)
    return c, sel.reshape(P, -1), tok, pad, np.zeros((MINT * TT, D), np.float32)


def kernel(**inputs):
    import concourse.bacc as bacc
    from concourse.bass_utils import run_bass_kernel_spmd

    i = {k: np.asarray(v) for k, v in inputs.items()}

    def rows(w):
        return np.ascontiguousarray(w.reshape(-1, P, w.shape[-1]).transpose(1, 0, 2))

    w = [[rows(i[f"L0_xattn_w{n}"].T) for n in "qkvo"], [rows(i[f"L1_xattn_W{n}"]) for n in "qkvo"]]
    bias = lambda n: np.stack([i[f"L{l}_xattn_b{n}"] for l in range(2)])
    bcol = np.stack([bias("q"), bias("k")], 1).reshape(2, 2, KD, P).transpose(3, 0, 1, 2)
    every = lambda v: np.broadcast_to(v[None], (P,) + v.shape)
    ctxT = rows(i["ctx_1024"].reshape(B * SK, D).T).reshape(P, KD, B, 1, SK).repeat(2, axis=3).reshape(P, -1)
    mask = i["mask_Bx1x1xS2_ff0"].reshape(B, SK)
    router = rows(np.broadcast_to(i["L0_ffn_w_router"][:, None], (D, P)))
    gu = i["L1_ffn_gate_up_proj"].transpose(0, 2, 1).reshape(E, KD, P, 2 * F).transpose(0, 2, 1, 3)
    dn = i["L1_ffn_down_proj"].transpose(0, 2, 1).reshape(E, FC, P, D).transpose(0, 2, 1, 3)
    const, sel, tok, pad, zero = _constants()
    arrays = dict(
        x_in=i["x"].reshape(T, D), ctxT_in=ctxT, maskr_in=mask.reshape(1, B * SK), maskc_in=np.concatenate([mask.T, mask.T]),
        w_in=np.stack([np.stack(l, 1) for l in w]), bcol_in=bcol, bv_in=every(bias("v")), bo_in=every(bias("o")),
        wb_in=rows(i["L0_ffn_w_block"]), wr_in=router, gate_in=rows(i["L1_ffn_gate_w"].T),
        gu_in=gu, dn_in=dn, const_in=const, sel_in=sel, tok_in=tok, pad_in=pad, zero_in=zero)
    arrays = {k: np.ascontiguousarray(v) for k, v in arrays.items()}
    nc = bacc.Bacc("TRN2", target_bir_lowering=False, num_devices=1)
    aps = {k: nc.dram_tensor(k, list(v.shape), mybir.dt.from_np(v.dtype), kind="ExternalInput").ap() for k, v in arrays.items()}
    aps["out"] = nc.dram_tensor("out", [T + MINT * TT, D], mybir.dt.float32, kind="ExternalOutput").ap()
    build(nc, **aps)
    r = run_bass_kernel_spmd(nc, [arrays], core_ids=[0])
    return r.results[0]["out"][:T].reshape(B, S, D)
```
